# Optimizing a Trainium2 kernel written in Bass

```python
import numpy as np
import jax
import jax.numpy as jnp

def _softmax(x, axis=-1):
    return jax.nn.softmax(x, axis=axis)

def _gelu(x):
    return jax.nn.gelu(x, approximate=True)

def _silu(x):
    return jax.nn.silu(x)

def _sigmoid(x):
    return jax.nn.sigmoid(x)

def _layernorm(x, axis=-1, eps=1e-05):
    m = jnp.mean(x, axis=axis, keepdims=True)
    v = jnp.var(x, axis=axis, keepdims=True)
    return (x - m) / jnp.sqrt(v + eps)

def _scatter_add(tgt, idx, src, axis=0):
    return tgt.at[idx].add(src)

def _segment_sum(src, seg, n):
    return jax.ops.segment_sum(src, seg, n)
kernel_name = 'mk_adj_ffn_d2_adj_r2_1b211c'

def setup_inputs(seed: int=0):
    np.random.seed(seed)
    _w = jnp.asarray

    def _rec_inputs():
        import jax
        import jax.numpy as jnp
        _gk = jax.random.key(seed)
        x = 7.22e-05 + 1 * jax.random.normal(jax.random.fold_in(_gk, 1), (32, 256, 256), jnp.float32)
        _w = (1.0 + jnp.arange(256, dtype=jnp.float32)) ** (-0.5)
        _w = _w / _w.mean()
        _pij = jnp.clip(0.0625 * _w[:, None] * _w[None, :], 0.0, 1.0)
        _a = jax.random.uniform(jax.random.fold_in(_gk, 2), (32, 256, 256)) < _pij
        adj = _a.astype(jnp.int32)
        return (x, adj)
    x, adj = _rec_inputs()

    def _L0_gnn_setup():
        import jax, jax.numpy as jnp
        import numpy as np
        EMBED_DIM = 256
        N_HEADS = 8
        HEAD_DIM = EMBED_DIM // N_HEADS
        NEG_INF = -1000000000.0
        key = jax.random.key(seed)
        ks = jax.random.split(key, 10)
        bs, n_agents = (64, 128)
        inputs = jax.random.normal(ks[0], (bs, n_agents, EMBED_DIM), dtype=jnp.float32)
        adj = jax.random.randint(ks[1], (bs, n_agents, n_agents), 0, 2, dtype=jnp.int32)
        s = 1.0 / np.sqrt(EMBED_DIM)
        Wq = jax.random.normal(ks[2], (EMBED_DIM, EMBED_DIM), dtype=jnp.float32) * s
        Wk = jax.random.normal(ks[3], (EMBED_DIM, EMBED_DIM), dtype=jnp.float32) * s
        Wv = jax.random.normal(ks[4], (EMBED_DIM, EMBED_DIM), dtype=jnp.float32) * s
        Wo = jax.random.normal(ks[5], (EMBED_DIM, EMBED_DIM), dtype=jnp.float32) * s
        bq = jnp.zeros((EMBED_DIM,), jnp.float32)
        bk = jnp.zeros((EMBED_DIM,), jnp.float32)
        bv = jnp.zeros((EMBED_DIM,), jnp.float32)
        bo = jnp.zeros((EMBED_DIM,), jnp.float32)
        return {'inputs': inputs, 'adj': adj, 'Wq': Wq, 'bq': bq, 'Wk': Wk, 'bk': bk, 'Wv': Wv, 'bv': bv, 'Wo': Wo, 'bo': bo}
    _L0_gnn_all = _L0_gnn_setup()
    _L0_gnn_in = {k: v for k, v in _L0_gnn_all.items() if k in ('Wq', 'bq', 'Wk', 'bk', 'Wv', 'bv', 'Wo', 'bo')}
    del _L0_gnn_all

    def _L0_ffn_setup():
        import jax, jax.numpy as jnp
        import numpy as np
        INPUT_SIZE = 256
        HIDDEN_SIZE = 256
        key = jax.random.key(seed)
        ks = jax.random.split(key, 9)
        B, T, I, H = (64, 256, INPUT_SIZE, HIDDEN_SIZE)
        scale = 1.0 / np.sqrt(I + H)
        x = jax.random.normal(ks[0], (B, T, I), dtype=jnp.float32)

        def lin(kw, kb):
            W = jax.random.uniform(kw, (I + H, H), minval=-scale, maxval=scale, dtype=jnp.float32)
            b = jax.random.uniform(kb, (H,), minval=-scale, maxval=scale, dtype=jnp.float32)
            return (W, b)
        W_f, b_f = lin(ks[1], ks[2])
        W_i, b_i = lin(ks[3], ks[4])
        W_c, b_c = lin(ks[5], ks[6])
        W_o, b_o = lin(ks[7], ks[8])
        return {'x': x, 'W_f': W_f, 'b_f': b_f, 'W_i': W_i, 'b_i': b_i, 'W_c': W_c, 'b_c': b_c, 'W_o': W_o, 'b_o': b_o}
    _L0_ffn_all = _L0_ffn_setup()
    _L0_ffn_in = {k: v for k, v in _L0_ffn_all.items() if k in ('W_f', 'b_f', 'W_i', 'b_i', 'W_c', 'b_c', 'W_o', 'b_o')}
    del _L0_ffn_all

    def _L1_gnn_setup():
        import jax, jax.numpy as jnp
        import numpy as np
        L = 3
        D = 256
        B, N = (8, 512)
        EPS = 1e-05

        def layernorm(x, gamma, beta):
            mu = jnp.mean(x, axis=-1, keepdims=True)
            var = jnp.var(x, axis=-1, keepdims=True)
            return (x - mu) * jax.lax.rsqrt(var + EPS) * gamma + beta
        key = jax.random.key(seed)
        ks = jax.random.split(key, 12)
        s = 1.0 / np.sqrt(D)
        node_features = jax.random.normal(ks[0], (B, N, D), dtype=jnp.float32)
        adjacency_matrix = jax.random.randint(ks[1], (B, N, N), 0, 2, dtype=jnp.int32)
        return {'node_features': node_features, 'adjacency_matrix': adjacency_matrix, 'attn_w': jax.random.normal(ks[2], (L, 2 * D), dtype=jnp.float32) * (1.0 / np.sqrt(2 * D)), 'attn_b': jax.random.normal(ks[3], (L,), dtype=jnp.float32) * 0.01, 'W1': jax.random.normal(ks[4], (L, D, 4 * D), dtype=jnp.float32) * s, 'b1': jnp.zeros((L, 4 * D), dtype=jnp.float32), 'W2': jax.random.normal(ks[5], (L, 4 * D, D), dtype=jnp.float32) * (1.0 / np.sqrt(4 * D)), 'b2': jnp.zeros((L, D), dtype=jnp.float32), 'g1': jnp.ones((L, D), dtype=jnp.float32), 'beta1': jnp.zeros((L, D), dtype=jnp.float32), 'g2': jnp.ones((L, D), dtype=jnp.float32), 'beta2': jnp.zeros((L, D), dtype=jnp.float32)}
    _L1_gnn_all = _L1_gnn_setup()
    _L1_gnn_in = {k: v for k, v in _L1_gnn_all.items() if k in ('attn_w', 'attn_b', 'W1', 'b1', 'W2', 'b2', 'g1', 'beta1', 'g2', 'beta2')}
    del _L1_gnn_all

    def _L1_ffn_setup():
        import jax, jax.numpy as jnp
        import numpy as np
        FP8_MAX = 448.0
        K, N = (256, 256)
        key = jax.random.key(seed)
        kx, kw = jax.random.split(key)
        x = jax.random.normal(kx, (8, 4096, K), dtype=jnp.float32)
        weight = jax.random.normal(kw, (K, N), dtype=jnp.float32) * 0.02
        return {'x': x, 'weight': weight}
    _L1_ffn_all = _L1_ffn_setup()
    _L1_ffn_in = {k: v for k, v in _L1_ffn_all.items() if k in ('weight',)}
    del _L1_ffn_all
    return {'x': x, 'adj': adj, 'L0_gnn_Wq': _L0_gnn_in['Wq'], 'L0_gnn_bq': _L0_gnn_in['bq'], 'L0_gnn_Wk': _L0_gnn_in['Wk'], 'L0_gnn_bk': _L0_gnn_in['bk'], 'L0_gnn_Wv': _L0_gnn_in['Wv'], 'L0_gnn_bv': _L0_gnn_in['bv'], 'L0_gnn_Wo': _L0_gnn_in['Wo'], 'L0_gnn_bo': _L0_gnn_in['bo'], 'L0_ffn_W_f': _L0_ffn_in['W_f'], 'L0_ffn_b_f': _L0_ffn_in['b_f'], 'L0_ffn_W_i': _L0_ffn_in['W_i'], 'L0_ffn_b_i': _L0_ffn_in['b_i'], 'L0_ffn_W_c': _L0_ffn_in['W_c'], 'L0_ffn_b_c': _L0_ffn_in['b_c'], 'L0_ffn_W_o': _L0_ffn_in['W_o'], 'L0_ffn_b_o': _L0_ffn_in['b_o'], 'L1_gnn_attn_w': _L1_gnn_in['attn_w'], 'L1_gnn_attn_b': _L1_gnn_in['attn_b'], 'L1_gnn_W1': _L1_gnn_in['W1'], 'L1_gnn_b1': _L1_gnn_in['b1'], 'L1_gnn_W2': _L1_gnn_in['W2'], 'L1_gnn_b2': _L1_gnn_in['b2'], 'L1_gnn_g1': _L1_gnn_in['g1'], 'L1_gnn_beta1': _L1_gnn_in['beta1'], 'L1_gnn_g2': _L1_gnn_in['g2'], 'L1_gnn_beta2': _L1_gnn_in['beta2'], 'L1_ffn_weight': _L1_ffn_in['weight']}

def reference(x, adj, L0_gnn_Wq, L0_gnn_bq, L0_gnn_Wk, L0_gnn_bk, L0_gnn_Wv, L0_gnn_bv, L0_gnn_Wo, L0_gnn_bo, L0_ffn_W_f, L0_ffn_b_f, L0_ffn_W_i, L0_ffn_b_i, L0_ffn_W_c, L0_ffn_b_c, L0_ffn_W_o, L0_ffn_b_o, L1_gnn_attn_w, L1_gnn_attn_b, L1_gnn_W1, L1_gnn_b1, L1_gnn_W2, L1_gnn_b2, L1_gnn_g1, L1_gnn_beta1, L1_gnn_g2, L1_gnn_beta2, L1_ffn_weight):
    import jax
    import jax.numpy as jnp

    def _L0_gnn_ref(inputs, adj, Wq, bq, Wk, bk, Wv, bv, Wo, bo):
        import jax, jax.numpy as jnp
        import numpy as np
        EMBED_DIM = 256
        N_HEADS = 8
        HEAD_DIM = EMBED_DIM // N_HEADS
        NEG_INF = -1000000000.0
        bs, n, _ = inputs.shape
        q = (inputs @ Wq + bq).reshape(bs, n, N_HEADS, HEAD_DIM)
        k = (inputs @ Wk + bk).reshape(bs, n, N_HEADS, HEAD_DIM)
        v = (inputs @ Wv + bv).reshape(bs, n, N_HEADS, HEAD_DIM)
        logits = jnp.einsum('bqhd,bkhd->bhqk', q, k) / np.sqrt(HEAD_DIM)
        mask = (adj > 0)[:, None, :, :]
        logits = jnp.where(mask, logits, NEG_INF)
        attn = jax.nn.softmax(logits, axis=-1)
        out = jnp.einsum('bhqk,bkhd->bqhd', attn, v).reshape(bs, n, EMBED_DIM)
        out = out @ Wo + bo
        return jax.nn.relu(out)

    def _L0_ffn_ref(x, W_f, b_f, W_i, b_i, W_c, b_c, W_o, b_o):
        import jax, jax.numpy as jnp
        import numpy as np
        INPUT_SIZE = 256
        HIDDEN_SIZE = 256
        B, T, I = x.shape
        H = W_f.shape[1]
        h0 = jnp.zeros((B, H), dtype=x.dtype)
        c0 = jnp.zeros((B, H), dtype=x.dtype)

        def step(carry, x_t):
            h_prev, c_prev = carry
            combined = jnp.concatenate((x_t, h_prev), axis=1)
            f_t = jax.nn.sigmoid(combined @ W_f + b_f)
            i_t = jax.nn.sigmoid(combined @ W_i + b_i)
            c_tilde = jnp.tanh(combined @ W_c + b_c)
            c_t = f_t * c_prev + i_t * c_tilde
            o_t = jax.nn.sigmoid(combined @ W_o + b_o)
            h_t = o_t * jnp.tanh(c_t)
            return ((h_t, c_t), h_t)
        _, hs = jax.lax.scan(step, (h0, c0), jnp.swapaxes(x, 0, 1))
        return jnp.swapaxes(hs, 0, 1)

    def _L1_gnn_ref(node_features, adjacency_matrix, attn_w, attn_b, W1, b1, W2, b2, g1, beta1, g2, beta2):
        import jax, jax.numpy as jnp
        import numpy as np
        L = 3
        D = 256
        B, N = (8, 512)
        EPS = 1e-05

        def layernorm(x, gamma, beta):
            mu = jnp.mean(x, axis=-1, keepdims=True)
            var = jnp.var(x, axis=-1, keepdims=True)
            return (x - mu) * jax.lax.rsqrt(var + EPS) * gamma + beta
        n = adjacency_matrix.shape[-1]
        mask = adjacency_matrix.astype(jnp.float32) + jnp.eye(n, dtype=jnp.float32) > 0
        x = node_features
        d = x.shape[-1]
        for l in range(attn_w.shape[0]):
            si = x @ attn_w[l, :d]
            sj = x @ attn_w[l, d:]
            scores = si[:, :, None] + sj[:, None, :] + attn_b[l]
            scores = jnp.where(scores >= 0, scores, 0.2 * scores)
            scores = jnp.where(mask, scores, -jnp.inf)
            attn = jax.nn.softmax(scores, axis=-1)
            agg = jnp.einsum('bij,bjd->bid', attn, x)
            h = layernorm(x + agg, g1[l], beta1[l])
            ff = jax.nn.gelu(h @ W1[l] + b1[l], approximate=False) @ W2[l] + b2[l]
            x = layernorm(h + ff, g2[l], beta2[l])
        return x

    def _L1_ffn_ref(x, weight):
        import jax, jax.numpy as jnp
        import numpy as np
        FP8_MAX = 448.0
        K, N = (256, 256)
        B, S, _ = x.shape
        x2d = x.reshape(-1, K)
        x_amax = jnp.max(jnp.abs(x2d))
        x_scale = FP8_MAX / jnp.maximum(x_amax, 1e-12)
        x_fp8 = jnp.clip(x2d * x_scale, -FP8_MAX, FP8_MAX).astype(jnp.float8_e4m3fn)
        w_amax = jnp.max(jnp.abs(weight))
        w_scale = FP8_MAX / jnp.maximum(w_amax, 1e-12)
        w_fp8 = jnp.clip(weight.T * w_scale, -FP8_MAX, FP8_MAX).astype(jnp.float8_e4m3fn)
        res = jnp.matmul(x_fp8.astype(jnp.float32), w_fp8.astype(jnp.float32).T)
        out = res * (1.0 / x_scale * (1.0 / w_scale))
        return out.reshape(B, S, N).astype(x.dtype)
    x = x + _L0_gnn_ref(_layernorm(x, axis=-1), adj, L0_gnn_Wq, L0_gnn_bq, L0_gnn_Wk, L0_gnn_bk, L0_gnn_Wv, L0_gnn_bv, L0_gnn_Wo, L0_gnn_bo)
    x = x + _L0_ffn_ref(_layernorm(x, axis=-1), L0_ffn_W_f, L0_ffn_b_f, L0_ffn_W_i, L0_ffn_b_i, L0_ffn_W_c, L0_ffn_b_c, L0_ffn_W_o, L0_ffn_b_o)
    x = x + _L1_gnn_ref(_layernorm(x, axis=-1), adj, L1_gnn_attn_w, L1_gnn_attn_b, L1_gnn_W1, L1_gnn_b1, L1_gnn_W2, L1_gnn_b2, L1_gnn_g1, L1_gnn_beta1, L1_gnn_g2, L1_gnn_beta2)
    x = x + _L1_ffn_ref(_layernorm(x, axis=-1), L1_ffn_weight)
    return x

_drawn_inputs = setup_inputs


def setup_inputs(seed=0):
    import zlib

    import numpy as np

    out = dict(_drawn_inputs(seed))
    spreads = {'L0_gnn_bq': (0.0, 0.355),
     'L0_gnn_bk': (0.0, 2.0),
     'L0_gnn_bv': (0.0, 0.1),
     'L0_gnn_bo': (0.0, 0.1),
     'L1_gnn_b1': (0.0, 0.1),
     'L1_gnn_b2': (0.0, 0.1),
     'L1_gnn_g1': (1.0, 0.2),
     'L1_gnn_beta1': (0.0, 0.1),
     'L1_gnn_g2': (1.0, 0.2),
     'L1_gnn_beta2': (0.0, 0.1)}
    factors = {'L0_ffn_W_f': 5.04,
     'L0_ffn_b_f': 58.8,
     'L0_ffn_W_i': 3.014,
     'L0_ffn_b_i': 51.448,
     'L0_ffn_W_o': 3.03,
     'L0_ffn_b_o': 47.338,
     'L1_gnn_attn_b': 64.0}
    for name, (base, spread) in spreads.items():
        noise = np.random.default_rng([zlib.crc32(name.encode()), seed]).standard_normal(out[name].shape)
        drawn = base * np.exp(spread * noise) if base else spread * noise
        out[name] = jnp.asarray(drawn.astype(out[name].dtype))
    for name, factor in factors.items():
        out[name] = (out[name] * factor).astype(out[name].dtype)
    return out
```

```python
from contextlib import ExitStack

import concourse.bass as bass
from concourse import mybir

F32 = mybir.dt.float32
BF16 = mybir.dt.bfloat16
I32 = mybir.dt.int32
ALU = mybir.AluOpType
ACT = mybir.ActivationFunctionType
AX = mybir.AxisListType

P = 128
B, N, D = 32, 256, 256
NT = N // P
KC = D // P
H, HD = 8, 32
HG = P // HD
L = 3
FF = 4 * D
MC = FF // P
EPS = 1e-5
MASKED = -1e30
GATES = 4
Q = 4
HQ = D // Q
SEG = 8
FP8_MAX = 448.0


def after(eng, sem, value):
    if isinstance(value, int) and value <= 0:
        return
    eng.wait_ge(sem, value)


def alone(eng, sem, value, passed):
    eng.wait_ge(sem, value)
    eng.sem_inc(passed, 1)


def constants(nc, t):
    with ExitStack() as ctx:
        cleared = ctx.enter_context(nc.semaphore("cleared"))
        made = ctx.enter_context(nc.semaphore("made"))
        with nc.Block() as block:

            @block.gpsimd
            def _(pool):
                pool.memset(t.ident[:, :], 0.0).then_inc(cleared, 1)
                pool.memset(t.ones[:, :], 1.0)
                pool.memset(t.power[:, :], -0.5)
                pool.memset(t.eps[:, :], EPS)
                pool.wait_ge(cleared, 1)
                pool.affine_select(out=t.ident[:, :], in_=t.ident[:, :], compare_op=ALU.not_equal, fill=1.0,
                                   base=0, pattern=[[-1, P]], channel_multiplier=1).then_inc(made, 1)

            @block.vector
            def _(dve):
                dve.wait_ge(made, 1)
                dve.tensor_copy(t.identb[:, :], t.ident[:, :])


def attention_phase(nc, t, a):
    with ExitStack() as ctx:
        def sb(name, shape, dt=F32):
            return ctx.enter_context(nc.sbuf_tensor("a_" + name, shape, dt))

        def ps(name):
            return ctx.enter_context(nc.psum_tensor("a_" + name, [P, 512], F32))

        def sem(name):
            return ctx.enter_context(nc.semaphore("a_" + name))

        wq, wk, wv, wo = (sb(f"w{n}", [P, KC, D]) for n in "qkvo")
        bq_col, bk_col, bqs_col = (sb(n, [P, KC]) for n in ("bq", "bk", "bqs"))
        bv_row, bo_row = sb("bv_row", [P, D]), sb("bo_row", [P, D])
        adj = sb("adj", [P, NT, N], I32)
        mask = sb("mask", [P, NT * N], BF16)
        selfadj = sb("selfadj", [P, NT, N])
        xn, xn2 = sb("xn", [P, NT, D]), sb("xn2", [P, NT, D])
        xnT, qT, kT = (sb(n, [P, KC, N]) for n in ("xnT", "qT", "kT"))
        v = sb("v", [P, NT, D])
        probs = [sb(f"probs{i}", [P, NT, N]) for i in range(2)]
        probsT = [sb(f"probsT{i}", [P, NT, N]) for i in range(HG)]
        rden = sb("rden", [P, N])
        outT = sb("outT", [P, KC, N])
        gated = xn2
        nmax = sb("nmax", [P, H, NT])
        stats1, mv1, veps1, rstd1 = (sb(n, [P, NT, w]) for n, w in (("stats1", 6), ("mv1", 2), ("veps1", 1), ("rstd1", 1)))
        stats2, mv2, veps2, rstd2 = (sb(n, [P, NT, w]) for n, w in (("stats2", 6), ("mv2", 2), ("veps2", 1), ("rstd2", 1)))

        score_bank = [ps("S0"), ps("S1")]
        turn_bank = [ps("T0"), ps("T1")]
        q_bank, k_bank, v_bank, head_bank = ps("Q"), ps("K"), ps("V"), ps("O")

        weights_in, rows_in, bqs_done = sem("weights_in"), sem("rows_in"), sem("bqs_done")
        x_in, adj_in = sem("x_in"), sem("adj_in")
        selfadj_done, mask_done = sem("selfadj_done"), sem("mask_done")
        stats1_done, mv1_done, veps1_done, rstd1_done, xn_done = (
            sem(n) for n in ("stats1_done", "mv1_done", "veps1_done", "rstd1_done", "xn_done"))
        stats2_done, mv2_done, veps2_done, rstd2_done, xn2_done = (
            sem(n) for n in ("stats2_done", "mv2_done", "veps2_done", "rstd2_done", "xn2_done"))
        xnT_ps, xnT_done, xn2T_ps, xn2T_done = sem("xnT_ps"), sem("xnT_done"), sem("xn2T_ps"), sem("xn2T_done")
        q_ps, k_ps, v_ps = sem("q_ps"), sem("k_ps"), sem("v_ps")
        q_done, k_done, v_done = sem("q_done"), sem("k_done"), sem("v_done")
        scores_ps, max_done, probs_done = sem("scores_ps"), sem("max_done"), sem("probs_done")
        turned_ps, even_done, odd_done = sem("turned_ps"), sem("even_done"), sem("odd_done")
        heads_ps, rden_done, heads_done = sem("heads_ps"), sem("rden_done"), sem("heads_done")
        proj_ps, gated_done, x_done = sem("proj_ps"), sem("gated_done"), sem("x_done")

        passed = sem("passed")
        with nc.Block() as block:

            @block.sync
            def _(sp):
                def load(b):
                    sp.wait_ge(x_in, b * 16)
                    sp.dma_start(t.x[:, b, :, :], a["x"][b].rearrange("(t p) d -> p t d", p=P)).then_inc(x_in, 16)
                    sp.wait_ge(mask_done, b)
                    sp.dma_start(adj[:, :, :], a["adj"][b].rearrange("(t p) d -> p t d", p=P)).then_inc(adj_in, 16)

                load(0)
                for w, src in ((wq, a["L0_gnn_Wq"]), (wk, a["L0_gnn_Wk"]), (wv, a["L0_gnn_Wv"]), (wo, a["L0_gnn_Wo"])):
                    sp.dma_start(w[:, :, :], src.rearrange("(c p) n -> p c n", p=P)).then_inc(weights_in, 16)
                with nc.allow_non_contiguous_dma(reason="bias columns"):
                    sp.dma_start(bq_col[:, :], a["L0_gnn_bq"].rearrange("(c p) -> p c", p=P)).then_inc(rows_in, 16)
                    sp.dma_start(bk_col[:, :], a["L0_gnn_bk"].rearrange("(c p) -> p c", p=P)).then_inc(rows_in, 16)
                sp.dma_start(bv_row[:, :], a["L0_gnn_bv"].partition_broadcast(P)).then_inc(rows_in, 16)
                sp.dma_start(bo_row[:, :], a["L0_gnn_bo"].partition_broadcast(P)).then_inc(rows_in, 16)
                with sp.Fori(1, B) as b:
                    load(b)

            @block.gpsimd
            def _(pool):
                def rsqrt1(b):
                    pool.wait_ge(mv1_done, b + 1)
                    pool.tensor_tensor(veps1[:, :, 0], mv1[:, :, 1], t.eps[:, :], ALU.add).then_inc(veps1_done, 1)
                    pool.wait_ge(veps1_done, b + 1)
                    pool.tensor_tensor(rstd1[:, :, 0], veps1[:, :, 0], t.power[:, :], ALU.pow).then_inc(rstd1_done, 1)

                def rsqrt2(b):
                    pool.wait_ge(mv2_done, b + 1)
                    pool.tensor_tensor(veps2[:, :, 0], mv2[:, :, 1], t.eps[:, :], ALU.add).then_inc(veps2_done, 1)
                    pool.wait_ge(veps2_done, b + 1)
                    pool.tensor_tensor(rstd2[:, :, 0], veps2[:, :, 0], t.power[:, :], ALU.pow).then_inc(rstd2_done, 1)

                rsqrt1(0)
                with pool.Fori(0, B - 1) as b:
                    rsqrt1(b + 1)
                    rsqrt2(b)
                rsqrt2(B - 1)

            @block.scalar
            def _(act):
                def xnT_out(b):
                    act.wait_ge(xnT_ps, b + 1)
                    act.activation(xnT[:, :, :], q_bank[:, :], ACT.Copy).then_inc(xnT_done, 1)

                def q_out(b):
                    act.wait_ge(q_ps, b + 1)
                    for c in range(KC):
                        last = act.activation(qT[:, c, :], q_bank[:, c * N:(c + 1) * N], ACT.Identity,
                                              bias=bqs_col[:, c:c + 1], scale=HD ** -0.5)
                    last.then_inc(q_done, 1)

                def k_out(b):
                    act.wait_ge(k_ps, b + 1)
                    for c in range(KC):
                        last = act.activation(kT[:, c, :], k_bank[:, c * N:(c + 1) * N], ACT.Identity,
                                              bias=bk_col[:, c:c + 1])
                    last.then_inc(k_done, 1)

                def exponent(b, h):
                    act.wait_ge(max_done, b * H + h + 1)
                    after(act, turned_ps, b * H + h - 1)
                    for it in range(NT):
                        last = act.activation(probs[h % 2][:, it, :], score_bank[h % 2][:, it * N:(it + 1) * N],
                                              ACT.Exp, bias=nmax[:, h, it:it + 1])
                    last.then_inc(probs_done, 1)

                def even_out(b, h):
                    act.wait_ge(turned_ps, b * H + h + 1)
                    after(act, heads_ps, b * 2 + h // HG - 0 if h >= HG else b * 2)
                    act.activation(probsT[h % HG][:, :, :], turn_bank[0][:, :], ACT.Copy).then_inc(even_done, 1)

                def graph(b, has_next):
                    for h in range(H):
                        exponent(b, h)
                        if h == H - 1 and has_next:
                            xnT_out(b + 1)
                        if h % 2 == 1:
                            even_out(b, h - 1)
                    if has_next:
                        q_out(b + 1)
                        k_out(b + 1)

                xnT_out(0)
                act.wait_ge(bqs_done, 1)
                q_out(0)
                k_out(0)
                graph(0, True)
                with act.Fori(1, B - 1) as b:
                    graph(b, True)
                graph(B - 1, False)

            @block.vector
            def _(dve):
                def masks(b):
                    dve.wait_ge(adj_in, b * 16 + 16)
                    after(dve, scores_ps, b * H)
                    dve.tensor_scalar(mask[:, :], adj[:, :, :].rearrange("p t n -> p (t n)"), 0.0, MASKED,
                                      ALU.is_le, ALU.mult)
                    for it in range(NT):
                        own, rest = slice(it * P, (it + 1) * P), slice((1 - it) * P, (2 - it) * P)
                        dve.tensor_tensor(selfadj[:, it, own], adj[:, it, own], t.ident[:, :], ALU.add)
                        last = dve.tensor_copy(selfadj[:, it, rest], adj[:, it, rest])
                    last.then_inc(selfadj_done, 1)
                    dve.wait_ge(selfadj_done, b + 1)
                    dve.tensor_scalar(t.gmask[:, b, :], selfadj[:, :, :].rearrange("p t n -> p (t n)"), 0.0, MASKED,
                                      ALU.is_le, ALU.mult).then_inc(mask_done, 1)

                def moments1(b):
                    alone(dve, x_in, b * 16 + 16, passed)
                    for it in range(NT):
                        last = dve.bn_stats(stats1[:, it, :], t.x[:, b, it, :])
                    last.then_inc(stats1_done, 1)
                    alone(dve, stats1_done, b + 1, passed)
                    for it in range(NT):
                        last = dve.bn_aggr(mv1[:, it, :], stats1[:, it, :])
                    last.then_inc(mv1_done, 1)

                def norm1(b):
                    dve.wait_ge(rstd1_done, b + 1)
                    after(dve, xnT_ps, b)
                    for it in range(NT):
                        last = dve.tensor_scalar(xn[:, it, :], t.x[:, b, it, :], mv1[:, it, 0:1], rstd1[:, it, :],
                                                 ALU.subtract, ALU.mult)
                    last.then_inc(xn_done, 1)

                def v_out(b):
                    dve.wait_ge(v_ps, b + 1)
                    for it in range(NT):
                        last = dve.tensor_tensor(v[:, it, :], v_bank[:, it * D:(it + 1) * D], bv_row[:, :], ALU.add)
                    last.then_inc(v_done, 1)

                def largest(b, h):
                    dve.wait_ge(scores_ps, b * H + h + 1)
                    dve.tensor_reduce(nmax[:, h, :], score_bank[h % 2][:, :].rearrange("p (t k) -> p t k", t=NT), AX.X,
                                      ALU.max, negate=True).then_inc(max_done, 1)

                def odd_out(b, h):
                    dve.wait_ge(turned_ps, b * H + h + 1)
                    after(dve, heads_ps, b * 2 + h // HG)
                    dve.tensor_copy(probsT[h % HG][:, :, :], turn_bank[1][:, :]).then_inc(odd_done, 1)

                def heads_out(b, g):
                    dve.wait_ge(heads_ps, b * 2 + g + 1)
                    after(dve, proj_ps, b)
                    dve.reciprocal(rden[:, :], head_bank[:, N:2 * N]).then_inc(rden_done, 1)
                    dve.wait_ge(rden_done, b * 2 + g + 1)
                    dve.tensor_tensor(outT[:, g, :], head_bank[:, 0:N], rden[:, :], ALU.mult).then_inc(heads_done, 1)

                def residual(b):
                    dve.wait_ge(proj_ps, b + 1)
                    after(dve, xn2T_ps, b)
                    for it in range(NT):
                        last = dve.tensor_tensor(gated[:, it, :], head_bank[:, it * D:(it + 1) * D], bo_row[:, :], ALU.add)
                    last.then_inc(gated_done, 1)
                    dve.wait_ge(gated_done, b + 1)
                    dve.scalar_tensor_tensor(out=t.x[:, b, :, :], in0=gated[:, :, :], scalar=0.0, in1=t.x[:, b, :, :],
                                             op0=ALU.max, op1=ALU.add).then_inc(x_done, 1)
                    alone(dve, x_done, b + 1, passed)
                    for it in range(NT):
                        last = dve.bn_stats(stats2[:, it, :], t.x[:, b, it, :])
                    last.then_inc(stats2_done, 1)
                    alone(dve, stats2_done, b + 1, passed)
                    for it in range(NT):
                        last = dve.bn_aggr(mv2[:, it, :], stats2[:, it, :])
                    last.then_inc(mv2_done, 1)

                def norm2(b):
                    dve.wait_ge(rstd2_done, b + 1)
                    for it in range(NT):
                        last = dve.tensor_scalar(xn2[:, it, :], t.x[:, b, it, :], mv2[:, it, 0:1], rstd2[:, it, :],
                                                 ALU.subtract, ALU.mult)
                    last.then_inc(xn2_done, 1)

                def xn2T_out(b):
                    dve.wait_ge(xn2T_ps, b + 1)
                    dve.tensor_copy(t.seq[:, :, :, b], k_bank[:, :].rearrange("p (c n) -> p c n", c=KC)).then_inc(xn2T_done, 1)

                def graph(b, has_prev, has_next):
                    largest(b, 0)
                    largest(b, 1)
                    if has_prev:
                        norm2(b - 1)
                    largest(b, 2)
                    odd_out(b, 1)
                    largest(b, 3)
                    if has_prev:
                        xn2T_out(b - 1)
                    if has_next:
                        moments1(b + 1)
                    largest(b, 4)
                    odd_out(b, 3)
                    largest(b, 5)
                    heads_out(b, 0)
                    if has_next:
                        norm1(b + 1)
                    largest(b, 6)
                    odd_out(b, 5)
                    largest(b, 7)
                    if has_next:
                        masks(b + 1)
                    odd_out(b, 7)
                    heads_out(b, 1)
                    residual(b)
                    if has_next:
                        v_out(b + 1)

                moments1(0)
                norm1(0)
                masks(0)
                dve.wait_ge(rows_in, 4 * 16)
                dve.tensor_scalar(bqs_col[:, :], bq_col[:, :], HD ** -0.5, None, ALU.mult).then_inc(bqs_done, 1)
                v_out(0)
                graph(0, False, True)
                with dve.Fori(1, B - 1) as b:
                    graph(b, True, True)
                graph(B - 1, True, False)
                norm2(B - 1)
                xn2T_out(B - 1)

            @block.tensor
            def _(pe):
                def turn(bank, x):
                    for c in range(KC):
                        for it in range(NT):
                            last = pe.transpose(bank[:, c * N + it * P:c * N + (it + 1) * P], x[:, it, c * P:(c + 1) * P],
                                                t.ident[:, :])
                    return last

                def turn_xn(b):
                    pe.wait_ge(xn_done, b + 1)
                    after(pe, q_done, b)
                    turn(q_bank, xn).then_inc(xnT_ps, 1)

                def turn_xn2(b):
                    pe.wait_ge(xn2_done, b + 1)
                    pe.wait_ge(k_done, min(b + 2, B) if isinstance(b, int) else b + 2)
                    turn(k_bank, xn2).then_inc(xn2T_ps, 1)

                def queries_keys(b):
                    pe.wait_ge(xnT_done, b + 1)
                    after(pe, xn2T_done, b - 1)
                    for w, bank, done in ((wq, q_bank, q_ps), (wk, k_bank, k_ps)):
                        for m in range(KC):
                            for c in range(KC):
                                last = pe.matmul(bank[:, m * N:(m + 1) * N], w[:, c, m * P:(m + 1) * P], xnT[:, c, :],
                                                 start=(c == 0), stop=(c == KC - 1))
                        last.then_inc(done, 1)

                def values(b):
                    after(pe, v_done, b)
                    for it in range(NT):
                        for c in range(KC):
                            last = pe.matmul(v_bank[:, it * D:(it + 1) * D], xnT[:, c, it * P:(it + 1) * P], wv[:, c, :],
                                             start=(c == 0), stop=(c == KC - 1))
                    last.then_inc(v_ps, 1)

                def scores(b, h):
                    if h == 0:
                        pe.wait_ge(q_done, b + 1)
                        pe.wait_ge(k_done, b + 1)
                        pe.wait_ge(mask_done, b + 1)
                    after(pe, probs_done, b * H + h - 1)
                    o, c, bank = HD * (h % HG), h // HG, score_bank[h % 2]
                    pe.matmul(bank[:, :], t.identb[:, :], mask[:, :], start=True, stop=False, skip_group_check=True)
                    for it in range(NT):
                        last = pe.matmul(bank[:, it * N:(it + 1) * N], qT[o:o + HD, c, it * P:(it + 1) * P],
                                         kT[o:o + HD, c, :], start=False, stop=True, skip_group_check=True)
                    last.then_inc(scores_ps, 1)

                def turn_probs(b, h):
                    pe.wait_ge(probs_done, b * H + h + 1)
                    after(pe, odd_done if h % 2 else even_done, b * (H // 2) + h // 2)
                    for kt in range(NT):
                        for it in range(NT):
                            last = pe.transpose(turn_bank[h % 2][:, kt * N + it * P:kt * N + (it + 1) * P],
                                                probs[h % 2][:, it, kt * P:(kt + 1) * P], t.ident[:, :])
                    last.then_inc(turned_ps, 1)

                def weigh(b, g):
                    pe.wait_ge(even_done, b * (H // 2) + 2 * g + 2)
                    pe.wait_ge(odd_done, b * (H // 2) + 2 * g + 2)
                    pe.wait_ge(v_done, b + 1)
                    if g == 0:
                        after(pe, gated_done, b)
                    else:
                        pe.wait_ge(heads_done, b * 2 + 1)
                    for part in range(2):
                        for kt in range(NT):
                            for j in range(HG):
                                h = g * HG + j
                                w = v[:, kt, h * HD:(h + 1) * HD] if part == 0 else t.ones[:, 0:HD]
                                last = pe.matmul(head_bank[j * HD:(j + 1) * HD, part * N:(part + 1) * N], w,
                                                 probsT[j][:, kt, :], start=(kt == 0), stop=(kt == NT - 1),
                                                 tile_position=(0, j * HD))
                    last.then_inc(heads_ps, 1)

                def project(b):
                    pe.wait_ge(heads_done, b * 2 + 2)
                    for it in range(NT):
                        for c in range(KC):
                            last = pe.matmul(head_bank[:, it * D:(it + 1) * D], outT[:, c, it * P:(it + 1) * P],
                                             wo[:, c, :], start=(c == 0), stop=(c == KC - 1))
                    last.then_inc(proj_ps, 1)

                def graph(b, has_prev, has_next):
                    scores(b, 0)
                    scores(b, 1)
                    turn_probs(b, 0)
                    scores(b, 2)
                    turn_probs(b, 1)
                    scores(b, 3)
                    if has_prev:
                        turn_xn2(b - 1)
                    turn_probs(b, 2)
                    scores(b, 4)
                    turn_probs(b, 3)
                    scores(b, 5)
                    weigh(b, 0)
                    turn_probs(b, 4)
                    scores(b, 6)
                    turn_probs(b, 5)
                    scores(b, 7)
                    if has_next:
                        turn_xn(b + 1)
                    turn_probs(b, 6)
                    turn_probs(b, 7)
                    if has_next:
                        queries_keys(b + 1)
                    weigh(b, 1)
                    project(b)
                    if has_next:
                        values(b + 1)

                turn_xn(0)
                pe.wait_ge(weights_in, 4 * 16)
                queries_keys(0)
                values(0)
                graph(0, False, True)
                with pe.Fori(1, B - 1) as b:
                    graph(b, True, True)
                graph(B - 1, True, False)
                turn_xn2(B - 1)


def lstm_phase(nc, t, a, hidden):
    with ExitStack() as ctx:
        def sb(name, shape, dt=F32):
            return ctx.enter_context(nc.sbuf_tensor("l_" + name, shape, dt))

        def sem(name):
            return ctx.enter_context(nc.semaphore("l_" + name))

        wx, wh = sb("wx", [P, KC, GATES, D]), sb("wh", [P, KC, GATES, D])
        bias = sb("bias", [P, GATES, HQ])
        xt = [sb(f"xt{i}", [P, KC, B]) for i in range(2)]
        hT = sb("hT", [P, KC, B])
        cell = sb("cell", [P, HQ])
        fi, og, cand = sb("fi", [P, 2, HQ]), sb("og", [P, HQ]), sb("cand", [P, HQ])
        kept, fresh, tanh_c = sb("kept", [P, HQ]), sb("fresh", [P, HQ]), sb("tanh_c", [P, HQ])
        hs = [sb(f"hs{i}", [P, SEG, HQ]) for i in range(2)]
        gate_bank = [ctx.enter_context(nc.psum_tensor(f"l_G{i}", [P, 512], F32)) for i in range(2)]

        weights_in = sem("weights_in")
        xt_done, xt_free, hT_done = sem("xt_done"), sem("xt_free"), sem("hT_done")
        gates_ps, fi_done, cand_done, og_done, tanh_done = (
            sem(n) for n in ("gates_ps", "fi_done", "cand_done", "og_done", "tanh_done"))
        fresh_done, cell_done, h_done = sem("fresh_done"), sem("cell_done"), sem("h_done")
        stored = [sem("stored0"), sem("stored1")]
        STEPS = 2 * SEG
        names = ("f", "i", "o", "c")
        n_weights = 16 * (GATES + GATES * KC * Q + GATES * Q)

        with nc.Block() as block:

            @block.sync
            def _(sp):
                for g, n in enumerate(names):
                    w, b = a[f"L0_ffn_W_{n}"], a[f"L0_ffn_b_{n}"]
                    sp.dma_start(wx[:, :, g, :], w[0:D, :].rearrange("(c p) n -> p c n", p=P)).then_inc(weights_in, 16)
                    rows = w[D:2 * D, :].rearrange("(j c d) n -> j c d n", j=Q, c=KC)
                    for j in range(Q):
                        part = slice(j * B, (j + 1) * B)
                        for c in range(KC):
                            sp.dma_start(wh[part, c, g, :], rows[j, c]).then_inc(weights_in, 16)
                        sp.dma_start(bias[part, g, :], b[j * HQ:(j + 1) * HQ].partition_broadcast(B)).then_inc(weights_in, 16)
                with sp.Fori(0, N // STEPS) as s:
                    for half in range(2):
                        sp.wait_ge(h_done, s * STEPS + (half + 1) * SEG)
                        for j in range(Q):
                            sp.dma_start(hidden[:, bass.ds(s * STEPS + half * SEG, SEG), j * HQ:(j + 1) * HQ],
                                         hs[half][j * B:(j + 1) * B, :, :]).then_inc(stored[half], 16)
                for half in range(2):
                    sp.wait_ge(stored[half], N // STEPS * Q * 16)

            @block.gpsimd
            def _(pool):
                with pool.Fori(0, N // 2) as s:
                    for i in range(2):
                        pool.wait_ge(xt_free, s * 2 + i + 1)
                        pool.tensor_copy(xt[i][:, :, :], t.seq[:, :, s * 2 + i, :]).then_inc(xt_done, 1)

            @block.tensor
            def _(pe):
                def step(n, u):
                    bank = gate_bank[u % 2]
                    pe.matmul(bank[:, 0:D], t.ident[:, :], bias[:, :, :], start=True, stop=False, skip_group_check=True)
                    pe.wait_ge(xt_done, n + 1)
                    for c in range(KC):
                        for j in range(Q):
                            last = pe.matmul(bank[j * B:(j + 1) * B, 0:D], xt[u % 2][:, c, :],
                                             wx[:, c, :, j * HQ:(j + 1) * HQ], start=False, stop=False,
                                             skip_group_check=True, tile_position=(0, j * B))
                    last.then_inc(xt_free, 1)
                    pe.wait_ge(hT_done, n + 1)
                    for c in range(KC):
                        for j in range(Q):
                            last = pe.matmul(bank[j * B:(j + 1) * B, 0:D], hT[:, c, :],
                                             wh[:, c, :, j * HQ:(j + 1) * HQ], start=False, stop=(c == KC - 1),
                                             skip_group_check=True, tile_position=(0, j * B))
                    last.then_inc(gates_ps, 1)

                pe.sem_inc(xt_free, 2)
                pe.wait_ge(weights_in, n_weights)
                with pe.Fori(0, N // STEPS) as s:
                    for u in range(STEPS):
                        step(s * STEPS + u, u)

            @block.scalar
            def _(act):
                def step(n, u):
                    bank = gate_bank[u % 2]
                    act.wait_ge(gates_ps, n + 1)
                    act.activation(fi[:, :, :], bank[:, 0:2 * HQ], ACT.Sigmoid).then_inc(fi_done, 1)
                    act.activation(cand[:, :], bank[:, 3 * HQ:4 * HQ], ACT.Tanh).then_inc(cand_done, 1)
                    act.activation(og[:, :], bank[:, 2 * HQ:3 * HQ], ACT.Sigmoid).then_inc(og_done, 1)
                    act.wait_ge(cell_done, n + 2)
                    act.activation(tanh_c[:, :], cell[:, :], ACT.Tanh).then_inc(tanh_done, 1)

                with act.Fori(0, N // STEPS) as s:
                    for u in range(STEPS):
                        step(s * STEPS + u, u)

            @block.vector
            def _(dve):
                def step(s, u):
                    n, half = s * STEPS + u, u // SEG
                    dve.wait_ge(fi_done, n + 1)
                    dve.wait_ge(cell_done, n + 1)
                    dve.tensor_tensor(kept[:, :], fi[:, 0, :], cell[:, :], ALU.mult)
                    dve.wait_ge(cand_done, n + 1)
                    dve.tensor_tensor(fresh[:, :], fi[:, 1, :], cand[:, :], ALU.mult).then_inc(fresh_done, 1)
                    dve.wait_ge(fresh_done, n + 1)
                    dve.tensor_tensor(cell[:, :], kept[:, :], fresh[:, :], ALU.add).then_inc(cell_done, 1)
                    if u % SEG == 0:
                        dve.wait_ge(stored[half], s * Q * 16)
                    dve.wait_ge(og_done, n + 1)
                    dve.wait_ge(tanh_done, n + 1)
                    dve.tensor_tensor(hs[half][:, u % SEG, :], og[:, :], tanh_c[:, :], ALU.mult).then_inc(h_done, 1)
                    dve.wait_ge(h_done, n + 1)
                    dve.transpose(hT[:, :, :], hs[half][:, u % SEG, :]).then_inc(hT_done, 1)

                dve.memset(cell[:, :], 0.0).then_inc(cell_done, 1)
                dve.memset(hT[:, :, :], 0.0).then_inc(hT_done, 1)
                with dve.Fori(0, N // STEPS) as s:
                    for u in range(STEPS):
                        step(s, u)


def nodes_phase(nc, t, a, hidden):
    with ExitStack() as ctx:
        def sb(name, shape, dt=F32):
            return ctx.enter_context(nc.sbuf_tensor("n_" + name, shape, dt))

        def sem(name):
            return ctx.enter_context(nc.semaphore("n_" + name))

        aw = sb("aw", [P, 2, D])
        product = sb("product", [P, D])
        hs = [sb(f"hs{i}", [P, NT, D]) for i in range(2)]
        stats, mv, veps, rstd = ([sb(f"{n}{i}", [P, NT, w]) for i in range(2)]
                                 for n, w in (("stats", 6), ("mv", 2), ("veps", 1), ("rstd", 1)))
        aw_in, product_done = sem("aw_in"), sem("product_done")
        hs_in, x_done, stats_done, mv_done, veps_done, rstd_done, norm_done = (
            [sem(f"{n}{i}") for i in range(2)]
            for n in ("hs_in", "x_done", "stats_done", "mv_done", "veps_done", "rstd_done", "norm_done"))

        passed = sem("passed")
        with nc.Block() as block:

            @block.sync
            def _(sp):
                sp.dma_start(aw[:, :, :], a["L1_gnn_attn_w"][0].rearrange("(s d) -> s d", s=2).partition_broadcast(P)
                             ).then_inc(aw_in, 16)
                with sp.Fori(0, B // 2) as g:
                    for i in range(2):
                        sp.wait_ge(x_done[i], g)
                        sp.dma_start(hs[i][:, :, :], hidden[g * 2 + i].rearrange("(t p) d -> p t d", p=P)
                                     ).then_inc(hs_in[i], 16)

            @block.gpsimd
            def _(pool):
                with pool.Fori(0, B // 2) as g:
                    for i in range(2):
                        b = g * 2 + i
                        pool.wait_ge(hs_in[i], g * 16 + 16)
                        pool.tensor_tensor(t.x[:, b, :, :], t.x[:, b, :, :], hs[i][:, :, :], ALU.add).then_inc(x_done[i], 1)
                    for i in range(2):
                        pool.wait_ge(mv_done[i], g + 1)
                        pool.tensor_tensor(veps[i][:, :, 0], mv[i][:, :, 1], t.eps[:, :], ALU.add).then_inc(veps_done[i], 1)
                        pool.wait_ge(veps_done[i], g + 1)
                        pool.tensor_tensor(rstd[i][:, :, 0], veps[i][:, :, 0], t.power[:, :], ALU.pow).then_inc(rstd_done[i], 1)

            @block.vector
            def _(dve):
                dve.wait_ge(aw_in, 16)
                with dve.Fori(0, B // 2) as g:
                    for i in range(2):
                        alone(dve, x_done[i], g + 1, passed)
                        for it in range(NT):
                            last = dve.bn_stats(stats[i][:, it, :], t.x[:, g * 2 + i, it, :])
                        last.then_inc(stats_done[i], 1)
                        alone(dve, stats_done[i], g + 1, passed)
                        for it in range(NT):
                            last = dve.bn_aggr(mv[i][:, it, :], stats[i][:, it, :])
                        last.then_inc(mv_done[i], 1)
                    for i in range(2):
                        b = g * 2 + i
                        dve.wait_ge(rstd_done[i], g + 1)
                        for it in range(NT):
                            last = dve.tensor_scalar(t.nodes[:, b, it, :], t.x[:, b, it, :], mv[i][:, it, 0:1],
                                                     rstd[i][:, it, :], ALU.subtract, ALU.mult)
                        last.then_inc(norm_done[i], 1)
                        dve.wait_ge(norm_done[i], g + 1)
                        for k in range(2 * NT):
                            it, s = k // 2, k % 2
                            dve.wait_ge(product_done, b * 2 * NT + k)
                            dve.scalar_tensor_tensor(out=product[:, :], in0=t.nodes[:, b, it, :], scalar=1.0,
                                                     in1=aw[:, s, :], op0=ALU.mult, op1=ALU.mult,
                                                     accum_out=t.pair[:, b, it, s:s + 1]).then_inc(product_done, 1)


def gnn_phase(nc, t, a):
    with ExitStack() as ctx:
        def sb(name, shape, dt=F32):
            return ctx.enter_context(nc.sbuf_tensor("g_" + name, shape, dt))

        def ps(name):
            return ctx.enter_context(nc.psum_tensor("g_" + name, [P, 512], F32))

        def sem(name):
            return ctx.enter_context(nc.semaphore("g_" + name))

        w1, w2 = sb("w1", [P, KC, FF]), sb("w2", [P, MC, D])
        aw = sb("aw", [P, 2, D])
        g1_row, beta1_row, b2_row, g2_row, beta2_row = (
            sb(n, [P, D]) for n in ("g1_row", "beta1_row", "b2_row", "g2_row", "beta2_row"))
        g1_col, beta1_col, b1_col, ab_col = sb("g1_col", [P, KC]), sb("beta1_col", [P, KC]), sb("b1_col", [P, MC]), sb("ab_col", [P, 1])
        warm = sb("warm", [P, NT])
        diag = sb("diag", [P, NT, P])
        own, top, lead = sb("own", [P, NT]), sb("top", [P, NT]), sb("lead", [P, NT])
        most, shift, shift2 = sb("most", [P, NT]), sb("shift", [P, NT]), sb("shift2", [P, NT])
        probs = sb("probs", [P, NT, N])
        total, rtotal = sb("total", [P, NT]), sb("rtotal", [P, NT])
        probsT = sb("probsT", [P, NT, N])
        r1, h, hT = sb("r1", [P, NT, D]), sb("h", [P, NT, D]), sb("hT", [P, KC, N])
        steep = r1
        act1 = sb("act1", [P, MC, N])
        r2 = sb("r2", [P, NT, D])
        product = sb("product", [P, D])
        stats1, mv1, veps1, rstd1 = (sb(n, [P, NT, w]) for n, w in (("stats1", 6), ("mv1", 2), ("veps1", 1), ("rstd1", 1)))
        stats2, mv2, veps2, rstd2 = (sb(n, [P, NT, w]) for n, w in (("stats2", 6), ("mv2", 2), ("veps2", 1), ("rstd2", 1)))

        score_bank, turn_bank, agg_bank, ff_bank = ps("S"), ps("T"), ps("A"), ps("F")
        hidden_bank = [ps(f"H{q}") for q in range(MC // 2)]
        NB = MC // 2

        att_in, net_in, finish_in = sem("att_in"), sem("net_in"), sem("finish_in")
        ATT_IN, NET_IN, FINISH_IN = 6 * 16, 3 * 16, 3 * 16
        pair_done, nodes_done = sem("pair_done"), sem("nodes_done")
        (diag_done, scores_ps, own_done, top_done, lead_done, most_done, shift_done, exp_done, probs_done,
         rtotal_done, turned_ps, turned_done, agg_ps, r1_done, stats1_done, mv1_done, veps1_done, rstd1_done,
         norm1_done, hg_done, h_done, hT_ps, hT_done, hidden_ps, gelu_done, ff_ps, r2_done, stats2_done,
         mv2_done, veps2_done, rstd2_done, norm2_done, scaled_done, product_done) = (sem(n) for n in (
            "diag_done", "scores_ps", "own_done", "top_done", "lead_done", "most_done", "shift_done", "exp_done",
            "probs_done", "rtotal_done", "turned_ps", "turned_done", "agg_ps", "r1_done", "stats1_done", "mv1_done",
            "veps1_done", "rstd1_done", "norm1_done", "hg_done", "h_done", "hT_ps", "hT_done",
            "hidden_ps", "gelu_done", "ff_ps", "r2_done", "stats2_done", "mv2_done", "veps2_done", "rstd2_done",
            "norm2_done", "scaled_done", "product_done"))
        rows_done, warm_done = sem("rows_done"), sem("warm_done")

        def walk(eng, start, body, end):
            start((0, 0))
            body((0, 1), (0, 0), None)
            with eng.Fori(0, L - 1) as l:
                with eng.Fori(1, B - 1) as b:
                    body((l, b + 1), (l, b), (l, b - 1))
                body((l + 1, 0), (l, B - 1), (l, B - 2))
                body((l + 1, 1), (l + 1, 0), (l, B - 1))
            with eng.Fori(1, B - 1) as b:
                body((L - 1, b + 1), (L - 1, b), (L - 1, b - 1))
            body(None, (L - 1, B - 1), (L - 1, B - 2))
            end((L - 1, B - 1))

        passed = sem("passed")
        with nc.Block() as block:

            @block.sync
            def _(sp):
                for l in range(L):
                    after(sp, h_done, l * B)
                    after(sp, hT_done, l * B)
                    row = lambda name, dst, done: sp.dma_start(dst[:, :], a[name][l].partition_broadcast(P)).then_inc(done, 16)
                    row("L1_gnn_g1", g1_row, att_in)
                    row("L1_gnn_beta1", beta1_row, att_in)
                    row("L1_gnn_b2", b2_row, att_in)
                    with nc.allow_non_contiguous_dma(reason="columns"):
                        sp.dma_start(g1_col[:, :], a["L1_gnn_g1"][l].rearrange("(c p) -> p c", p=P)).then_inc(att_in, 16)
                        sp.dma_start(beta1_col[:, :], a["L1_gnn_beta1"][l].rearrange("(c p) -> p c", p=P)).then_inc(att_in, 16)
                        sp.dma_start(ab_col[:, :], a["L1_gnn_attn_b"][l:l + 1].partition_broadcast(P)).then_inc(att_in, 16)
                    after(sp, ff_ps, l * B)
                    sp.dma_start(w1[:, :, :], a["L1_gnn_W1"][l].rearrange("(c p) n -> p c n", p=P)).then_inc(net_in, 16)
                    sp.dma_start(w2[:, :, :], a["L1_gnn_W2"][l].rearrange("(c p) n -> p c n", p=P)).then_inc(net_in, 16)
                    with nc.allow_non_contiguous_dma(reason="columns"):
                        sp.dma_start(b1_col[:, :], a["L1_gnn_b1"][l].rearrange("(c p) -> p c", p=P)).then_inc(net_in, 16)
                    after(sp, nodes_done, l * B)
                    sp.wait_ge(pair_done, (l + 1) * B)
                    row("L1_gnn_g2", g2_row, finish_in)
                    row("L1_gnn_beta2", beta2_row, finish_in)
                    sp.dma_start(aw[:, :, :], a["L1_gnn_attn_w"][min(l + 1, L - 1)].rearrange("(s d) -> s d", s=2
                                 ).partition_broadcast(P)).then_inc(finish_in, 16)

            @block.gpsimd
            def _(pool):
                def rsqrt1(l, b):
                    n = l * B + b
                    pool.wait_ge(mv1_done, n + 1)
                    pool.tensor_tensor(veps1[:, :, 0], mv1[:, :, 1], t.eps[:, :], ALU.add).then_inc(veps1_done, 1)
                    pool.wait_ge(veps1_done, n + 1)
                    pool.tensor_tensor(rstd1[:, :, 0], veps1[:, :, 0], t.power[:, :], ALU.pow).then_inc(rstd1_done, 1)

                def residual(l, b):
                    n = l * B + b
                    if isinstance(b, int) and b == 0:
                        pool.wait_ge(att_in, (l + 1) * ATT_IN)
                        pool.tensor_tensor(beta1_row[:, :], beta1_row[:, :], b2_row[:, :], ALU.add).then_inc(rows_done, 1)
                    pool.wait_ge(norm1_done, n + 1)
                    after(pool, r2_done, n)
                    for it in range(NT):
                        last = pool.tensor_tensor(h[:, it, :], r1[:, it, :], g1_row[:, :], ALU.mult)
                    last.then_inc(hg_done, 1)
                    pool.wait_ge(hg_done, n + 1)
                    pool.wait_ge(rows_done, l + 1)
                    for it in range(NT):
                        last = pool.tensor_tensor(h[:, it, :], h[:, it, :], beta1_row[:, :], ALU.add)
                    last.then_inc(h_done, 1)

                def finish(l, b):
                    n = l * B + b
                    pool.wait_ge(mv2_done, n + 1)
                    pool.tensor_tensor(veps2[:, :, 0], mv2[:, :, 1], t.eps[:, :], ALU.add).then_inc(veps2_done, 1)
                    pool.wait_ge(veps2_done, n + 1)
                    pool.tensor_tensor(rstd2[:, :, 0], veps2[:, :, 0], t.power[:, :], ALU.pow).then_inc(rstd2_done, 1)
                    pool.wait_ge(norm2_done, n + 1)
                    pool.wait_ge(finish_in, (l + 1) * FINISH_IN)
                    for it in range(NT):
                        last = pool.tensor_tensor(r2[:, it, :], r2[:, it, :], g2_row[:, :], ALU.mult)
                    last.then_inc(scaled_done, 1)
                    pool.wait_ge(scaled_done, n + 1)
                    for it in range(NT):
                        last = pool.tensor_tensor(t.nodes[:, b, it, :], r2[:, it, :], beta2_row[:, :], ALU.add)
                    last.then_inc(nodes_done, 1)

                def body(ahead, now, behind):
                    residual(*now)
                    if behind:
                        finish(*behind)
                    if ahead:
                        rsqrt1(*ahead)

                walk(pool, lambda at: rsqrt1(*at), body, lambda at: finish(*at))

            @block.scalar
            def _(act):
                def attend(l, b):
                    n = l * B + b
                    after(act, warm_done, n)
                    act.activation(warm[:, :], t.eps[:, :], ACT.Exp).then_inc(warm_done, 1)
                    act.wait_ge(shift_done, n + 1)
                    after(act, turned_ps, n)
                    after(act, hT_ps, n)
                    after(act, h_done, n)
                    for it in range(NT):
                        act.activation(probs[:, it, :], score_bank[:, it * N:(it + 1) * N], ACT.Exp, bias=shift[:, it:it + 1])
                        last = act.activation(steep[:, it, :], score_bank[:, it * N:(it + 1) * N], ACT.Exp,
                                              bias=shift2[:, it:it + 1], scale=0.2)
                    last.then_inc(exp_done, 1)

                def feed(l, b):
                    n = l * B + b
                    act.wait_ge(net_in, (l + 1) * NET_IN)
                    after(act, ff_ps, n)
                    for q in range(NB):
                        act.wait_ge(hidden_ps, n * NB + q + 1)
                        for i in range(2):
                            last = act.activation(act1[:, 2 * q + i, :], hidden_bank[q][:, i * N:(i + 1) * N], ACT.Gelu,
                                                  bias=b1_col[:, 2 * q + i:2 * q + i + 1])
                        last.then_inc(gelu_done, 1)

                def body(ahead, now, behind):
                    if ahead:
                        attend(*ahead)
                    feed(*now)

                walk(act, lambda at: attend(*at), body, lambda at: None)

            @block.vector
            def _(dve):
                def as_neighbour(l, b):
                    n = l * B + b
                    pair = t.pair[:, b, :, :]
                    dve.wait_ge(pair_done, n + 1)
                    after(dve, scores_ps, n)
                    for it in range(NT):
                        last = dve.tensor_scalar(diag[:, it, :], t.ident[:, :], pair[:, it, 1:2], None, ALU.mult)
                    last.then_inc(diag_done, 1)

                def largest(l, b):
                    n = l * B + b
                    dve.wait_ge(att_in, (l + 1) * ATT_IN)
                    dve.tensor_scalar(own[:, :], t.pair[:, b, :, 0], ab_col[:, 0:1], None, ALU.add).then_inc(own_done, 1)
                    dve.wait_ge(scores_ps, n + 1)
                    dve.tensor_reduce(top[:, :], score_bank[:, :].rearrange("p (t k) -> p t k", t=NT), AX.X,
                                      ALU.max).then_inc(top_done, 1)
                    dve.wait_ge(top_done, n + 1)
                    dve.wait_ge(own_done, n + 1)
                    dve.tensor_tensor(lead[:, :], top[:, :], own[:, :], ALU.add).then_inc(lead_done, 1)
                    dve.wait_ge(lead_done, n + 1)
                    dve.scalar_tensor_tensor(out=most[:, :], in0=lead[:, :], scalar=0.2, in1=lead[:, :], op0=ALU.mult,
                                             op1=ALU.max).then_inc(most_done, 1)
                    dve.wait_ge(most_done, n + 1)
                    after(dve, exp_done, n)
                    dve.tensor_tensor(shift[:, :], own[:, :], most[:, :], ALU.subtract)
                    dve.scalar_tensor_tensor(out=shift2[:, :], in0=own[:, :], scalar=0.2, in1=most[:, :], op0=ALU.mult,
                                             op1=ALU.subtract).then_inc(shift_done, 1)

                def larger(l, b):
                    n = l * B + b
                    dve.wait_ge(exp_done, n + 1)
                    for it in range(NT):
                        last = dve.scalar_tensor_tensor(out=probs[:, it, :], in0=probs[:, it, :], scalar=1.0,
                                                        in1=steep[:, it, :], op0=ALU.mult, op1=ALU.max,
                                                        accum_out=total[:, it:it + 1])
                    last.then_inc(probs_done, 1)
                    dve.wait_ge(probs_done, n + 1)
                    dve.reciprocal(rtotal[:, :], total[:, :]).then_inc(rtotal_done, 1)

                def turned(l, b):
                    n = l * B + b
                    dve.wait_ge(turned_ps, n + 1)
                    after(dve, agg_ps, n)
                    dve.tensor_copy(probsT[:, :, :], turn_bank[:, :]).then_inc(turned_done, 1)

                def norm1(l, b):
                    n = l * B + b
                    dve.wait_ge(agg_ps, n + 1)
                    dve.wait_ge(rtotal_done, n + 1)
                    after(dve, hT_ps, n)
                    after(dve, h_done, n)
                    for it in range(NT):
                        last = dve.scalar_tensor_tensor(out=r1[:, it, :], in0=agg_bank[:, it * D:(it + 1) * D],
                                                        scalar=rtotal[:, it:it + 1], in1=t.nodes[:, b, it, :],
                                                        op0=ALU.mult, op1=ALU.add)
                    last.then_inc(r1_done, 1)
                    alone(dve, r1_done, n + 1, passed)
                    for it in range(NT):
                        last = dve.bn_stats(stats1[:, it, :], r1[:, it, :])
                    last.then_inc(stats1_done, 1)
                    alone(dve, stats1_done, n + 1, passed)
                    for it in range(NT):
                        last = dve.bn_aggr(mv1[:, it, :], stats1[:, it, :])
                    last.then_inc(mv1_done, 1)
                    dve.wait_ge(rstd1_done, n + 1)
                    for it in range(NT):
                        last = dve.tensor_scalar(r1[:, it, :], r1[:, it, :], mv1[:, it, 0:1], rstd1[:, it, :],
                                                 ALU.subtract, ALU.mult)
                    last.then_inc(norm1_done, 1)
                    dve.wait_ge(hT_ps, n + 1)
                    after(dve, hidden_ps, n * NB)
                    for c in range(KC):
                        last = dve.tensor_scalar(hT[:, c, :], turn_bank[:, c * N:(c + 1) * N], g1_col[:, c:c + 1],
                                                 beta1_col[:, c:c + 1], ALU.mult, ALU.add)
                    last.then_inc(hT_done, 1)

                def feed(l, b):
                    n = l * B + b
                    dve.wait_ge(ff_ps, n + 1)
                    dve.wait_ge(h_done, n + 1)
                    after(dve, nodes_done, n)
                    dve.tensor_tensor(r2[:, :, :], ff_bank[:, :].rearrange("p (t d) -> p t d", t=NT), h[:, :, :],
                                      ALU.add).then_inc(r2_done, 1)
                    alone(dve, r2_done, n + 1, passed)
                    for it in range(NT):
                        last = dve.bn_stats(stats2[:, it, :], r2[:, it, :])
                    last.then_inc(stats2_done, 1)
                    alone(dve, stats2_done, n + 1, passed)
                    for it in range(NT):
                        last = dve.bn_aggr(mv2[:, it, :], stats2[:, it, :])
                    last.then_inc(mv2_done, 1)

                def norm2(l, b):
                    n = l * B + b
                    dve.wait_ge(rstd2_done, n + 1)
                    for it in range(NT):
                        last = dve.tensor_scalar(r2[:, it, :], r2[:, it, :], mv2[:, it, 0:1], rstd2[:, it, :],
                                                 ALU.subtract, ALU.mult)
                    last.then_inc(norm2_done, 1)

                def next_pair(l, b):
                    n = l * B + b
                    dve.wait_ge(nodes_done, n + 1)
                    dve.wait_ge(finish_in, (l + 1) * FINISH_IN)
                    for k in range(2 * NT):
                        it, s = k // 2, k % 2
                        dve.wait_ge(product_done, n * (2 * NT - 1) + k) if k < 2 * NT - 1 else dve.wait_ge(product_done, (n + 1) * (2 * NT - 1))
                        if k == 0:
                            dve.wait_ge(pair_done, B + n)
                        ins = dve.scalar_tensor_tensor(out=product[:, :], in0=t.nodes[:, b, it, :], scalar=1.0,
                                                       in1=aw[:, s, :], op0=ALU.mult, op1=ALU.mult,
                                                       accum_out=t.pair[:, b, it, s:s + 1])
                        ins.then_inc(product_done if k < 2 * NT - 1 else pair_done, 1)

                def start(at):
                    as_neighbour(*at)
                    largest(*at)
                    larger(*at)
                    turned(*at)
                    norm1(*at)

                def body(ahead, now, behind):
                    if ahead:
                        as_neighbour(*ahead)
                    if behind:
                        feed(*behind)
                    if ahead:
                        largest(*ahead)
                    if behind:
                        norm2(*behind)
                    if ahead:
                        larger(*ahead)
                        turned(*ahead)
                    if behind:
                        next_pair(*behind)
                    if ahead:
                        norm1(*ahead)

                def end(at):
                    feed(*at)
                    norm2(*at)
                    next_pair(*at)

                dve.sem_inc(pair_done, B)
                walk(dve, start, body, end)

            @block.tensor
            def _(pe):
                def scores(l, b):
                    n = l * B + b
                    pe.wait_ge(diag_done, n + 1)
                    after(pe, exp_done, n)
                    pe.matmul(score_bank[:, :], t.identb[:, :], t.gmask[:, b, :], start=True, stop=False,
                              skip_group_check=True)
                    for it in range(NT):
                        for jt in range(NT):
                            last = pe.matmul(score_bank[:, it * N + jt * P:it * N + (jt + 1) * P], t.ones[:, :],
                                             diag[:, jt, :], start=False, stop=True, skip_group_check=True)
                    last.then_inc(scores_ps, 1)

                def turn_probs(l, b):
                    n = l * B + b
                    pe.wait_ge(probs_done, n + 1)
                    after(pe, hT_done, n)
                    for jt in range(NT):
                        for it in range(NT):
                            last = pe.transpose(turn_bank[:, jt * N + it * P:jt * N + (it + 1) * P],
                                                probs[:, it, jt * P:(jt + 1) * P], t.ident[:, :])
                    last.then_inc(turned_ps, 1)

                def aggregate(l, b):
                    n = l * B + b
                    pe.wait_ge(turned_done, n + 1)
                    after(pe, r1_done, n)
                    for it in range(NT):
                        for jt in range(NT):
                            last = pe.matmul(agg_bank[:, it * D:(it + 1) * D], probsT[:, jt, it * P:(it + 1) * P],
                                             t.nodes[:, b, jt, :], start=(jt == 0), stop=(jt == NT - 1))
                    last.then_inc(agg_ps, 1)

                def turn_h(l, b):
                    n = l * B + b
                    pe.wait_ge(norm1_done, n + 1)
                    pe.wait_ge(turned_done, n + 1)
                    for c in range(KC):
                        for it in range(NT):
                            last = pe.transpose(turn_bank[:, c * N + it * P:c * N + (it + 1) * P],
                                                r1[:, it, c * P:(c + 1) * P], t.ident[:, :])
                    last.then_inc(hT_ps, 1)

                def up(l, b, chunks):
                    n = l * B + b
                    if chunks[0] == 0:
                        pe.wait_ge(hT_done, n + 1)
                        pe.wait_ge(net_in, (l + 1) * NET_IN)
                        after(pe, gelu_done, n * NB)
                    for m in chunks:
                        for c in range(KC):
                            last = pe.matmul(hidden_bank[m // 2][:, m % 2 * N:(m % 2 + 1) * N],
                                             w1[:, c, m * P:(m + 1) * P], hT[:, c, :], start=(c == 0), stop=(c == KC - 1))
                        if m % 2 == 1:
                            last.then_inc(hidden_ps, 1)

                def down(l, b, chunks):
                    n = l * B + b
                    if chunks[0] == 0:
                        after(pe, r2_done, n)
                    for m in chunks:
                        if m % 2 == 0:
                            pe.wait_ge(gelu_done, n * NB + m // 2 + 1)
                        for it in range(NT):
                            last = pe.matmul(ff_bank[:, it * D:(it + 1) * D], act1[:, m, it * P:(it + 1) * P],
                                             w2[:, m, :], start=(m == 0 and it == 0), stop=(m == MC - 1),
                                             skip_group_check=True)
                        if m == MC - 1:
                            last.then_inc(ff_ps, 1)

                def start(at):
                    scores(*at)
                    turn_probs(*at)
                    aggregate(*at)
                    turn_h(*at)

                def body(ahead, now, behind):
                    up(*now, range(0, 2))
                    if ahead:
                        scores(*ahead)
                    up(*now, range(2, MC - 1))
                    if ahead:
                        turn_probs(*ahead)
                    up(*now, range(MC - 1, MC))
                    down(*now, range(0, 1))
                    if ahead:
                        aggregate(*ahead)
                    down(*now, range(1, 6))
                    if ahead:
                        turn_h(*ahead)
                    down(*now, range(6, MC))

                walk(pe, start, body, lambda at: None)


def last_phase(nc, t, a, out):
    STEP = float(2 ** 20)
    LEAST = 1.5 * 2 ** 14
    EXPONENT, HALF = 0x7F800000, 0x00400000
    U32 = mybir.dt.uint32
    with ExitStack() as ctx:
        def sb(name, shape, dt=F32):
            return ctx.enter_context(nc.sbuf_tensor("q_" + name, shape, dt))

        def sem(name):
            return ctx.enter_context(nc.semaphore("q_" + name))

        weight, wstep, wsum = (sb(n, [P, KC, D]) for n in ("weight", "wstep", "wsum"))
        wq = sb("wq", [P, KC, D], BF16)
        most, mosts, tops = sb("most", [P, 2]), sb("mosts", [P, B]), sb("tops", [P, 2])
        floor, inv, scale, rscale, oscale = (sb(n, [P, 2]) for n in ("floor", "inv", "scale", "rscale", "oscale"))
        stats, mv, veps, rstd = ([sb(f"{n}{i}", [P, NT, w]) for i in range(2)]
                                 for n, w in (("stats", 6), ("mv", 2), ("veps", 1), ("rstd", 1)))
        val, step_of, total = ([sb(f"{n}{i}", [P, NT, D]) for i in range(2)] for n in ("val", "step", "total"))
        xq = [sb(f"xq{i}", [P, NT, D], BF16) for i in range(2)]
        xqT = [sb(f"xqT{i}", [P, KC, N], BF16) for i in range(2)]
        res = [sb(f"res{i}", [P, NT, D]) for i in range(2)]
        turn_bank = [ctx.enter_context(nc.psum_tensor(f"q_T{i}", [P, 1024], BF16)) for i in range(2)]
        out_bank = [ctx.enter_context(nc.psum_tensor(f"q_O{i}", [P, 512], F32)) for i in range(2)]

        weight_in, most_done, tops_done, math_done, wq_done, wchain = (
            sem(n) for n in ("weight_in", "most_done", "tops_done", "math_done", "wq_done", "wchain"))
        (x_done, stats_done, mv_done, veps_done, rstd_done, norm_done, scaled_done, val_done, power_done, step_done,
         sum_done, xq_done, turned_ps, turned_done, out_ps, res_done, stored) = ([sem(f"{n}{i}") for i in range(2)] for n in (
            "x_done", "stats_done", "mv_done", "veps_done", "rstd_done", "norm_done", "scaled_done", "val_done",
            "power_done", "step_done", "sum_done", "xq_done", "turned_ps", "turned_done", "out_ps", "res_done", "stored"))
        G = B // 2

        passed = sem("passed")
        with nc.Block() as block:

            @block.sync
            def _(sp):
                sp.dma_start(weight[:, :, :], a["L1_ffn_weight"].rearrange("(c p) n -> p c n", p=P)).then_inc(weight_in, 16)
                with sp.Fori(0, G) as g:
                    for i in range(2):
                        sp.wait_ge(res_done[i], g + 1)
                        sp.dma_start(out[g * 2 + i].rearrange("(t p) d -> p t d", p=P), res[i][:, :, :]).then_inc(stored[i], 16)
                for i in range(2):
                    sp.wait_ge(stored[i], G * 16)

            @block.gpsimd
            def _(pool):
                with pool.Fori(0, G) as g:
                    for i in range(2):
                        b = g * 2 + i
                        pool.tensor_tensor(t.x[:, b, :, :], t.x[:, b, :, :], t.nodes[:, b, :, :], ALU.add).then_inc(x_done[i], 1)
                    for i in range(2):
                        pool.wait_ge(mv_done[i], g + 1)
                        pool.tensor_tensor(veps[i][:, :, 0], mv[i][:, :, 1], t.eps[:, :], ALU.add).then_inc(veps_done[i], 1)
                        pool.wait_ge(veps_done[i], g + 1)
                        pool.tensor_tensor(rstd[i][:, :, 0], veps[i][:, :, 0], t.power[:, :], ALU.pow).then_inc(rstd_done[i], 1)
                pool.wait_ge(most_done, 2)
                pool.partition_all_reduce(tops[:, :], most[:, :], P, bass.bass_isa.ReduceOp.max).then_inc(tops_done, 1)
                with pool.Fori(0, G) as g:
                    for i in range(2):
                        pool.wait_ge(step_done[i], g + 1)
                        pool.tensor_tensor(total[i][:, :, :], val[i][:, :, :], step_of[i][:, :, :], ALU.add).then_inc(sum_done[i], 1)
                        pool.wait_ge(sum_done[i], g + 1)
                        pool.wait_ge(turned_ps[i], g)
                        pool.tensor_tensor(xq[i][:, :, :], total[i][:, :, :], step_of[i][:, :, :], ALU.subtract).then_inc(xq_done[i], 1)

            @block.scalar
            def _(act):
                with act.Fori(0, G) as g:
                    for i in range(2):
                        act.wait_ge(turned_ps[i], g + 1)
                        act.wait_ge(out_ps[i], g)
                        act.activation(xqT[i][:, :, :], turn_bank[i][:, 0:KC * N], ACT.Copy).then_inc(turned_done[i], 1)

            @block.tensor
            def _(pe):
                pe.wait_ge(wq_done, 1)
                with pe.Fori(0, G) as g:
                    for i in range(2):
                        pe.wait_ge(xq_done[i], g + 1)
                        pe.wait_ge(turned_done[i], g)
                        for c in range(KC):
                            for it in range(NT):
                                last = pe.transpose(turn_bank[i][:, c * N + it * P:c * N + (it + 1) * P],
                                                    xq[i][:, it, c * P:(c + 1) * P], t.identb[:, :])
                        last.then_inc(turned_ps[i], 1)
                        pe.wait_ge(turned_done[i], g + 1)
                        pe.wait_ge(res_done[i], g)
                        for it in range(NT):
                            for c in range(KC):
                                last = pe.matmul(out_bank[i][:, it * D:(it + 1) * D], xqT[i][:, c, it * P:(it + 1) * P],
                                                 wq[:, c, :], start=(c == 0), stop=(c == KC - 1))
                        last.then_inc(out_ps[i], 1)

            @block.vector
            def _(dve):
                with dve.Fori(0, G) as g:
                    for i in range(2):
                        alone(dve, x_done[i], g + 1, passed)
                        for it in range(NT):
                            last = dve.bn_stats(stats[i][:, it, :], t.x[:, g * 2 + i, it, :])
                        last.then_inc(stats_done[i], 1)
                        alone(dve, stats_done[i], g + 1, passed)
                        for it in range(NT):
                            last = dve.bn_aggr(mv[i][:, it, :], stats[i][:, it, :])
                        last.then_inc(mv_done[i], 1)
                    for i in range(2):
                        b = g * 2 + i
                        dve.wait_ge(rstd_done[i], g + 1)
                        for it in range(NT):
                            last = dve.tensor_scalar(t.nodes[:, b, it, :], t.x[:, b, it, :], mv[i][:, it, 0:1],
                                                     rstd[i][:, it, :], ALU.subtract, ALU.mult)
                        last.then_inc(norm_done[i], 1)
                        dve.wait_ge(norm_done[i], g + 1)
                        dve.tensor_reduce(mosts[:, bass.ds(b, 1)], t.nodes[:, b, :, :], AX.XY, ALU.max,
                                          apply_absolute_value=True).then_inc(scaled_done[i], 1)
                dve.wait_ge(scaled_done[0], G)
                dve.wait_ge(scaled_done[1], G)
                dve.tensor_reduce(most[:, 0:1], mosts[:, :], AX.X, ALU.max).then_inc(most_done, 1)
                dve.wait_ge(weight_in, 16)
                dve.tensor_reduce(most[:, 1:2], weight[:, :, :], AX.XY, ALU.max, apply_absolute_value=True).then_inc(most_done, 1)
                dve.wait_ge(tops_done, 1)
                dve.tensor_scalar(floor[:, :], tops[:, :], 1e-12, None, ALU.max).then_inc(math_done, 1)
                dve.wait_ge(math_done, 1)
                dve.reciprocal(inv[:, :], floor[:, :]).then_inc(math_done, 1)
                dve.wait_ge(math_done, 2)
                dve.tensor_scalar(scale[:, :], inv[:, :], FP8_MAX, None, ALU.mult).then_inc(math_done, 1)
                dve.wait_ge(math_done, 3)
                dve.reciprocal(rscale[:, :], scale[:, :]).then_inc(math_done, 1)
                dve.wait_ge(math_done, 4)
                dve.tensor_tensor(oscale[:, 0:1], rscale[:, 0:1], rscale[:, 1:2], ALU.mult).then_inc(math_done, 1)
                dve.wait_ge(math_done, 5)

                dve.tensor_scalar(weight[:, :, :], weight[:, :, :], scale[:, 1:2], FP8_MAX, ALU.mult, ALU.min).then_inc(wchain, 1)
                dve.wait_ge(wchain, 1)
                dve.tensor_scalar(weight[:, :, :], weight[:, :, :], -FP8_MAX, None, ALU.max).then_inc(wchain, 1)
                dve.wait_ge(wchain, 2)
                dve.tensor_scalar(wstep[:, :, :].bitcast(U32), weight[:, :, :].bitcast(U32), EXPONENT, HALF,
                                  ALU.bitwise_and, ALU.bitwise_or).then_inc(wchain, 1)
                dve.wait_ge(wchain, 3)
                dve.tensor_scalar(wstep[:, :, :], wstep[:, :, :], STEP, LEAST, ALU.mult, ALU.max).then_inc(wchain, 1)
                dve.wait_ge(wchain, 4)
                dve.tensor_tensor(wsum[:, :, :], weight[:, :, :], wstep[:, :, :], ALU.add).then_inc(wchain, 1)
                dve.wait_ge(wchain, 5)
                dve.tensor_tensor(wq[:, :, :], wsum[:, :, :], wstep[:, :, :], ALU.subtract).then_inc(wq_done, 1)

                def quantise(g, i):
                    b = g * 2 + i
                    dve.wait_ge(xq_done[i], g)
                    dve.tensor_scalar(val[i][:, :, :], t.nodes[:, b, :, :], scale[:, 0:1], FP8_MAX, ALU.mult,
                                      ALU.min).then_inc(val_done[i], 1)
                    dve.wait_ge(val_done[i], g * 2 + 1)
                    dve.tensor_scalar(val[i][:, :, :], val[i][:, :, :], -FP8_MAX, None, ALU.max).then_inc(val_done[i], 1)
                    dve.wait_ge(val_done[i], g * 2 + 2)
                    dve.tensor_scalar(step_of[i][:, :, :].bitcast(U32), val[i][:, :, :].bitcast(U32), EXPONENT, HALF,
                                      ALU.bitwise_and, ALU.bitwise_or).then_inc(power_done[i], 1)
                    dve.wait_ge(power_done[i], g + 1)
                    dve.tensor_scalar(step_of[i][:, :, :], step_of[i][:, :, :], STEP, LEAST, ALU.mult,
                                      ALU.max).then_inc(step_done[i], 1)

                def result(g, i):
                    dve.wait_ge(out_ps[i], g + 1)
                    dve.wait_ge(stored[i], g * 16)
                    dve.scalar_tensor_tensor(out=res[i][:, :, :], in0=out_bank[i][:, :].rearrange("p (t d) -> p t d", t=NT),
                                             scalar=oscale[:, 0:1], in1=t.x[:, g * 2 + i, :, :], op0=ALU.mult,
                                             op1=ALU.add).then_inc(res_done[i], 1)

                with dve.Fori(0, G) as g:
                    for i in range(2):
                        quantise(g, i)
                    for i in range(2):
                        result(g, i)


class Shared:
    pass


def build_program(nc, a, out):
    hidden = nc.dram_tensor("hidden", (B, N, D), F32, kind="Internal").ap()
    t = Shared()
    with ExitStack() as ctx:
        def sb(name, shape, dt=F32):
            return ctx.enter_context(nc.sbuf_tensor(name, shape, dt))

        t.x = sb("x", [P, B, NT, D])
        t.seq = sb("seq", [P, KC, N, B])
        t.nodes = t.seq[:, :, :, :].rearrange("p c n b -> p (c n b)").rearrange("p (g t d) -> p g t d", g=B, t=NT)
        t.pair = sb("pair", [P, B, NT, 2])
        t.gmask = sb("gmask", [P, B, NT * N], BF16)
        t.ident, t.identb, t.ones = sb("ident", [P, P]), sb("identb", [P, P], BF16), sb("ones", [P, P])
        t.eps, t.power = sb("eps", [P, NT]), sb("power", [P, NT])
        constants(nc, t)
        attention_phase(nc, t, a)
        lstm_phase(nc, t, a, hidden)
        nodes_phase(nc, t, a, hidden)
        gnn_phase(nc, t, a)
        last_phase(nc, t, a, out)


_INS = ['x', 'adj', 'L0_gnn_Wq', 'L0_gnn_bq', 'L0_gnn_Wk', 'L0_gnn_bk', 'L0_gnn_Wv', 'L0_gnn_bv', 'L0_gnn_Wo',
        'L0_gnn_bo', 'L0_ffn_W_f', 'L0_ffn_b_f', 'L0_ffn_W_i', 'L0_ffn_b_i', 'L0_ffn_W_c', 'L0_ffn_b_c',
        'L0_ffn_W_o', 'L0_ffn_b_o', 'L1_gnn_attn_w', 'L1_gnn_attn_b', 'L1_gnn_W1', 'L1_gnn_b1', 'L1_gnn_W2',
        'L1_gnn_b2', 'L1_gnn_g1', 'L1_gnn_beta1', 'L1_gnn_g2', 'L1_gnn_beta2', 'L1_ffn_weight']


def kernel(**inputs):
    import numpy as _np
    import concourse.bacc as _bacc
    from concourse import mybir as _mybir
    from concourse.bass_utils import run_bass_kernel_spmd as _run

    nc = _bacc.Bacc("TRN2", target_bir_lowering=False, num_devices=1)
    arrays, args = {}, {}
    for name in _INS:
        x = _np.ascontiguousarray(inputs[name])
        arrays[f"in_{name}_dram"] = x
        args[name] = nc.dram_tensor(f"in_{name}_dram", x.shape, _mybir.dt.from_np(x.dtype), kind="ExternalInput").ap()
    out = nc.dram_tensor("out_0_dram", (B, N, D), F32, kind="ExternalOutput").ap()
    build_program(nc, args, out)
    r = _run(nc, [arrays], core_ids=[0])
    return r.results[0]["out_0_dram"]
```

```python
from contextlib import ExitStack

import numpy as np

import concourse.bass as bass
from concourse import mybir

F32 = mybir.dt.float32
F32R = mybir.dt.float32r
BF16 = mybir.dt.bfloat16
I32 = mybir.dt.int32
ALU = mybir.AluOpType
ACT = mybir.ActivationFunctionType
AX = mybir.AxisListType

P = 128
B, N, D = 32, 256, 256
NT = N // P
KC = D // P
H, HD = 8, 32
HG = P // HD
L = 3
FF = 4 * D
MC = FF // P
EPS = 1e-5
MASKED = -1e30
GATES = 4
Q = 4
HQ = D // Q
SEG = 8
FP8_MAX = 448.0


def after(eng, sem, value):
    if isinstance(value, int) and value <= 0:
        return
    eng.wait_ge(sem, value)


def alone(eng, sem, value, passed):
    eng.wait_ge(sem, value)
    eng.sem_inc(passed, 1)


def constants(nc, t):
    with ExitStack() as ctx:
        cleared = ctx.enter_context(nc.semaphore("cleared"))
        made = ctx.enter_context(nc.semaphore("made"))
        with nc.Block() as block:

            @block.gpsimd
            def _(pool):
                pool.memset(t.ident[:, :], 0.0).then_inc(cleared, 1)
                pool.memset(t.ones[:, :], 1.0)
                pool.memset(t.power[:, :], -0.5)
                pool.memset(t.eps[:, :], EPS)
                pool.wait_ge(cleared, 1)
                pool.affine_select(out=t.ident[:, :], in_=t.ident[:, :], compare_op=ALU.not_equal, fill=1.0,
                                   base=0, pattern=[[-1, P]], channel_multiplier=1).then_inc(made, 1)

            @block.vector
            def _(dve):
                dve.wait_ge(made, 1)
                dve.tensor_copy(t.identb[:, :], t.ident[:, :])


def attention_phase(nc, t, a):
    with ExitStack() as ctx:
        def sb(name, shape, dt=F32):
            return ctx.enter_context(nc.sbuf_tensor("a_" + name, shape, dt))

        def ps(name):
            return ctx.enter_context(nc.psum_tensor("a_" + name, [P, 512], F32))

        def sem(name):
            return ctx.enter_context(nc.semaphore("a_" + name))

        wq, wk, wv, wo = (sb(f"w{n}", [P, KC, D]) for n in "qkvo")
        bq_col, bk_col, bqs_col = (sb(n, [P, KC]) for n in ("bq", "bk", "bqs"))
        bv_row, bo_row = sb("bv_row", [P, D]), sb("bo_row", [P, D])
        adj = sb("adj", [P, NT, N], I32)
        mask = sb("mask", [P, NT * N], BF16)
        selfadj = sb("selfadj", [P, NT, P], BF16)
        xn, xn2 = sb("xn", [P, NT, D]), sb("xn2", [P, NT, D])
        xnT, qT, kT = (sb(n, [P, KC, N]) for n in ("xnT", "qT", "kT"))
        v = sb("v", [P, NT, D])
        probs = [sb(f"probs{i}", [P, NT, N]) for i in range(2)]
        probsT = [sb(f"probsT{i}", [P, NT, N]) for i in range(HG)]
        den, tiny_rden = sb("den", [P, H, NT]), sb("tiny_rden", [P, H, NT])
        spread, rden = xn[:, 0, :].rearrange("p (t j r) -> p t j r", t=NT, j=HG), xn[:, 1, :]
        outT = sb("outT", [P, KC, N])
        gated = xn2
        nmax = sb("nmax", [P, H, NT])
        stats1, mv1, veps1, rstd1 = (sb(n, [P, NT, w]) for n, w in (("stats1", 6), ("mv1", 2), ("veps1", 1), ("rstd1", 1)))
        stats2, mv2, veps2, rstd2 = (sb(n, [P, NT, w]) for n, w in (("stats2", 6), ("mv2", 2), ("veps2", 1), ("rstd2", 1)))

        score_bank = [ps("S0"), ps("S1")]
        turn_bank = [ps("T0"), ps("T1")]
        q_bank, k_bank, v_bank, head_bank = ps("Q"), ps("K"), ps("V"), ps("O")

        weights_in, rows_in, bqs_done = sem("weights_in"), sem("rows_in"), sem("bqs_done")
        x_in, adj_in = sem("x_in"), sem("adj_in")
        selfadj_done, mask_done = sem("selfadj_done"), sem("mask_done")
        stats1_done, mv1_done, veps1_done, rstd1_done, xn_done = (
            sem(n) for n in ("stats1_done", "mv1_done", "veps1_done", "rstd1_done", "xn_done"))
        stats2_done, mv2_done, veps2_done, rstd2_done, xn2_done = (
            sem(n) for n in ("stats2_done", "mv2_done", "veps2_done", "rstd2_done", "xn2_done"))
        xnT_ps, xnT_done, xn2T_ps, xn2T_done = sem("xnT_ps"), sem("xnT_done"), sem("xn2T_ps"), sem("xn2T_done")
        q_ps, k_ps, v_ps = sem("q_ps"), sem("k_ps"), sem("v_ps")
        q_done, k_done, v_done = sem("q_done"), sem("k_done"), sem("v_done")
        scores_ps, max_done, probs_done = sem("scores_ps"), sem("max_done"), sem("probs_done")
        turned_ps, even_done, odd_done = sem("turned_ps"), sem("even_done"), sem("odd_done")
        heads_ps, rden_done, heads_done = sem("heads_ps"), sem("rden_done"), sem("heads_done")
        tiny_done, spread_done = sem("tiny_done"), sem("spread_done")
        proj_ps, gated_done, x_done = sem("proj_ps"), sem("gated_done"), sem("x_done")

        passed = sem("passed")
        with nc.Block() as block:

            @block.sync
            def _(sp):
                def load(b):
                    sp.wait_ge(x_in, b * 16)
                    sp.dma_start(t.x[:, b, :, :], a["x"][b].rearrange("(t p) d -> p t d", p=P)).then_inc(x_in, 16)
                    sp.wait_ge(mask_done, b)
                    sp.dma_start(adj[:, :, :], a["adj"][b].rearrange("(t p) d -> p t d", p=P)).then_inc(adj_in, 16)

                load(0)
                for w, src in ((wq, a["L0_gnn_Wq"]), (wk, a["L0_gnn_Wk"]), (wv, a["L0_gnn_Wv"]), (wo, a["L0_gnn_Wo"])):
                    sp.dma_start(w[:, :, :], src.rearrange("(c p) n -> p c n", p=P)).then_inc(weights_in, 16)
                with nc.allow_non_contiguous_dma(reason="bias columns"):
                    sp.dma_start(bq_col[:, :], a["L0_gnn_bq"].rearrange("(c p) -> p c", p=P)).then_inc(rows_in, 16)
                    sp.dma_start(bk_col[:, :], a["L0_gnn_bk"].rearrange("(c p) -> p c", p=P)).then_inc(rows_in, 16)
                sp.dma_start(bv_row[:, :], a["L0_gnn_bv"].partition_broadcast(P)).then_inc(rows_in, 16)
                sp.dma_start(bo_row[:, :], a["L0_gnn_bo"].partition_broadcast(P)).then_inc(rows_in, 16)
                with sp.Fori(1, B) as b:
                    load(b)

            @block.gpsimd
            def _(pool):
                def rsqrt1(b):
                    pool.wait_ge(mv1_done, b + 1)
                    pool.tensor_tensor(veps1[:, :, 0], mv1[:, :, 1], t.eps[:, :], ALU.add).then_inc(veps1_done, 1)
                    pool.wait_ge(veps1_done, b + 1)
                    pool.tensor_tensor(rstd1[:, :, 0], veps1[:, :, 0], t.power[:, :], ALU.pow).then_inc(rstd1_done, 1)

                def rsqrt2(b):
                    pool.wait_ge(mv2_done, b + 1)
                    pool.tensor_tensor(veps2[:, :, 0], mv2[:, :, 1], t.eps[:, :], ALU.add).then_inc(veps2_done, 1)
                    pool.wait_ge(veps2_done, b + 1)
                    pool.tensor_tensor(rstd2[:, :, 0], veps2[:, :, 0], t.power[:, :], ALU.pow).then_inc(rstd2_done, 1)

                def spread_out(b, g):
                    pool.wait_ge(tiny_done, b * 2 + g + 1)
                    after(pool, heads_ps, b * 2 + g)
                    if g == 0 and not isinstance(b, int):
                        pool.wait_ge(xnT_ps, b + 2)
                    part = tiny_rden[:, g * HG:(g + 1) * HG, :].rearrange("p j t -> p t j").unsqueeze(3)
                    pool.tensor_tensor(spread, part.broadcast_to((P, NT, HG, HD)),
                                       t.ones.unsqueeze(2).unsqueeze(3).broadcast_to((P, NT, HG, HD)),
                                       ALU.mult).then_inc(spread_done, 1)

                def graph(b, has_prev, has_next):
                    if has_next:
                        rsqrt1(b + 1)
                    spread_out(b, 0)
                    if has_prev:
                        rsqrt2(b - 1)
                    spread_out(b, 1)

                rsqrt1(0)
                graph(0, False, True)
                with pool.Fori(1, B - 1) as b:
                    graph(b, True, True)
                graph(B - 1, True, False)
                rsqrt2(B - 1)

            @block.scalar
            def _(act):
                def xnT_out(b):
                    act.wait_ge(xnT_ps, b + 1)
                    act.activation(xnT[:, :, :], q_bank[:, :], ACT.Copy).then_inc(xnT_done, 1)

                def q_out(b):
                    act.wait_ge(q_ps, b + 1)
                    for c in range(KC):
                        last = act.activation(qT[:, c, :], q_bank[:, c * N:(c + 1) * N], ACT.Identity,
                                              bias=bqs_col[:, c:c + 1], scale=HD ** -0.5)
                    last.then_inc(q_done, 1)

                def k_out(b):
                    act.wait_ge(k_ps, b + 1)
                    for c in range(KC):
                        last = act.activation(kT[:, c, :], k_bank[:, c * N:(c + 1) * N], ACT.Identity,
                                              bias=bk_col[:, c:c + 1])
                    last.then_inc(k_done, 1)

                def exponent(b, h):
                    act.wait_ge(max_done, b * H + h + 1)
                    after(act, turned_ps, b * H + h - 1)
                    for it in range(NT):
                        last = act.activation(probs[h % 2][:, it, :], score_bank[h % 2][:, it * N:(it + 1) * N],
                                              ACT.Exp, bias=nmax[:, h, it:it + 1], accum_out=den[:, h, it:it + 1])
                    last.then_inc(probs_done, 1)

                def even_out(b, h):
                    act.wait_ge(turned_ps, b * H + h + 1)
                    after(act, heads_ps, b * 2 + h // HG)
                    act.activation(probsT[h % HG][:, :, :], turn_bank[0][:, :], ACT.Copy).then_inc(even_done, 1)

                def rden_out(b, g):
                    act.wait_ge(heads_ps, b * 2 + g + 1)
                    after(act, heads_done, b * 2 + g)
                    act.activation(rden, head_bank[:, N:2 * N], ACT.Copy).then_inc(rden_done, 1)

                def graph(b, has_next):
                    for h in range(H):
                        exponent(b, h)
                        if h == 5:
                            rden_out(b, 0)
                        if h == 3 and has_next:
                            xnT_out(b + 1)
                        if h == H - 1 and has_next:
                            q_out(b + 1)
                        if h % 2 == 1:
                            even_out(b, h - 1)
                    if has_next:
                        k_out(b + 1)
                    rden_out(b, 1)

                xnT_out(0)
                act.wait_ge(bqs_done, 1)
                q_out(0)
                k_out(0)
                graph(0, True)
                with act.Fori(1, B - 1) as b:
                    graph(b, True)
                graph(B - 1, False)

            @block.vector
            def _(dve):
                def gmasks(b):
                    dve.wait_ge(adj_in, b * 16 + 16)
                    for it in range(NT):
                        last = dve.tensor_tensor(selfadj[:, it, :], adj[:, it, it * P:(it + 1) * P], t.ident[:, :], ALU.add)
                    last.then_inc(selfadj_done, 1)
                    for it in range(NT):
                        dve.tensor_scalar(t.gmask[:, b, (it + 1) * P:(it + 2) * P],
                                          adj[:, it, (1 - it) * P:(2 - it) * P], 0.0, MASKED, ALU.is_le, ALU.mult)
                    dve.wait_ge(selfadj_done, b + 1)
                    for it in range(NT):
                        dve.tensor_scalar(t.gmask[:, b, 3 * it * P:(3 * it + 1) * P], selfadj[:, it, :], 0.0, MASKED,
                                          ALU.is_le, ALU.mult)

                def masks(b):
                    after(dve, scores_ps, b * H)
                    dve.tensor_scalar(mask[:, :], adj[:, :, :].rearrange("p t n -> p (t n)"), 0.0, MASKED,
                                      ALU.is_le, ALU.mult).then_inc(mask_done, 1)

                def moments1(b):
                    alone(dve, x_in, b * 16 + 16, passed)
                    for it in range(NT):
                        last = dve.bn_stats(stats1[:, it, :], t.x[:, b, it, :])
                    last.then_inc(stats1_done, 1)
                    alone(dve, stats1_done, b + 1, passed)
                    for it in range(NT):
                        last = dve.bn_aggr(mv1[:, it, :], stats1[:, it, :])
                    last.then_inc(mv1_done, 1)

                def norm1(b):
                    dve.wait_ge(rstd1_done, b + 1)
                    after(dve, xnT_ps, b)
                    after(dve, heads_ps, (b - 1) * 2)
                    after(dve, heads_done, (b - 1) * 2)
                    for it in range(NT):
                        last = dve.tensor_scalar(xn[:, it, :], t.x[:, b, it, :], mv1[:, it, 0:1], rstd1[:, it, :],
                                                 ALU.subtract, ALU.mult)
                    last.then_inc(xn_done, 1)

                def v_out(b):
                    dve.wait_ge(v_ps, b + 1)
                    for it in range(NT):
                        last = dve.tensor_tensor(v[:, it, :], v_bank[:, it * D:(it + 1) * D], bv_row[:, :], ALU.add)
                    last.then_inc(v_done, 1)

                def largest(b, h):
                    dve.wait_ge(scores_ps, b * H + h + 1)
                    dve.tensor_reduce(nmax[:, h, :], score_bank[h % 2][:, :].rearrange("p (t k) -> p t k", t=NT), AX.X,
                                      ALU.max, negate=True).then_inc(max_done, 1)

                def odd_out(b, h):
                    dve.wait_ge(turned_ps, b * H + h + 1)
                    after(dve, heads_ps, b * 2 + h // HG)
                    dve.tensor_copy(probsT[h % HG][:, :, :], turn_bank[1][:, :]).then_inc(odd_done, 1)

                def reciprocals(b, g):
                    dve.wait_ge(probs_done, b * H + (g + 1) * HG)
                    after(dve, spread_done, b * 2 + g)
                    part = slice(g * HG, (g + 1) * HG)
                    dve.reciprocal(tiny_rden[:, part, :], den[:, part, :]).then_inc(tiny_done, 1)

                def heads_out(b, g):
                    dve.wait_ge(rden_done, b * 2 + g + 1)
                    after(dve, proj_ps, b)
                    dve.tensor_tensor(outT[:, g, :], head_bank[:, 0:N], rden, ALU.mult).then_inc(heads_done, 1)

                def residual(b):
                    dve.wait_ge(proj_ps, b + 1)
                    after(dve, xn2T_ps, b)
                    for it in range(NT):
                        last = dve.tensor_tensor(gated[:, it, :], head_bank[:, it * D:(it + 1) * D], bo_row[:, :], ALU.add)
                    last.then_inc(gated_done, 1)
                    dve.wait_ge(gated_done, b + 1)
                    dve.scalar_tensor_tensor(out=t.x[:, b, :, :], in0=gated[:, :, :], scalar=0.0, in1=t.x[:, b, :, :],
                                             op0=ALU.max, op1=ALU.add).then_inc(x_done, 1)

                def moments2(b):
                    alone(dve, x_done, b + 1, passed)
                    for it in range(NT):
                        last = dve.bn_stats(stats2[:, it, :], t.x[:, b, it, :])
                    last.then_inc(stats2_done, 1)
                    alone(dve, stats2_done, b + 1, passed)
                    for it in range(NT):
                        last = dve.bn_aggr(mv2[:, it, :], stats2[:, it, :])
                    last.then_inc(mv2_done, 1)

                def norm2(b):
                    dve.wait_ge(rstd2_done, b + 1)
                    for it in range(NT):
                        last = dve.tensor_scalar(xn2[:, it, :], t.x[:, b, it, :], mv2[:, it, 0:1], rstd2[:, it, :],
                                                 ALU.subtract, ALU.mult)
                    last.then_inc(xn2_done, 1)

                def xn2T_out(b):
                    dve.wait_ge(xn2T_ps, b + 1)
                    dve.tensor_copy(t.seq[:, :, :, b], turn_bank[0][:, :].rearrange("p (c n) -> p c n", c=KC)).then_inc(xn2T_done, 1)

                def graph(b, has_prev, has_next):
                    largest(b, 0)
                    largest(b, 1)
                    if has_next:
                        moments1(b + 1)
                    v_out(b)
                    largest(b, 2)
                    if has_next:
                        norm1(b + 1)
                    odd_out(b, 1)
                    largest(b, 3)
                    if has_prev:
                        residual(b - 1)
                    largest(b, 4)
                    reciprocals(b, 0)
                    odd_out(b, 3)
                    if has_prev:
                        moments2(b - 1)
                    largest(b, 5)
                    heads_out(b, 0)
                    largest(b, 6)
                    odd_out(b, 5)
                    if has_prev:
                        norm2(b - 1)
                    largest(b, 7)
                    if has_next:
                        gmasks(b + 1)
                        masks(b + 1)
                    reciprocals(b, 1)
                    odd_out(b, 7)
                    if has_prev:
                        xn2T_out(b - 1)
                    heads_out(b, 1)

                moments1(0)
                norm1(0)
                gmasks(0)
                masks(0)
                dve.wait_ge(rows_in, 4 * 16)
                dve.tensor_scalar(bqs_col[:, :], bq_col[:, :], HD ** -0.5, None, ALU.mult).then_inc(bqs_done, 1)
                graph(0, False, True)
                with dve.Fori(1, B - 1) as b:
                    graph(b, True, True)
                graph(B - 1, True, False)
                residual(B - 1)
                moments2(B - 1)
                norm2(B - 1)
                xn2T_out(B - 1)

            @block.tensor
            def _(pe):
                def turn(bank, x):
                    for c in range(KC):
                        for it in range(NT):
                            last = pe.transpose(bank[:, c * N + it * P:c * N + (it + 1) * P], x[:, it, c * P:(c + 1) * P],
                                                t.ident[:, :])
                    return last

                def turn_xn(b):
                    pe.wait_ge(xn_done, b + 1)
                    after(pe, q_done, b)
                    turn(q_bank, xn).then_inc(xnT_ps, 1)

                def turn_xn2(b):
                    pe.wait_ge(xn2_done, b + 1)
                    pe.wait_ge(even_done, (H // 2) * (min(b + 2, B) if isinstance(b, int) else b + 2))
                    turn(turn_bank[0], xn2).then_inc(xn2T_ps, 1)

                def queries(b, m):
                    if m == 0:
                        pe.wait_ge(xnT_done, b + 1)
                    for c in range(KC):
                        last = pe.matmul(q_bank[:, m * N:(m + 1) * N], wq[:, c, m * P:(m + 1) * P], xnT[:, c, :],
                                         start=(c == 0), stop=(c == KC - 1))
                    if m == KC - 1:
                        last.then_inc(q_ps, 1)

                def keys(b, m):
                    if m == 0:
                        after(pe, k_done, b)
                    for c in range(KC):
                        last = pe.matmul(k_bank[:, m * N:(m + 1) * N], wk[:, c, m * P:(m + 1) * P], xnT[:, c, :],
                                         start=(c == 0), stop=(c == KC - 1))
                    if m == KC - 1:
                        last.then_inc(k_ps, 1)

                def values(b):
                    after(pe, v_done, b)
                    for it in range(NT):
                        for c in range(KC):
                            last = pe.matmul(v_bank[:, it * D:(it + 1) * D], xnT[:, c, it * P:(it + 1) * P], wv[:, c, :],
                                             start=(c == 0), stop=(c == KC - 1))
                    last.then_inc(v_ps, 1)

                def scores(b, h):
                    if h == 0:
                        pe.wait_ge(q_done, b + 1)
                        pe.wait_ge(k_done, b + 1)
                        pe.wait_ge(mask_done, b + 1)
                    after(pe, probs_done, b * H + h - 1)
                    o, c, bank = HD * (h % HG), h // HG, score_bank[h % 2]
                    pe.matmul(bank[:, :], t.identb[:, :], mask[:, :], start=True, stop=False, skip_group_check=True)
                    for it in range(NT):
                        last = pe.matmul(bank[:, it * N:(it + 1) * N], qT[o:o + HD, c, it * P:(it + 1) * P],
                                         kT[o:o + HD, c, :], start=False, stop=True, skip_group_check=True)
                    last.then_inc(scores_ps, 1)

                def turn_probs(b, h):
                    pe.wait_ge(probs_done, b * H + h + 1)
                    after(pe, odd_done if h % 2 else even_done, b * (H // 2) + h // 2)
                    if h == 0:
                        after(pe, xn2T_done, b - 1)
                    for kt in range(NT):
                        for it in range(NT):
                            last = pe.transpose(turn_bank[h % 2][:, kt * N + it * P:kt * N + (it + 1) * P],
                                                probs[h % 2][:, it, kt * P:(kt + 1) * P], t.ident[:, :])
                    last.then_inc(turned_ps, 1)

                def weigh(b, g):
                    pe.wait_ge(even_done, b * (H // 2) + 2 * g + 2)
                    pe.wait_ge(odd_done, b * (H // 2) + 2 * g + 2)
                    pe.wait_ge(v_done, b + 1)
                    if g == 0:
                        after(pe, gated_done, b)
                    else:
                        pe.wait_ge(heads_done, b * 2 + 1)
                    for kt in range(NT):
                        for j in range(HG):
                            h = g * HG + j
                            pe.matmul(head_bank[j * HD:(j + 1) * HD, 0:N], v[:, kt, h * HD:(h + 1) * HD],
                                      probsT[j][:, kt, :], start=(kt == 0), stop=(kt == NT - 1), tile_position=(0, j * HD))
                    pe.wait_ge(spread_done, b * 2 + g + 1)
                    for it in range(NT):
                        last = pe.transpose(head_bank[:, N + it * P:N + (it + 1) * P],
                                            spread[:, it, :, :].rearrange("p j r -> p (j r)"), t.ident[:, :])
                    last.then_inc(heads_ps, 1)

                def project(b):
                    pe.wait_ge(heads_done, b * 2 + 2)
                    for it in range(NT):
                        for c in range(KC):
                            last = pe.matmul(head_bank[:, it * D:(it + 1) * D], outT[:, c, it * P:(it + 1) * P],
                                             wo[:, c, :], start=(c == 0), stop=(c == KC - 1))
                    last.then_inc(proj_ps, 1)

                def graph(b, has_prev, has_next):
                    scores(b, 0)
                    scores(b, 1)
                    if has_prev:
                        project(b - 1)
                    turn_probs(b, 0)
                    scores(b, 2)
                    turn_probs(b, 1)
                    scores(b, 3)
                    if has_next:
                        turn_xn(b + 1)
                    turn_probs(b, 2)
                    scores(b, 4)
                    turn_probs(b, 3)
                    if has_next:
                        queries(b + 1, 0)
                    scores(b, 5)
                    if has_next:
                        queries(b + 1, 1)
                    weigh(b, 0)
                    turn_probs(b, 4)
                    scores(b, 6)
                    if has_next:
                        keys(b + 1, 0)
                    turn_probs(b, 5)
                    scores(b, 7)
                    if has_next:
                        values(b + 1)
                    turn_probs(b, 6)
                    turn_probs(b, 7)
                    if has_next:
                        keys(b + 1, 1)
                    if has_prev:
                        turn_xn2(b - 1)
                    weigh(b, 1)

                turn_xn(0)
                pe.wait_ge(weights_in, 4 * 16)
                for m in range(KC):
                    queries(0, m)
                for m in range(KC):
                    keys(0, m)
                values(0)
                graph(0, False, True)
                with pe.Fori(1, B - 1) as b:
                    graph(b, True, True)
                graph(B - 1, True, False)
                project(B - 1)
                turn_xn2(B - 1)


def lstm_phase(nc, t, a, hidden):
    with ExitStack() as ctx:
        def sb(name, shape, dt=F32):
            return ctx.enter_context(nc.sbuf_tensor("l_" + name, shape, dt))

        def sem(name):
            return ctx.enter_context(nc.semaphore("l_" + name))

        wx, wh = sb("wx", [P, KC, GATES, D]), sb("wh", [P, KC, GATES, D])
        bias = sb("bias", [P, GATES, HQ])
        xt = [sb(f"xt{i}", [P, KC, B]) for i in range(2)]
        hT = sb("hT", [P, KC, B])
        cell = sb("cell", [P, HQ])
        fi, og, cand = sb("fi", [P, 2, HQ]), sb("og", [P, HQ]), sb("cand", [P, HQ])
        kept, fresh, tanh_c = sb("kept", [P, HQ]), sb("fresh", [P, HQ]), sb("tanh_c", [P, HQ])
        hs = [sb(f"hs{i}", [P, SEG, HQ]) for i in range(2)]
        gate_bank, o_bank = ([ctx.enter_context(nc.psum_tensor(f"l_{n}{i}", [P, 512], F32)) for i in range(2)] for n in "GO")
        CELL = 3

        weights_in = sem("weights_in")
        xt_done, xt_free, hT_done = sem("xt_done"), sem("xt_free"), sem("hT_done")
        o_ps = sem("o_ps")
        gates_ps, fi_done, cand_done, og_done, tanh_done = (
            sem(n) for n in ("gates_ps", "fi_done", "cand_done", "og_done", "tanh_done"))
        fresh_done, cell_done, h_done = sem("fresh_done"), sem("cell_done"), sem("h_done")
        stored = [sem("stored0"), sem("stored1")]
        STEPS = 2 * SEG
        names = ("f", "i", "c", "o")
        n_weights = 16 * (GATES + GATES * KC * Q + GATES * Q)

        with nc.Block() as block:

            @block.sync
            def _(sp):
                for g, n in enumerate(names):
                    w, b = a[f"L0_ffn_W_{n}"], a[f"L0_ffn_b_{n}"]
                    sp.dma_start(wx[:, :, g, :], w[0:D, :].rearrange("(c p) n -> p c n", p=P)).then_inc(weights_in, 16)
                    rows = w[D:2 * D, :].rearrange("(j c d) n -> j c d n", j=Q, c=KC)
                    for j in range(Q):
                        part = slice(j * B, (j + 1) * B)
                        for c in range(KC):
                            sp.dma_start(wh[part, c, g, :], rows[j, c]).then_inc(weights_in, 16)
                        sp.dma_start(bias[part, g, :], b[j * HQ:(j + 1) * HQ].partition_broadcast(B)).then_inc(weights_in, 16)
                with sp.Fori(0, N // STEPS) as s:
                    for half in range(2):
                        sp.wait_ge(h_done, s * STEPS + (half + 1) * SEG)
                        for j in range(Q):
                            sp.dma_start(hidden[:, bass.ds(s * STEPS + half * SEG, SEG), j * HQ:(j + 1) * HQ],
                                         hs[half][j * B:(j + 1) * B, :, :]).then_inc(stored[half], 16)
                for half in range(2):
                    sp.wait_ge(stored[half], N // STEPS * Q * 16)

            @block.gpsimd
            def _(pool):
                with pool.Fori(0, N // 2) as s:
                    for i in range(2):
                        pool.wait_ge(xt_free, s * 2 + i + 1)
                        pool.tensor_copy(xt[i][:, :, :], t.seq[:, :, s * 2 + i, :]).then_inc(xt_done, 1)

            @block.tensor
            def _(pe):
                def step(n, u):
                    parts = ((gate_bank[u % 2], slice(0, CELL), gates_ps), (o_bank[u % 2], slice(CELL, GATES), o_ps))

                    def multiply(bank, gates, x, w, stop):
                        for c in range(KC):
                            for j in range(Q):
                                last = pe.matmul(bank[j * B:(j + 1) * B, 0:(gates.stop - gates.start) * HQ], x[:, c, :],
                                                 w[:, c, gates, j * HQ:(j + 1) * HQ], start=False,
                                                 stop=(stop and c == KC - 1), skip_group_check=True, tile_position=(0, j * B))
                        return last

                    for bank, gates, _ in parts:
                        pe.matmul(bank[:, 0:(gates.stop - gates.start) * HQ], t.ident[:, :], bias[:, gates, :],
                                  start=True, stop=False, skip_group_check=True)
                    pe.wait_ge(xt_done, n + 1)
                    for bank, gates, _ in parts:
                        last = multiply(bank, gates, xt[u % 2], wx, False)
                    last.then_inc(xt_free, 1)
                    pe.wait_ge(hT_done, n + 1)
                    for bank, gates, done in parts:
                        multiply(bank, gates, hT, wh, True).then_inc(done, 1)

                pe.sem_inc(xt_free, 2)
                pe.wait_ge(weights_in, n_weights)
                with pe.Fori(0, N // STEPS) as s:
                    for u in range(STEPS):
                        step(s * STEPS + u, u)

            @block.scalar
            def _(act):
                def step(n, u):
                    bank = gate_bank[u % 2]
                    act.wait_ge(gates_ps, n + 1)
                    act.activation(fi[:, :, :], bank[:, 0:2 * HQ], ACT.Sigmoid).then_inc(fi_done, 1)
                    act.activation(cand[:, :], bank[:, 2 * HQ:3 * HQ], ACT.Tanh).then_inc(cand_done, 1)
                    act.wait_ge(o_ps, n + 1)
                    act.activation(og[:, :], o_bank[u % 2][:, 0:HQ], ACT.Sigmoid).then_inc(og_done, 1)
                    act.wait_ge(cell_done, n + 2)
                    act.activation(tanh_c[:, :], cell[:, :], ACT.Tanh).then_inc(tanh_done, 1)

                with act.Fori(0, N // STEPS) as s:
                    for u in range(STEPS):
                        step(s * STEPS + u, u)

            @block.vector
            def _(dve):
                def step(s, u):
                    n, half = s * STEPS + u, u // SEG
                    dve.wait_ge(fi_done, n + 1)
                    dve.wait_ge(cell_done, n + 1)
                    dve.tensor_tensor(kept[:, :], fi[:, 0, :], cell[:, :], ALU.mult)
                    dve.wait_ge(cand_done, n + 1)
                    dve.tensor_tensor(fresh[:, :], fi[:, 1, :], cand[:, :], ALU.mult).then_inc(fresh_done, 1)
                    dve.wait_ge(fresh_done, n + 1)
                    dve.tensor_tensor(cell[:, :], kept[:, :], fresh[:, :], ALU.add).then_inc(cell_done, 1)
                    if u % SEG == 0:
                        dve.wait_ge(stored[half], s * Q * 16)
                    dve.wait_ge(og_done, n + 1)
                    dve.wait_ge(tanh_done, n + 1)
                    dve.tensor_tensor(hs[half][:, u % SEG, :], og[:, :], tanh_c[:, :], ALU.mult).then_inc(h_done, 1)
                    dve.wait_ge(h_done, n + 1)
                    dve.transpose(hT[:, :, :], hs[half][:, u % SEG, :]).then_inc(hT_done, 1)

                dve.memset(cell[:, :], 0.0).then_inc(cell_done, 1)
                dve.memset(hT[:, :, :], 0.0).then_inc(hT_done, 1)
                with dve.Fori(0, N // STEPS) as s:
                    for u in range(STEPS):
                        step(s, u)


def gnn_phase(nc, t, a, hidden):
    with ExitStack() as ctx:
        def sb(name, shape, dt=F32):
            return ctx.enter_context(nc.sbuf_tensor("g_" + name, shape, dt))

        def ps(name):
            return ctx.enter_context(nc.psum_tensor("g_" + name, [P, 512], F32))

        def sem(name):
            return ctx.enter_context(nc.semaphore("g_" + name))

        small, used = sb("small", [P, 96]), []

        def tiny(*shape):
            n, at = int(np.prod(shape)), sum(used)
            used.append(n)
            part = small[:, at:at + n]
            return part if len(shape) == 1 else part.rearrange("p (t w) -> p t w", w=shape[1])

        w1, w2 = sb("w1", [P, KC, FF]), sb("w2", [P, MC, D])
        aw, aw_first = sb("aw", [P, 2, D]), sb("aw_first", [P, 2, D])
        g1_row, beta1_row, g2_row, beta2_row = (sb(n, [P, D]) for n in ("g1_row", "beta1_row", "g2_row", "beta2_row"))
        g1_col, beta1_col, b1_col, ab_cols = tiny(KC), tiny(KC), tiny(MC), tiny(L)
        warm = tiny(NT)
        parts = sb("parts", [P, 2, NT], F32R)
        upper, lower = parts[:, 0, :], parts[:, 1, :]
        diag = sb("diag", [P, 2, NT, P], F32R)
        own, top, lead = tiny(NT), tiny(NT), tiny(NT)
        most, shift, shift2 = tiny(NT), tiny(NT), tiny(NT)
        probs = sb("probs", [P, NT, N])
        total, rtotal = tiny(NT), tiny(NT)
        probsT = sb("probsT", [P, NT, N])
        r1, h, hT = sb("r1", [P, NT, D]), sb("h", [P, NT, D]), sb("hT", [P, KC, N])
        steep = r1
        b2_rows = [h[:, 0, :]] + [aw_first[:, 0, :]] * (L - 1)
        product, entered_junk = r1, probs
        hs = probsT
        act1 = sb("act1", [P, MC, N])
        r2 = sb("r2", [P, NT, D])
        stats1, mv1, veps1, rstd1 = (tiny(NT, w) for w in (6, 2, 1, 1))
        stats3, mv3, veps3, rstd3 = (tiny(NT, w) for w in (6, 2, 1, 1))
        stats2, mv2, veps2, rstd2 = (tiny(NT, w) for w in (6, 2, 1, 1))

        score_bank, turn_bank, agg_bank, ff_bank = ps("S"), ps("T"), ps("A"), ps("F")
        hidden_bank = [ps(f"H{q}") for q in range(MC // 2)]
        NB = MC // 2

        att_in, net_in, finish_in = sem("att_in"), sem("net_in"), sem("finish_in")
        ATT_IN, NET_IN, FINISH_IN = 5 * 16, 2 * 16, 2 * 16
        w1_in, aw_in, aw_first_in, hs_in = sem("w1_in"), sem("aw_in"), sem("aw_first_in"), sem("hs_in")
        (entered_x, entered_stats, entered_mv, entered_veps, entered_rstd, entered_nodes, entered_product,
         entered_pair) = (sem("entered_" + n) for n in ("x", "stats", "mv", "veps", "rstd", "nodes", "product", "pair"))
        left_x, left_stats, left_mv, left_veps, left_rstd, left_nodes, left_most = (
            sem("left_" + n) for n in ("x", "stats", "mv", "veps", "rstd", "nodes", "most"))
        pair_done, nodes_done = sem("pair_done"), sem("nodes_done")
        (diag_done, scores_ps, own_done, top_done, lead_done, most_done, shift_done, exp_done, probs_done,
         rtotal_done, turned_ps, turned_done, agg_ps, r1_done, stats1_done, mv1_done, veps1_done, rstd1_done,
         norm1_done, hg_done, h_done, hT_ps, hT_done, hidden_ps, gelu_done, ff_ps, r2_done, stats2_done,
         mv2_done, veps2_done, rstd2_done, norm2_done, scaled_done, product_done) = (sem(n) for n in (
            "diag_done", "scores_ps", "own_done", "top_done", "lead_done", "most_done", "shift_done", "exp_done",
            "probs_done", "rtotal_done", "turned_ps", "turned_done", "agg_ps", "r1_done", "stats1_done", "mv1_done",
            "veps1_done", "rstd1_done", "norm1_done", "hg_done", "h_done", "hT_ps", "hT_done",
            "hidden_ps", "gelu_done", "ff_ps", "r2_done", "stats2_done", "mv2_done", "veps2_done", "rstd2_done",
            "norm2_done", "scaled_done", "product_done"))
        parts_done = sem("parts_done")
        rows_done, warm_done = sem("rows_done"), sem("warm_done")

        def walk(eng, start, body, end):
            start((0, 0))
            body((0, 1), (0, 0), None, 2)
            with eng.Fori(1, B - 2) as b:
                body((0, b + 1), (0, b), (0, b - 1), b + 2)
            body((0, B - 1), (0, B - 2), (0, B - 3), None)
            for l in range(1, L):
                body((l, 0), (l - 1, B - 1), (l - 1, B - 2), None)
                body((l, 1), (l, 0), (l - 1, B - 1), None)
                with eng.Fori(1, B - 1) as b:
                    body((l, b + 1), (l, b), (l, b - 1), None)
            body(None, (L - 1, B - 1), (L - 1, B - 2), None)
            end((L - 1, B - 1))

        passed = sem("passed")
        with nc.Block() as block:

            @block.sync
            def _(sp):
                def load_hidden(e):
                    sp.dma_start(hs[:, :, :], hidden[e].rearrange("(t p) d -> p t d", p=P)).then_inc(hs_in, 16)

                load_hidden(0)
                sp.dma_start(aw_first[:, :, :], a["L1_gnn_attn_w"][0].rearrange("(s d) -> s d", s=2).partition_broadcast(P)
                             ).then_inc(aw_first_in, 16)
                sp.dma_start(ab_cols[:, :], a["L1_gnn_attn_b"].partition_broadcast(P)).then_inc(aw_first_in, 16)
                for l in range(L):
                    after(sp, hidden_ps, l * B * NB)
                    sp.dma_start(w1[:, :, :], a["L1_gnn_W1"][l].rearrange("(c p) n -> p c n", p=P)).then_inc(w1_in, 16)
                    after(sp, h_done, l * B)
                    after(sp, hT_done, l * B)
                    row = lambda name, dst, done: sp.dma_start(dst[:, :], a[name][l].partition_broadcast(P)).then_inc(done, 16)
                    row("L1_gnn_g1", g1_row, att_in)
                    row("L1_gnn_beta1", beta1_row, att_in)
                    after(sp, entered_pair, min(l, 1) * B)
                    row("L1_gnn_b2", b2_rows[l], att_in)
                    with nc.allow_non_contiguous_dma(reason="columns"):
                        sp.dma_start(g1_col[:, :], a["L1_gnn_g1"][l].rearrange("(c p) -> p c", p=P)).then_inc(att_in, 16)
                        sp.dma_start(beta1_col[:, :], a["L1_gnn_beta1"][l].rearrange("(c p) -> p c", p=P)).then_inc(att_in, 16)
                    after(sp, ff_ps, l * B)
                    sp.dma_start(w2[:, :, :], a["L1_gnn_W2"][l].rearrange("(c p) n -> p c n", p=P)).then_inc(net_in, 16)
                    with nc.allow_non_contiguous_dma(reason="columns"):
                        sp.dma_start(b1_col[:, :], a["L1_gnn_b1"][l].rearrange("(c p) -> p c", p=P)).then_inc(net_in, 16)
                    after(sp, nodes_done, l * B)
                    row("L1_gnn_g2", g2_row, finish_in)
                    row("L1_gnn_beta2", beta2_row, finish_in)
                    if l < L - 1:
                        after(sp, pair_done, l * B)
                        sp.dma_start(aw[:, :, :], a["L1_gnn_attn_w"][l + 1].rearrange("(s d) -> s d", s=2
                                     ).partition_broadcast(P)).then_inc(aw_in, 16)
                    if l == 0:
                        sp.wait_ge(entered_x, 1)
                        load_hidden(1)
                        with sp.Fori(2, B) as e:
                            sp.wait_ge(agg_ps, e - 1)
                            load_hidden(e)

            @block.gpsimd
            def _(pool):
                def rsqrt1(l, b):
                    n = l * B + b
                    pool.wait_ge(mv1_done, n + 1)
                    pool.tensor_tensor(veps1[:, :, 0], mv1[:, :, 1], t.eps[:, :], ALU.add).then_inc(veps1_done, 1)
                    pool.wait_ge(veps1_done, n + 1)
                    pool.tensor_tensor(rstd1[:, :, 0], veps1[:, :, 0], t.power[:, :], ALU.pow).then_inc(rstd1_done, 1)

                def residual(l, b):
                    n = l * B + b
                    if isinstance(b, int) and b == 0:
                        pool.wait_ge(att_in, (l + 1) * ATT_IN)
                        pool.tensor_tensor(beta1_row[:, :], beta1_row[:, :], b2_rows[l], ALU.add).then_inc(rows_done, 1)
                        pool.wait_ge(rows_done, l + 1)
                    pool.wait_ge(norm1_done, n + 1)
                    after(pool, r2_done, n)
                    for it in range(NT):
                        last = pool.tensor_tensor(h[:, it, :], r1[:, it, :], g1_row[:, :], ALU.mult)
                    last.then_inc(hg_done, 1)

                def residual_end(l, b):
                    n = l * B + b
                    pool.wait_ge(hg_done, n + 1)
                    for it in range(NT):
                        last = pool.tensor_tensor(h[:, it, :], h[:, it, :], beta1_row[:, :], ALU.add)
                    last.then_inc(h_done, 1)

                def rsqrt2(l, b):
                    n = l * B + b
                    pool.wait_ge(mv2_done, n + 1)
                    pool.tensor_tensor(veps2[:, :, 0], mv2[:, :, 1], t.eps[:, :], ALU.add).then_inc(veps2_done, 1)
                    pool.wait_ge(veps2_done, n + 1)
                    pool.tensor_tensor(rstd2[:, :, 0], veps2[:, :, 0], t.power[:, :], ALU.pow).then_inc(rstd2_done, 1)

                def scale(l, b):
                    n = l * B + b
                    pool.wait_ge(norm2_done, n + 1)
                    pool.wait_ge(finish_in, (l + 1) * FINISH_IN)
                    for it in range(NT):
                        last = pool.tensor_tensor(r2[:, it, :], r2[:, it, :], g2_row[:, :], ALU.mult)
                    last.then_inc(scaled_done, 1)

                def move(l, b):
                    n = l * B + b
                    pool.wait_ge(scaled_done, n + 1)
                    for it in range(NT):
                        last = pool.tensor_tensor(t.nodes[:, b, it, :], r2[:, it, :], beta2_row[:, :], ALU.add)
                    last.then_inc(nodes_done, 1)

                def enter(e):
                    pool.wait_ge(hs_in, e * 16 + 16)
                    pool.tensor_tensor(t.x[:, e, :, :], t.x[:, e, :, :], hs[:, :, :], ALU.add).then_inc(entered_x, 1)

                def rsqrt_entered(e):
                    pool.wait_ge(entered_mv, e + 1)
                    pool.tensor_tensor(veps3[:, :, 0], mv3[:, :, 1], t.eps[:, :], ALU.add).then_inc(entered_veps, 1)
                    pool.wait_ge(entered_veps, e + 1)
                    pool.tensor_tensor(rstd3[:, :, 0], veps3[:, :, 0], t.power[:, :], ALU.pow).then_inc(entered_rstd, 1)

                def leave(b):
                    pool.wait_ge(nodes_done, (L - 1) * B + b + 1)
                    pool.tensor_tensor(t.x[:, b, :, :], t.x[:, b, :, :], t.nodes[:, b, :, :], ALU.add).then_inc(left_x, 1)

                def rsqrt_left(b):
                    pool.wait_ge(left_mv, b + 1)
                    pool.tensor_tensor(veps3[:, :, 0], mv3[:, :, 1], t.eps[:, :], ALU.add).then_inc(left_veps, 1)
                    pool.wait_ge(left_veps, b + 1)
                    pool.tensor_tensor(rstd3[:, :, 0], veps3[:, :, 0], t.power[:, :], ALU.pow).then_inc(left_rstd, 1)

                def start(at):
                    for e in range(2):
                        enter(e)
                        rsqrt_entered(e)
                    rsqrt1(*at)

                def body(ahead, now, behind, entering):
                    if entering is not None:
                        enter(entering)
                    residual(*now)
                    if behind:
                        rsqrt2(*behind)
                        scale(*behind)
                    if entering is not None:
                        rsqrt_entered(entering)
                    leaving = behind and behind[0] == L - 1
                    if behind:
                        move(*behind)
                    if leaving:
                        leave(behind[1])
                    residual_end(*now)
                    if leaving:
                        rsqrt_left(behind[1])
                    if ahead:
                        rsqrt1(*ahead)

                def end(at):
                    rsqrt2(*at)
                    scale(*at)
                    move(*at)
                    leave(at[1])
                    rsqrt_left(at[1])

                walk(pool, start, body, end)

            @block.scalar
            def _(act):
                def attend(l, b):
                    n = l * B + b
                    after(act, warm_done, n)
                    act.activation(warm[:, :], t.eps[:, :], ACT.Exp).then_inc(warm_done, 1)
                    act.wait_ge(shift_done, n + 1)
                    after(act, turned_ps, n)
                    after(act, hT_ps, n)
                    after(act, hg_done, n)
                    for it in range(NT):
                        act.activation(probs[:, it, :], score_bank[:, it * N:(it + 1) * N], ACT.Exp, bias=shift[:, it:it + 1])
                        last = act.activation(steep[:, it, :], score_bank[:, it * N:(it + 1) * N], ACT.Exp,
                                              bias=shift2[:, it:it + 1], scale=0.2)
                    last.then_inc(exp_done, 1)

                def feed(l, b):
                    n = l * B + b
                    act.wait_ge(net_in, (l + 1) * NET_IN)
                    after(act, ff_ps, n)
                    for q in range(NB):
                        act.wait_ge(hidden_ps, n * NB + q + 1)
                        for i in range(2):
                            last = act.activation(act1[:, 2 * q + i, :], hidden_bank[q][:, i * N:(i + 1) * N], ACT.Gelu,
                                                  bias=b1_col[:, 2 * q + i:2 * q + i + 1])
                        last.then_inc(gelu_done, 1)

                def body(ahead, now, behind, entering):
                    if ahead:
                        attend(*ahead)
                    feed(*now)

                walk(act, lambda at: attend(*at), body, lambda at: None)

            @block.vector
            def _(dve):
                def as_neighbour(l, b):
                    n = l * B + b
                    pair = t.pair[:, b, :, :]
                    if l == 0:
                        dve.wait_ge(entered_pair, b + 1)
                    else:
                        dve.wait_ge(pair_done, n - B + 1)
                    after(dve, parts_done, 2 * n)
                    dve.tensor_copy(upper[:, :], pair[:, :, 1]).then_inc(parts_done, 1)
                    dve.wait_ge(parts_done, 2 * n + 1)
                    dve.tensor_tensor(lower[:, :], pair[:, :, 1], upper[:, :].bitcast(F32), ALU.subtract).then_inc(parts_done, 1)
                    after(dve, scores_ps, n)
                    dve.wait_ge(parts_done, 2 * n + 2)
                    for k, part in enumerate((upper, lower)):
                        for it in range(NT):
                            last = dve.tensor_scalar(diag[:, k, it, :], t.ident[:, :], part[:, it:it + 1].bitcast(F32),
                                                     None, ALU.mult)
                    last.then_inc(diag_done, 1)

                def largest(l, b):
                    n = l * B + b
                    dve.tensor_scalar(own[:, :], t.pair[:, b, :, 0], ab_cols[:, l:l + 1], None, ALU.add).then_inc(own_done, 1)
                    dve.wait_ge(scores_ps, n + 1)
                    dve.tensor_reduce(top[:, :], score_bank[:, :].rearrange("p (t k) -> p t k", t=NT), AX.X,
                                      ALU.max).then_inc(top_done, 1)
                    dve.wait_ge(top_done, n + 1)
                    dve.wait_ge(own_done, n + 1)
                    dve.tensor_tensor(lead[:, :], top[:, :], own[:, :], ALU.add).then_inc(lead_done, 1)
                    dve.wait_ge(lead_done, n + 1)
                    dve.scalar_tensor_tensor(out=most[:, :], in0=lead[:, :], scalar=0.2, in1=lead[:, :], op0=ALU.mult,
                                             op1=ALU.max).then_inc(most_done, 1)
                    dve.wait_ge(most_done, n + 1)
                    after(dve, exp_done, n)
                    dve.tensor_tensor(shift[:, :], own[:, :], most[:, :], ALU.subtract)
                    dve.scalar_tensor_tensor(out=shift2[:, :], in0=own[:, :], scalar=0.2, in1=most[:, :], op0=ALU.mult,
                                             op1=ALU.subtract).then_inc(shift_done, 1)

                def larger(l, b):
                    n = l * B + b
                    dve.wait_ge(exp_done, n + 1)
                    for it in range(NT):
                        last = dve.scalar_tensor_tensor(out=probs[:, it, :], in0=probs[:, it, :], scalar=1.0,
                                                        in1=steep[:, it, :], op0=ALU.mult, op1=ALU.max,
                                                        accum_out=total[:, it:it + 1])
                    last.then_inc(probs_done, 1)
                    dve.wait_ge(probs_done, n + 1)
                    dve.reciprocal(rtotal[:, :], total[:, :]).then_inc(rtotal_done, 1)

                def turned(l, b):
                    n = l * B + b
                    dve.wait_ge(turned_ps, n + 1)
                    after(dve, agg_ps, n)
                    if l == 0:
                        dve.wait_ge(entered_x, min(b + 2, B) if isinstance(b, int) else b + 2)
                    dve.tensor_copy(probsT[:, :, :], turn_bank[:, :]).then_inc(turned_done, 1)

                def norm1(l, b, meanwhile):
                    n = l * B + b
                    dve.wait_ge(agg_ps, n + 1)
                    dve.wait_ge(rtotal_done, n + 1)
                    after(dve, hT_ps, n)
                    after(dve, hg_done, n)
                    for it in range(NT):
                        last = dve.scalar_tensor_tensor(out=r1[:, it, :], in0=agg_bank[:, it * D:(it + 1) * D],
                                                        scalar=rtotal[:, it:it + 1], in1=t.nodes[:, b, it, :],
                                                        op0=ALU.mult, op1=ALU.add)
                    last.then_inc(r1_done, 1)
                    alone(dve, r1_done, n + 1, passed)
                    for it in range(NT):
                        last = dve.bn_stats(stats1[:, it, :], r1[:, it, :])
                    last.then_inc(stats1_done, 1)
                    alone(dve, stats1_done, n + 1, passed)
                    for it in range(NT):
                        last = dve.bn_aggr(mv1[:, it, :], stats1[:, it, :])
                    last.then_inc(mv1_done, 1)
                    meanwhile()
                    dve.wait_ge(rstd1_done, n + 1)
                    for it in range(NT):
                        last = dve.tensor_scalar(r1[:, it, :], r1[:, it, :], mv1[:, it, 0:1], rstd1[:, it, :],
                                                 ALU.subtract, ALU.mult)
                    last.then_inc(norm1_done, 1)
                    dve.wait_ge(hT_ps, n + 1)
                    dve.wait_ge(att_in, (l + 1) * ATT_IN)
                    after(dve, hidden_ps, n * NB)
                    for c in range(KC):
                        last = dve.tensor_scalar(hT[:, c, :], turn_bank[:, c * N:(c + 1) * N], g1_col[:, c:c + 1],
                                                 beta1_col[:, c:c + 1], ALU.mult, ALU.add)
                    last.then_inc(hT_done, 1)

                def feed(l, b):
                    n = l * B + b
                    dve.wait_ge(ff_ps, n + 1)
                    dve.wait_ge(h_done, n + 1)
                    after(dve, nodes_done, n)
                    dve.tensor_tensor(r2[:, :, :], ff_bank[:, :].rearrange("p (t d) -> p t d", t=NT), h[:, :, :],
                                      ALU.add).then_inc(r2_done, 1)
                    alone(dve, r2_done, n + 1, passed)
                    for it in range(NT):
                        last = dve.bn_stats(stats2[:, it, :], r2[:, it, :])
                    last.then_inc(stats2_done, 1)
                    alone(dve, stats2_done, n + 1, passed)
                    for it in range(NT):
                        last = dve.bn_aggr(mv2[:, it, :], stats2[:, it, :])
                    last.then_inc(mv2_done, 1)

                def norm2(l, b):
                    n = l * B + b
                    dve.wait_ge(rstd2_done, n + 1)
                    for it in range(NT):
                        last = dve.tensor_scalar(r2[:, it, :], r2[:, it, :], mv2[:, it, 0:1], rstd2[:, it, :],
                                                 ALU.subtract, ALU.mult)
                    last.then_inc(norm2_done, 1)

                def pairs(b, weights, product, product_done, done, count):
                    for s in range(2):
                        if s == 1:
                            dve.wait_ge(product_done, count + 1)
                        for it in range(NT):
                            last = dve.scalar_tensor_tensor(out=product[:, it, :], in0=t.nodes[:, b, it, :], scalar=1.0,
                                                            in1=weights[:, s, :], op0=ALU.mult, op1=ALU.mult,
                                                            accum_out=t.pair[:, b, it, s:s + 1])
                        last.then_inc(product_done if s == 0 else done, 1)

                def next_pair(l, b):
                    n = l * B + b
                    dve.wait_ge(nodes_done, n + 1)
                    dve.wait_ge(aw_in, (l + 1) * 16)
                    dve.wait_ge(entered_pair, b + 1) if l == 0 else dve.wait_ge(pair_done, n - B + 1)
                    pairs(b, aw, product, product_done, pair_done, n)

                def moments_entered(e):
                    alone(dve, entered_x, e + 1, passed)
                    for it in range(NT):
                        last = dve.bn_stats(stats3[:, it, :], t.x[:, e, it, :])
                    last.then_inc(entered_stats, 1)
                    alone(dve, entered_stats, e + 1, passed)
                    for it in range(NT):
                        last = dve.bn_aggr(mv3[:, it, :], stats3[:, it, :])
                    last.then_inc(entered_mv, 1)

                def norm_entered(e):
                    dve.wait_ge(entered_rstd, e + 1)
                    for it in range(NT):
                        last = dve.tensor_scalar(t.nodes[:, e, it, :], t.x[:, e, it, :], mv3[:, it, 0:1], rstd3[:, it, :],
                                                 ALU.subtract, ALU.mult)
                    last.then_inc(entered_nodes, 1)

                def pair_entered(e):
                    dve.wait_ge(entered_nodes, e + 1)
                    after(dve, entered_pair, e)
                    pairs(e, aw_first, entered_junk, entered_product, entered_pair, e)

                def moments_left(b):
                    alone(dve, left_x, b + 1, passed)
                    for it in range(NT):
                        last = dve.bn_stats(stats3[:, it, :], t.x[:, b, it, :])
                    last.then_inc(left_stats, 1)
                    alone(dve, left_stats, b + 1, passed)
                    for it in range(NT):
                        last = dve.bn_aggr(mv3[:, it, :], stats3[:, it, :])
                    last.then_inc(left_mv, 1)

                def norm_left(b):
                    dve.wait_ge(left_rstd, b + 1)
                    for it in range(NT):
                        last = dve.tensor_scalar(t.nodes[:, b, it, :], t.x[:, b, it, :], mv3[:, it, 0:1], rstd3[:, it, :],
                                                 ALU.subtract, ALU.mult)
                    last.then_inc(left_nodes, 1)
                    dve.wait_ge(left_nodes, b + 1)
                    dve.tensor_reduce(t.mosts[:, bass.ds(b, 1)], t.nodes[:, b, :, :], AX.XY, ALU.max,
                                      apply_absolute_value=True).then_inc(left_most, 1)

                def start(at):
                    dve.wait_ge(aw_first_in, 2 * 16)
                    for e in range(2):
                        moments_entered(e)
                        norm_entered(e)
                        pair_entered(e)
                    as_neighbour(*at)
                    largest(*at)
                    larger(*at)
                    turned(*at)
                    norm1(*at, lambda: None)

                def body(ahead, now, behind, entering):
                    leaving = behind and behind[0] == L - 1
                    if ahead:
                        as_neighbour(*ahead)
                    if behind:
                        feed(*behind)
                    if ahead:
                        largest(*ahead)
                    if behind:
                        norm2(*behind)
                    if entering is not None:
                        moments_entered(entering)
                    if ahead:
                        larger(*ahead)
                        turned(*ahead)
                    if entering is not None:
                        norm_entered(entering)
                    if behind and not leaving:
                        next_pair(*behind)
                        dve.wait_ge(pair_done, behind[0] * B + behind[1] + 1)
                    if leaving:
                        moments_left(behind[1])

                    def meanwhile():
                        if entering is not None:
                            pair_entered(entering)
                        if leaving:
                            norm_left(behind[1])

                    if ahead:
                        norm1(*ahead, meanwhile)
                    else:
                        meanwhile()

                def end(at):
                    feed(*at)
                    norm2(*at)
                    moments_left(at[1])
                    norm_left(at[1])

                walk(dve, start, body, end)

            @block.tensor
            def _(pe):
                def scores(l, b):
                    n = l * B + b
                    pe.wait_ge(diag_done, n + 1)
                    after(pe, exp_done, n)
                    pe.matmul(score_bank[:, :], t.identb[:, :], t.gmask[:, b, :], start=True, stop=False,
                              skip_group_check=True)
                    for k in range(2):
                        for it in range(NT):
                            last = pe.matmul(score_bank[:, it * N:(it + 1) * N], t.ones_r[:, :].broadcast_to((P, P)),
                                             diag[:, k, :, :], start=False, stop=True, skip_group_check=True)
                    last.then_inc(scores_ps, 1)

                def turn_probs(l, b):
                    n = l * B + b
                    pe.wait_ge(probs_done, n + 1)
                    after(pe, hT_done, n)
                    for jt in range(NT):
                        for it in range(NT):
                            last = pe.transpose(turn_bank[:, jt * N + it * P:jt * N + (it + 1) * P],
                                                probs[:, it, jt * P:(jt + 1) * P], t.ident[:, :])
                    last.then_inc(turned_ps, 1)

                def aggregate(l, b):
                    n = l * B + b
                    pe.wait_ge(turned_done, n + 1)
                    after(pe, r1_done, n)
                    for it in range(NT):
                        for jt in range(NT):
                            last = pe.matmul(agg_bank[:, it * D:(it + 1) * D], probsT[:, jt, it * P:(it + 1) * P],
                                             t.nodes[:, b, jt, :], start=(jt == 0), stop=(jt == NT - 1))
                    last.then_inc(agg_ps, 1)

                def turn_h(l, b):
                    n = l * B + b
                    pe.wait_ge(norm1_done, n + 1)
                    pe.wait_ge(turned_done, n + 1)
                    for c in range(KC):
                        for it in range(NT):
                            last = pe.transpose(turn_bank[:, c * N + it * P:c * N + (it + 1) * P],
                                                r1[:, it, c * P:(c + 1) * P], t.ident[:, :])
                    last.then_inc(hT_ps, 1)

                def up(l, b, chunks):
                    n = l * B + b
                    if chunks[0] == 0:
                        pe.wait_ge(hT_done, n + 1)
                        pe.wait_ge(w1_in, (l + 1) * 16)
                        after(pe, gelu_done, n * NB)
                    for m in chunks:
                        for c in range(KC):
                            last = pe.matmul(hidden_bank[m // 2][:, m % 2 * N:(m % 2 + 1) * N],
                                             w1[:, c, m * P:(m + 1) * P], hT[:, c, :], start=(c == 0), stop=(c == KC - 1))
                        if m % 2 == 1:
                            last.then_inc(hidden_ps, 1)

                def down(l, b, chunks):
                    n = l * B + b
                    if chunks[0] == 0:
                        after(pe, r2_done, n)
                        pe.wait_ge(net_in, (l + 1) * NET_IN)
                    for m in chunks:
                        if m % 2 == 0:
                            pe.wait_ge(gelu_done, n * NB + m // 2 + 1)
                        for it in range(NT):
                            last = pe.matmul(ff_bank[:, it * D:(it + 1) * D], act1[:, m, it * P:(it + 1) * P],
                                             w2[:, m, :], start=(m == 0 and it == 0), stop=(m == MC - 1),
                                             skip_group_check=True)
                        if m == MC - 1:
                            last.then_inc(ff_ps, 1)

                def start(at):
                    scores(*at)
                    turn_probs(*at)
                    aggregate(*at)
                    turn_h(*at)

                def body(ahead, now, behind, entering):
                    up(*now, range(0, 2))
                    if ahead:
                        scores(*ahead)
                    up(*now, range(2, MC - 1))
                    if ahead:
                        turn_probs(*ahead)
                    up(*now, range(MC - 1, MC))
                    down(*now, range(0, 1))
                    if ahead:
                        aggregate(*ahead)
                    down(*now, range(1, 6))
                    if ahead:
                        turn_h(*ahead)
                    down(*now, range(6, MC))

                walk(pe, start, body, lambda at: None)


def last_phase(nc, t, a, out):
    STEP = float(2 ** 20)
    LEAST = 1.5 * 2 ** 14
    EXPONENT, HALF = 0x7F800000, 0x00400000
    U32 = mybir.dt.uint32
    with ExitStack() as ctx:
        def sb(name, shape, dt=F32):
            return ctx.enter_context(nc.sbuf_tensor("q_" + name, shape, dt))

        def sem(name):
            return ctx.enter_context(nc.semaphore("q_" + name))

        weight, wstep, wsum = (sb(n, [P, KC, D]) for n in ("weight", "wstep", "wsum"))
        wq = sb("wq", [P, KC, D], BF16)
        most, tops = sb("most", [P, 2]), sb("tops", [P, 2])
        floor, inv, scale, rscale, oscale = (sb(n, [P, 2]) for n in ("floor", "inv", "scale", "rscale", "oscale"))
        val, step_of, total = ([sb(f"{n}{i}", [P, NT, D]) for i in range(2)] for n in ("val", "step", "total"))
        xq = [sb(f"xq{i}", [P, NT, D], BF16) for i in range(2)]
        xqT = [sb(f"xqT{i}", [P, KC, N], BF16) for i in range(2)]
        res = [sb(f"res{i}", [P, NT, D]) for i in range(2)]
        turn_bank = [ctx.enter_context(nc.psum_tensor(f"q_T{i}", [P, 1024], BF16)) for i in range(2)]
        out_bank = [ctx.enter_context(nc.psum_tensor(f"q_O{i}", [P, 512], F32)) for i in range(2)]

        weight_in, most_done, tops_done, math_done, wq_done, wchain = (
            sem(n) for n in ("weight_in", "most_done", "tops_done", "math_done", "wq_done", "wchain"))
        (val_done, power_done, step_done,
         sum_done, xq_done, turned_ps, turned_done, out_ps, res_done, stored) = ([sem(f"{n}{i}") for i in range(2)] for n in (
            "val_done", "power_done", "step_done", "sum_done", "xq_done", "turned_ps", "turned_done", "out_ps", "res_done", "stored"))
        G = B // 2

        with nc.Block() as block:

            @block.sync
            def _(sp):
                sp.dma_start(weight[:, :, :], a["L1_ffn_weight"].rearrange("(c p) n -> p c n", p=P)).then_inc(weight_in, 16)
                with sp.Fori(0, G) as g:
                    for i in range(2):
                        sp.wait_ge(res_done[i], g + 1)
                        sp.dma_start(out[g * 2 + i].rearrange("(t p) d -> p t d", p=P), res[i][:, :, :]).then_inc(stored[i], 16)
                for i in range(2):
                    sp.wait_ge(stored[i], G * 16)

            @block.gpsimd
            def _(pool):
                pool.wait_ge(most_done, 2)
                pool.partition_all_reduce(tops[:, :], most[:, :], P, bass.bass_isa.ReduceOp.max).then_inc(tops_done, 1)
                with pool.Fori(0, G) as g:
                    for i in range(2):
                        pool.wait_ge(sum_done[i], g + 1)
                        pool.wait_ge(turned_ps[i], g)
                        pool.tensor_tensor(xq[i][:, :, :], total[i][:, :, :], step_of[i][:, :, :], ALU.subtract).then_inc(xq_done[i], 1)

            @block.scalar
            def _(act):
                with act.Fori(0, G) as g:
                    for i in range(2):
                        act.wait_ge(turned_ps[i], g + 1)
                        act.wait_ge(out_ps[i], g)
                        act.activation(xqT[i][:, :, :], turn_bank[i][:, 0:KC * N], ACT.Copy).then_inc(turned_done[i], 1)

            @block.tensor
            def _(pe):
                pe.wait_ge(wq_done, 1)
                with pe.Fori(0, G) as g:
                    for i in range(2):
                        pe.wait_ge(xq_done[i], g + 1)
                        pe.wait_ge(turned_done[i], g)
                        for c in range(KC):
                            for it in range(NT):
                                last = pe.transpose(turn_bank[i][:, c * N + it * P:c * N + (it + 1) * P],
                                                    xq[i][:, it, c * P:(c + 1) * P], t.identb[:, :])
                        last.then_inc(turned_ps[i], 1)
                        pe.wait_ge(turned_done[i], g + 1)
                        pe.wait_ge(res_done[i], g)
                        for it in range(NT):
                            for c in range(KC):
                                last = pe.matmul(out_bank[i][:, it * D:(it + 1) * D], xqT[i][:, c, it * P:(it + 1) * P],
                                                 wq[:, c, :], start=(c == 0), stop=(c == KC - 1))
                        last.then_inc(out_ps[i], 1)

            @block.vector
            def _(dve):
                dve.tensor_reduce(most[:, 0:1], t.mosts[:, :], AX.X, ALU.max).then_inc(most_done, 1)
                dve.wait_ge(weight_in, 16)
                dve.tensor_reduce(most[:, 1:2], weight[:, :, :], AX.XY, ALU.max, apply_absolute_value=True).then_inc(most_done, 1)
                dve.wait_ge(tops_done, 1)
                dve.tensor_scalar(floor[:, :], tops[:, :], 1e-12, None, ALU.max).then_inc(math_done, 1)
                dve.wait_ge(math_done, 1)
                dve.reciprocal(inv[:, :], floor[:, :]).then_inc(math_done, 1)
                dve.wait_ge(math_done, 2)
                dve.tensor_scalar(scale[:, :], inv[:, :], FP8_MAX, None, ALU.mult).then_inc(math_done, 1)
                dve.wait_ge(math_done, 3)
                dve.reciprocal(rscale[:, :], scale[:, :]).then_inc(math_done, 1)
                dve.wait_ge(math_done, 4)
                dve.tensor_tensor(oscale[:, 0:1], rscale[:, 0:1], rscale[:, 1:2], ALU.mult).then_inc(math_done, 1)
                dve.wait_ge(math_done, 5)

                dve.tensor_scalar(weight[:, :, :], weight[:, :, :], scale[:, 1:2], FP8_MAX, ALU.mult, ALU.min).then_inc(wchain, 1)
                dve.wait_ge(wchain, 1)
                dve.tensor_scalar(weight[:, :, :], weight[:, :, :], -FP8_MAX, None, ALU.max).then_inc(wchain, 1)
                dve.wait_ge(wchain, 2)
                dve.tensor_scalar(wstep[:, :, :].bitcast(U32), weight[:, :, :].bitcast(U32), EXPONENT, HALF,
                                  ALU.bitwise_and, ALU.bitwise_or).then_inc(wchain, 1)
                dve.wait_ge(wchain, 3)
                dve.tensor_scalar(wstep[:, :, :], wstep[:, :, :], STEP, LEAST, ALU.mult, ALU.max).then_inc(wchain, 1)
                dve.wait_ge(wchain, 4)
                dve.tensor_tensor(wsum[:, :, :], weight[:, :, :], wstep[:, :, :], ALU.add).then_inc(wchain, 1)
                dve.wait_ge(wchain, 5)
                dve.tensor_tensor(wq[:, :, :], wsum[:, :, :], wstep[:, :, :], ALU.subtract).then_inc(wq_done, 1)

                def quantise(g, i):
                    b = g * 2 + i
                    dve.wait_ge(xq_done[i], g)
                    dve.tensor_scalar(val[i][:, :, :], t.nodes[:, b, :, :], scale[:, 0:1], FP8_MAX, ALU.mult,
                                      ALU.min).then_inc(val_done[i], 1)
                    dve.wait_ge(val_done[i], g + 1)
                    dve.tensor_scalar(step_of[i][:, :, :].bitcast(U32), val[i][:, :, :].bitcast(U32), EXPONENT, HALF,
                                      ALU.bitwise_and, ALU.bitwise_or).then_inc(power_done[i], 1)
                    dve.wait_ge(power_done[i], g + 1)
                    dve.tensor_scalar(step_of[i][:, :, :], step_of[i][:, :, :], STEP, LEAST, ALU.mult,
                                      ALU.max).then_inc(step_done[i], 1)
                    dve.wait_ge(step_done[i], g + 1)
                    dve.scalar_tensor_tensor(out=total[i][:, :, :], in0=val[i][:, :, :], scalar=-FP8_MAX,
                                             in1=step_of[i][:, :, :], op0=ALU.max, op1=ALU.add).then_inc(sum_done[i], 1)

                def result(g, i):
                    dve.wait_ge(out_ps[i], g + 1)
                    dve.wait_ge(stored[i], g * 16)
                    dve.scalar_tensor_tensor(out=res[i][:, :, :], in0=out_bank[i][:, :].rearrange("p (t d) -> p t d", t=NT),
                                             scalar=oscale[:, 0:1], in1=t.x[:, g * 2 + i, :, :], op0=ALU.mult,
                                             op1=ALU.add).then_inc(res_done[i], 1)

                for i in range(2):
                    quantise(0, i)
                with dve.Fori(1, G) as g:
                    for i in range(2):
                        quantise(g, i)
                        result(g - 1, i)
                for i in range(2):
                    result(G - 1, i)


class Shared:
    pass


def build_program(nc, a, out):
    hidden = nc.dram_tensor("hidden", (B, N, D), F32, kind="Internal").ap()
    t = Shared()
    with ExitStack() as ctx:
        def sb(name, shape, dt=F32):
            return ctx.enter_context(nc.sbuf_tensor(name, shape, dt))

        t.x = sb("x", [P, B, NT, D])
        t.seq = sb("seq", [P, KC, N, B])
        t.nodes = t.seq[:, :, :, :].rearrange("p c n b -> p (c n b)").rearrange("p (g t d) -> p g t d", g=B, t=NT)
        t.pair = sb("pair", [P, B, NT, 2])
        t.mosts = sb("mosts", [P, B])
        t.gmask = sb("gmask", [P, B, NT * N], BF16)
        t.ident, t.identb, t.ones_r = sb("ident", [P, P]), sb("identb", [P, P], BF16), sb("ones_r", [P, 1], F32R)
        t.ones = t.ones_r[:, :].bitcast(F32)
        small = sb("eps_power", [P, 2, NT])
        t.eps, t.power = small[:, 0, :], small[:, 1, :]
        constants(nc, t)
        attention_phase(nc, t, a)
        lstm_phase(nc, t, a, hidden)
        gnn_phase(nc, t, a, hidden)
        last_phase(nc, t, a, out)


_INS = ['x', 'adj', 'L0_gnn_Wq', 'L0_gnn_bq', 'L0_gnn_Wk', 'L0_gnn_bk', 'L0_gnn_Wv', 'L0_gnn_bv', 'L0_gnn_Wo',
        'L0_gnn_bo', 'L0_ffn_W_f', 'L0_ffn_b_f', 'L0_ffn_W_i', 'L0_ffn_b_i', 'L0_ffn_W_c', 'L0_ffn_b_c',
        'L0_ffn_W_o', 'L0_ffn_b_o', 'L1_gnn_attn_w', 'L1_gnn_attn_b', 'L1_gnn_W1', 'L1_gnn_b1', 'L1_gnn_W2',
        'L1_gnn_b2', 'L1_gnn_g1', 'L1_gnn_beta1', 'L1_gnn_g2', 'L1_gnn_beta2', 'L1_ffn_weight']


def kernel(**inputs):
    import numpy as _np
    import concourse.bacc as _bacc
    from concourse import mybir as _mybir
    from concourse.bass_utils import run_bass_kernel_spmd as _run

    nc = _bacc.Bacc("TRN2", target_bir_lowering=False, num_devices=1)
    arrays, args = {}, {}
    for name in _INS:
        x = _np.ascontiguousarray(inputs[name])
        arrays[f"in_{name}_dram"] = x
        args[name] = nc.dram_tensor(f"in_{name}_dram", x.shape, _mybir.dt.from_np(x.dtype), kind="ExternalInput").ap()
    out = nc.dram_tensor("out_0_dram", (B, N, D), F32, kind="ExternalOutput").ap()
    build_program(nc, args, out)
    r = _run(nc, [arrays], core_ids=[0])
    return r.results[0]["out_0_dram"]
```

```python
from contextlib import ExitStack

import numpy as np

import concourse.bass as bass
from concourse import mybir

F32 = mybir.dt.float32
F32R = mybir.dt.float32r
BF16 = mybir.dt.bfloat16
I32 = mybir.dt.int32
ALU = mybir.AluOpType
ACT = mybir.ActivationFunctionType
AX = mybir.AxisListType

P = 128
B, N, D = 32, 256, 256
NT = N // P
KC = D // P
H, HD = 8, 32
HG = P // HD
L = 3
FF = 4 * D
MC = FF // P
EPS = 1e-5
MASKED = -1e30
GATES = 4
Q = 4
HQ = D // Q
SEG = 8
FP8_MAX = 448.0


def after(eng, sem, value):
    if isinstance(value, int) and value <= 0:
        return
    eng.wait_ge(sem, value)


def alone(eng, sem, value, passed):
    eng.wait_ge(sem, value)
    eng.sem_inc(passed, 1)


def constants(nc, t):
    with ExitStack() as ctx:
        cleared = ctx.enter_context(nc.semaphore("cleared"))
        made = ctx.enter_context(nc.semaphore("made"))
        with nc.Block() as block:

            @block.gpsimd
            def _(pool):
                pool.memset(t.ident[:, :], 0.0).then_inc(cleared, 1)
                pool.memset(t.ones[:, :], 1.0)
                pool.memset(t.power[:, :], -0.5)
                pool.memset(t.eps[:, :], EPS)
                pool.wait_ge(cleared, 1)
                pool.affine_select(out=t.ident[:, :], in_=t.ident[:, :], compare_op=ALU.not_equal, fill=1.0,
                                   base=0, pattern=[[-1, P]], channel_multiplier=1).then_inc(made, 1)

            @block.vector
            def _(dve):
                dve.wait_ge(made, 1)
                dve.tensor_copy(t.identb[:, :], t.ident[:, :])


def attention_phase(nc, t, a, masks_out):
    with ExitStack() as ctx:
        def sb(name, shape, dt=F32):
            return ctx.enter_context(nc.sbuf_tensor("a_" + name, shape, dt))

        def ps(name):
            return ctx.enter_context(nc.psum_tensor("a_" + name, [P, 512], F32))

        def sem(name):
            return ctx.enter_context(nc.semaphore("a_" + name))

        wq, wk, wv, wo = (sb(f"w{n}", [P, KC, D]) for n in "qkvo")
        w_upper, w_rest = ([sb(f"w{n}_{part}", [P, KC, D], F32R) for n in "qkv"] for part in ("upper", "rest"))
        bq_col, bk_col, bqs_col = (sb(n, [P, KC]) for n in ("bq", "bk", "bqs"))
        bv_row, bo_row = sb("bv_row", [P, D]), sb("bo_row", [P, D])
        adj = sb("adj", [P, NT, N], I32)
        mask = sb("mask", [P, NT * N], BF16)
        selfadj = sb("selfadj", [P, NT, P], BF16)
        xn, xn2 = sb("xn", [P, NT, D]), sb("xn2", [P, NT, D])
        xnT_upper, xnT_rest = (sb(n, [P, KC, N], F32R) for n in ("xnT_upper", "xnT_rest"))
        qT, kT = (sb(n, [P, KC, N]) for n in ("qT", "kT"))
        v = sb("v", [P, NT, D])
        probs = [sb(f"probs{i}", [P, NT, N]) for i in range(2)]
        probsT = [sb(f"probsT{i}", [P, NT, N]) for i in range(HG)]
        den, tiny_rden = sb("den", [P, H, NT]), sb("tiny_rden", [P, H, NT])
        spread, rden = xn[:, 0, :].rearrange("p (t j r) -> p t j r", t=NT, j=HG), xn[:, 1, :]
        outT = sb("outT", [P, KC, N])
        gated = xn2
        nmax = sb("nmax", [P, H, NT])
        stats1, mv1, veps1, rstd1 = (sb(n, [P, NT, w]) for n, w in (("stats1", 6), ("mv1", 2), ("veps1", 1), ("rstd1", 1)))
        stats2, mv2, veps2, rstd2 = (sb(n, [P, NT, w]) for n, w in (("stats2", 6), ("mv2", 2), ("veps2", 1), ("rstd2", 1)))

        score_bank = [ps("S0"), ps("S1")]
        turn_bank = [ps("T0"), ps("T1")]
        q_bank, k_bank, v_bank, head_bank = ps("Q"), ps("K"), ps("V"), ps("O")

        weights_in, rows_in, bqs_done = sem("weights_in"), sem("rows_in"), sem("bqs_done")
        x_in, adj_in = sem("x_in"), sem("adj_in")
        gmask_stored = sem("gmask_stored")
        selfadj_done, mask_done = sem("selfadj_done"), sem("mask_done")
        stats1_done, mv1_done, veps1_done, rstd1_done, xn_done = (
            sem(n) for n in ("stats1_done", "mv1_done", "veps1_done", "rstd1_done", "xn_done"))
        stats2_done, mv2_done, veps2_done, rstd2_done, xn2_done = (
            sem(n) for n in ("stats2_done", "mv2_done", "veps2_done", "rstd2_done", "xn2_done"))
        xnT_ps, xnT_done, xn2T_ps, xn2T_done = sem("xnT_ps"), sem("xnT_done"), sem("xn2T_ps"), sem("xn2T_done")
        xnT_rest_done, upper_done, split_done = sem("xnT_rest_done"), sem("upper_done"), sem("split_done")
        q_ps, k_ps, v_ps = sem("q_ps"), sem("k_ps"), sem("v_ps")
        q_done, k_done, v_done = sem("q_done"), sem("k_done"), sem("v_done")
        scores_ps, max_done, probs_done = sem("scores_ps"), sem("max_done"), sem("probs_done")
        turned_ps, even_done, odd_done = sem("turned_ps"), sem("even_done"), sem("odd_done")
        heads_ps, rden_done, heads_done = sem("heads_ps"), sem("rden_done"), sem("heads_done")
        tiny_done, spread_done = sem("tiny_done"), sem("spread_done")
        proj_ps, gated_done, x_done = sem("proj_ps"), sem("gated_done"), sem("x_done")

        passed = sem("passed")
        with nc.Block() as block:

            @block.sync
            def _(sp):
                def store(b):
                    sp.dma_start(masks_out[b], t.gmask[:, :]).then_inc(gmask_stored, 16)

                def load(b):
                    sp.wait_ge(x_in, b * 16)
                    sp.dma_start(t.x[:, b, :, :], a["x"][b].rearrange("(t p) d -> p t d", p=P)).then_inc(x_in, 16)
                    after(sp, mask_done, b)
                    if not (isinstance(b, int) and b == 0):
                        store(b - 1)
                    sp.dma_start(adj[:, :, :], a["adj"][b].rearrange("(t p) d -> p t d", p=P)).then_inc(adj_in, 16)

                load(0)
                for w, src in ((wq, a["L0_gnn_Wq"]), (wk, a["L0_gnn_Wk"]), (wv, a["L0_gnn_Wv"]), (wo, a["L0_gnn_Wo"])):
                    sp.dma_start(w[:, :, :], src.rearrange("(c p) n -> p c n", p=P)).then_inc(weights_in, 16)
                with nc.allow_non_contiguous_dma(reason="bias columns"):
                    sp.dma_start(bq_col[:, :], a["L0_gnn_bq"].rearrange("(c p) -> p c", p=P)).then_inc(rows_in, 16)
                    sp.dma_start(bk_col[:, :], a["L0_gnn_bk"].rearrange("(c p) -> p c", p=P)).then_inc(rows_in, 16)
                sp.dma_start(bv_row[:, :], a["L0_gnn_bv"].partition_broadcast(P)).then_inc(rows_in, 16)
                sp.dma_start(bo_row[:, :], a["L0_gnn_bo"].partition_broadcast(P)).then_inc(rows_in, 16)
                load(1)
                load_lstm_weights(sp, t, a)
                with sp.Fori(2, B) as b:
                    load(b)
                sp.wait_ge(mask_done, B)
                store(B - 1)
                sp.wait_ge(gmask_stored, B * 16)

            @block.gpsimd
            def _(pool):
                def rsqrt1(b):
                    pool.wait_ge(mv1_done, b + 1)
                    pool.tensor_tensor(veps1[:, :, 0], mv1[:, :, 1], t.eps[:, :], ALU.add).then_inc(veps1_done, 1)
                    pool.wait_ge(veps1_done, b + 1)
                    pool.tensor_tensor(rstd1[:, :, 0], veps1[:, :, 0], t.power[:, :], ALU.pow).then_inc(rstd1_done, 1)

                def rsqrt2(b):
                    pool.wait_ge(mv2_done, b + 1)
                    pool.tensor_tensor(veps2[:, :, 0], mv2[:, :, 1], t.eps[:, :], ALU.add).then_inc(veps2_done, 1)
                    pool.wait_ge(veps2_done, b + 1)
                    pool.tensor_tensor(rstd2[:, :, 0], veps2[:, :, 0], t.power[:, :], ALU.pow).then_inc(rstd2_done, 1)

                def spread_out(b, g):
                    pool.wait_ge(tiny_done, b * 2 + g + 1)
                    after(pool, heads_ps, b * 2 + g)
                    if g == 0 and not isinstance(b, int):
                        pool.wait_ge(xnT_ps, b + 2)
                    part = tiny_rden[:, g * HG:(g + 1) * HG, :].rearrange("p j t -> p t j").unsqueeze(3)
                    pool.tensor_tensor(spread, part.broadcast_to((P, NT, HG, HD)),
                                       t.ones.unsqueeze(2).unsqueeze(3).broadcast_to((P, NT, HG, HD)),
                                       ALU.mult).then_inc(spread_done, 1)

                def graph(b, has_prev, has_next):
                    if has_next:
                        rsqrt1(b + 1)
                    spread_out(b, 0)
                    if has_prev:
                        rsqrt2(b - 1)
                    spread_out(b, 1)

                rsqrt1(0)
                graph(0, False, True)
                with pool.Fori(1, B - 1) as b:
                    graph(b, True, True)
                graph(B - 1, True, False)
                rsqrt2(B - 1)

            @block.scalar
            def _(act):
                def xnT_out(b):
                    act.wait_ge(xnT_ps, b + 1)
                    act.activation(xnT_upper[:, :, :], q_bank[:, :], ACT.Copy).then_inc(xnT_done, 1)

                def q_out(b):
                    act.wait_ge(q_ps, b + 1)
                    for c in range(KC):
                        last = act.activation(qT[:, c, :], q_bank[:, c * N:(c + 1) * N], ACT.Identity,
                                              bias=bqs_col[:, c:c + 1], scale=HD ** -0.5)
                    last.then_inc(q_done, 1)

                def k_out(b):
                    act.wait_ge(k_ps, b + 1)
                    for c in range(KC):
                        last = act.activation(kT[:, c, :], k_bank[:, c * N:(c + 1) * N], ACT.Identity,
                                              bias=bk_col[:, c:c + 1])
                    last.then_inc(k_done, 1)

                def exponent(b, h):
                    act.wait_ge(max_done, b * H + h + 1)
                    after(act, turned_ps, b * H + h - 1)
                    for it in range(NT):
                        last = act.activation(probs[h % 2][:, it, :], score_bank[h % 2][:, it * N:(it + 1) * N],
                                              ACT.Exp, bias=nmax[:, h, it:it + 1], accum_out=den[:, h, it:it + 1])
                    last.then_inc(probs_done, 1)

                def even_out(b, h):
                    act.wait_ge(turned_ps, b * H + h + 1)
                    after(act, heads_ps, b * 2 + h // HG)
                    act.activation(probsT[h % HG][:, :, :], turn_bank[0][:, :], ACT.Copy).then_inc(even_done, 1)

                def rden_out(b, g):
                    act.wait_ge(heads_ps, b * 2 + g + 1)
                    after(act, heads_done, b * 2 + g)
                    act.activation(rden, head_bank[:, N:2 * N], ACT.Copy).then_inc(rden_done, 1)

                def graph(b, has_next):
                    for h in range(H):
                        exponent(b, h)
                        if h == 5:
                            rden_out(b, 0)
                        if h == 3 and has_next:
                            xnT_out(b + 1)
                        if h == H - 1 and has_next:
                            q_out(b + 1)
                        if h % 2 == 1:
                            even_out(b, h - 1)
                    if has_next:
                        k_out(b + 1)
                    rden_out(b, 1)

                xnT_out(0)
                act.wait_ge(bqs_done, 1)
                q_out(0)
                k_out(0)
                graph(0, True)
                with act.Fori(1, B - 1) as b:
                    graph(b, True)
                graph(B - 1, False)

            @block.vector
            def _(dve):
                def gmasks(b):
                    dve.wait_ge(adj_in, b * 16 + 16)
                    for it in range(NT):
                        last = dve.tensor_tensor(selfadj[:, it, :], adj[:, it, it * P:(it + 1) * P], t.ident[:, :], ALU.add)
                    last.then_inc(selfadj_done, 1)
                    after(dve, gmask_stored, b * 16)
                    for it in range(NT):
                        dve.tensor_scalar(t.gmask[:, (it + 1) * P:(it + 2) * P],
                                          adj[:, it, (1 - it) * P:(2 - it) * P], 0.0, MASKED, ALU.is_le, ALU.mult)
                    dve.wait_ge(selfadj_done, b + 1)
                    for it in range(NT):
                        dve.tensor_scalar(t.gmask[:, 3 * it * P:(3 * it + 1) * P], selfadj[:, it, :], 0.0, MASKED,
                                          ALU.is_le, ALU.mult)

                def masks(b):
                    after(dve, scores_ps, b * H)
                    dve.tensor_scalar(mask[:, :], adj[:, :, :].rearrange("p t n -> p (t n)"), 0.0, MASKED,
                                      ALU.is_le, ALU.mult).then_inc(mask_done, 1)

                def moments1(b):
                    alone(dve, x_in, b * 16 + 16, passed)
                    for it in range(NT):
                        last = dve.bn_stats(stats1[:, it, :], t.x[:, b, it, :])
                    last.then_inc(stats1_done, 1)
                    alone(dve, stats1_done, b + 1, passed)
                    for it in range(NT):
                        last = dve.bn_aggr(mv1[:, it, :], stats1[:, it, :])
                    last.then_inc(mv1_done, 1)

                def norm1(b):
                    dve.wait_ge(rstd1_done, b + 1)
                    after(dve, xnT_ps, b)
                    after(dve, heads_ps, (b - 1) * 2)
                    after(dve, heads_done, (b - 1) * 2)
                    for it in range(NT):
                        last = dve.tensor_scalar(xn[:, it, :], t.x[:, b, it, :], mv1[:, it, 0:1], rstd1[:, it, :],
                                                 ALU.subtract, ALU.mult)
                    last.then_inc(xn_done, 1)

                def xnT_rest_out(b):
                    dve.wait_ge(xnT_done, b + 1)
                    dve.tensor_tensor(xnT_rest[:, :, :], q_bank[:, :].rearrange("p (c n) -> p c n", c=KC),
                                      xnT_upper[:, :, :].bitcast(F32), ALU.subtract).then_inc(xnT_rest_done, 1)

                def v_out(b):
                    dve.wait_ge(v_ps, b + 1)
                    for it in range(NT):
                        last = dve.tensor_tensor(v[:, it, :], v_bank[:, it * D:(it + 1) * D], bv_row[:, :], ALU.add)
                    last.then_inc(v_done, 1)

                def largest(b, h):
                    dve.wait_ge(scores_ps, b * H + h + 1)
                    dve.tensor_reduce(nmax[:, h, :], score_bank[h % 2][:, :].rearrange("p (t k) -> p t k", t=NT), AX.X,
                                      ALU.max, negate=True).then_inc(max_done, 1)

                def odd_out(b, h):
                    dve.wait_ge(turned_ps, b * H + h + 1)
                    after(dve, heads_ps, b * 2 + h // HG)
                    dve.tensor_copy(probsT[h % HG][:, :, :], turn_bank[1][:, :]).then_inc(odd_done, 1)

                def reciprocals(b, g):
                    dve.wait_ge(probs_done, b * H + (g + 1) * HG)
                    after(dve, spread_done, b * 2 + g)
                    part = slice(g * HG, (g + 1) * HG)
                    dve.reciprocal(tiny_rden[:, part, :], den[:, part, :]).then_inc(tiny_done, 1)

                def heads_out(b, g):
                    dve.wait_ge(rden_done, b * 2 + g + 1)
                    after(dve, proj_ps, b)
                    dve.tensor_tensor(outT[:, g, :], head_bank[:, 0:N], rden, ALU.mult).then_inc(heads_done, 1)

                def residual(b):
                    dve.wait_ge(proj_ps, b + 1)
                    after(dve, xn2T_ps, b)
                    for it in range(NT):
                        last = dve.tensor_tensor(gated[:, it, :], head_bank[:, it * D:(it + 1) * D], bo_row[:, :], ALU.add)
                    last.then_inc(gated_done, 1)
                    dve.wait_ge(gated_done, b + 1)
                    dve.scalar_tensor_tensor(out=t.x[:, b, :, :], in0=gated[:, :, :], scalar=0.0, in1=t.x[:, b, :, :],
                                             op0=ALU.max, op1=ALU.add).then_inc(x_done, 1)

                def moments2(b):
                    alone(dve, x_done, b + 1, passed)
                    for it in range(NT):
                        last = dve.bn_stats(stats2[:, it, :], t.x[:, b, it, :])
                    last.then_inc(stats2_done, 1)
                    alone(dve, stats2_done, b + 1, passed)
                    for it in range(NT):
                        last = dve.bn_aggr(mv2[:, it, :], stats2[:, it, :])
                    last.then_inc(mv2_done, 1)

                def norm2(b):
                    dve.wait_ge(rstd2_done, b + 1)
                    for it in range(NT):
                        last = dve.tensor_scalar(xn2[:, it, :], t.x[:, b, it, :], mv2[:, it, 0:1], rstd2[:, it, :],
                                                 ALU.subtract, ALU.mult)
                    last.then_inc(xn2_done, 1)

                def xn2T_out(b):
                    dve.wait_ge(xn2T_ps, b + 1)
                    dve.tensor_copy(t.seq[:, :, :, b], turn_bank[0][:, :].rearrange("p (c n) -> p c n", c=KC)).then_inc(xn2T_done, 1)

                def graph(b, has_prev, has_next):
                    largest(b, 0)
                    largest(b, 1)
                    if has_next:
                        moments1(b + 1)
                    v_out(b)
                    largest(b, 2)
                    if has_next:
                        norm1(b + 1)
                    odd_out(b, 1)
                    largest(b, 3)
                    if has_prev:
                        residual(b - 1)
                    if has_next:
                        xnT_rest_out(b + 1)
                    largest(b, 4)
                    reciprocals(b, 0)
                    odd_out(b, 3)
                    if has_prev:
                        moments2(b - 1)
                    largest(b, 5)
                    heads_out(b, 0)
                    largest(b, 6)
                    odd_out(b, 5)
                    if has_prev:
                        norm2(b - 1)
                    largest(b, 7)
                    if has_next:
                        gmasks(b + 1)
                        masks(b + 1)
                    reciprocals(b, 1)
                    odd_out(b, 7)
                    if has_prev:
                        xn2T_out(b - 1)
                    heads_out(b, 1)

                moments1(0)
                norm1(0)
                gmasks(0)
                masks(0)
                dve.wait_ge(rows_in, 4 * 16)
                dve.tensor_scalar(bqs_col[:, :], bq_col[:, :], HD ** -0.5, None, ALU.mult).then_inc(bqs_done, 1)
                xnT_rest_out(0)
                dve.wait_ge(weights_in, 4 * 16)
                for upper, w in zip(w_upper, (wq, wk, wv)):
                    last = dve.tensor_copy(upper[:, :, :], w[:, :, :])
                last.then_inc(upper_done, 1)
                dve.wait_ge(upper_done, 1)
                for rest, upper, w in zip(w_rest, w_upper, (wq, wk, wv)):
                    last = dve.tensor_tensor(rest[:, :, :], w[:, :, :], upper[:, :, :].bitcast(F32), ALU.subtract)
                last.then_inc(split_done, 1)
                graph(0, False, True)
                with dve.Fori(1, B - 1) as b:
                    graph(b, True, True)
                graph(B - 1, True, False)
                residual(B - 1)
                moments2(B - 1)
                norm2(B - 1)
                xn2T_out(B - 1)

            @block.tensor
            def _(pe):
                def turn(bank, x):
                    for c in range(KC):
                        for it in range(NT):
                            last = pe.transpose(bank[:, c * N + it * P:c * N + (it + 1) * P], x[:, it, c * P:(c + 1) * P],
                                                t.ident[:, :])
                    return last

                def turn_xn(b):
                    pe.wait_ge(xn_done, b + 1)
                    after(pe, q_done, b)
                    turn(q_bank, xn).then_inc(xnT_ps, 1)

                def turn_xn2(b):
                    pe.wait_ge(xn2_done, b + 1)
                    pe.wait_ge(even_done, (H // 2) * (min(b + 2, B) if isinstance(b, int) else b + 2))
                    turn(turn_bank[0], xn2).then_inc(xn2T_ps, 1)

                def multiply(out, w, x, first, last):
                    (w_up, w_low), (x_up, x_low) = w, x
                    pe.matmul(out, w_up, x_up, start=first, stop=False)
                    pe.matmul(out, w_up, x_low, start=False, stop=False)
                    return pe.matmul(out, w_low, x_up, start=False, stop=last)

                def project_in(bank, which, m):
                    for c in range(KC):
                        last = multiply(bank[:, m * N:(m + 1) * N],
                                        [w[which][:, c, m * P:(m + 1) * P] for w in (w_upper, w_rest)],
                                        [xnT_upper[:, c, :], xnT_rest[:, c, :]], c == 0, c == KC - 1)
                    return last

                def queries(b, m):
                    if m == 0:
                        pe.wait_ge(xnT_rest_done, b + 1)
                    last = project_in(q_bank, 0, m)
                    if m == KC - 1:
                        last.then_inc(q_ps, 1)

                def keys(b, m):
                    if m == 0:
                        after(pe, k_done, b)
                    last = project_in(k_bank, 1, m)
                    if m == KC - 1:
                        last.then_inc(k_ps, 1)

                def values(b):
                    after(pe, v_done, b)
                    for it in range(NT):
                        for c in range(KC):
                            last = multiply(v_bank[:, it * D:(it + 1) * D],
                                            [x[:, c, it * P:(it + 1) * P] for x in (xnT_upper, xnT_rest)],
                                            [w[2][:, c, :] for w in (w_upper, w_rest)], c == 0, c == KC - 1)
                    last.then_inc(v_ps, 1)

                def scores(b, h):
                    if h == 0:
                        pe.wait_ge(q_done, b + 1)
                        pe.wait_ge(k_done, b + 1)
                        pe.wait_ge(mask_done, b + 1)
                    after(pe, probs_done, b * H + h - 1)
                    o, c, bank = HD * (h % HG), h // HG, score_bank[h % 2]
                    pe.matmul(bank[:, :], t.identb[:, :], mask[:, :], start=True, stop=False, skip_group_check=True)
                    for it in range(NT):
                        last = pe.matmul(bank[:, it * N:(it + 1) * N], qT[o:o + HD, c, it * P:(it + 1) * P],
                                         kT[o:o + HD, c, :], start=False, stop=True, skip_group_check=True)
                    last.then_inc(scores_ps, 1)

                def turn_probs(b, h):
                    pe.wait_ge(probs_done, b * H + h + 1)
                    after(pe, odd_done if h % 2 else even_done, b * (H // 2) + h // 2)
                    if h == 0:
                        after(pe, xn2T_done, b - 1)
                    for kt in range(NT):
                        for it in range(NT):
                            last = pe.transpose(turn_bank[h % 2][:, kt * N + it * P:kt * N + (it + 1) * P],
                                                probs[h % 2][:, it, kt * P:(kt + 1) * P], t.ident[:, :])
                    last.then_inc(turned_ps, 1)

                def weigh(b, g):
                    pe.wait_ge(even_done, b * (H // 2) + 2 * g + 2)
                    pe.wait_ge(odd_done, b * (H // 2) + 2 * g + 2)
                    pe.wait_ge(v_done, b + 1)
                    if g == 0:
                        after(pe, gated_done, b)
                    else:
                        pe.wait_ge(heads_done, b * 2 + 1)
                    for kt in range(NT):
                        for j in range(HG):
                            h = g * HG + j
                            pe.matmul(head_bank[j * HD:(j + 1) * HD, 0:N], v[:, kt, h * HD:(h + 1) * HD],
                                      probsT[j][:, kt, :], start=(kt == 0), stop=(kt == NT - 1), tile_position=(0, j * HD))
                    pe.wait_ge(spread_done, b * 2 + g + 1)
                    for it in range(NT):
                        last = pe.transpose(head_bank[:, N + it * P:N + (it + 1) * P],
                                            spread[:, it, :, :].rearrange("p j r -> p (j r)"), t.ident[:, :])
                    last.then_inc(heads_ps, 1)

                def project(b):
                    pe.wait_ge(heads_done, b * 2 + 2)
                    for it in range(NT):
                        for c in range(KC):
                            last = pe.matmul(head_bank[:, it * D:(it + 1) * D], outT[:, c, it * P:(it + 1) * P],
                                             wo[:, c, :], start=(c == 0), stop=(c == KC - 1))
                    last.then_inc(proj_ps, 1)

                def graph(b, has_prev, has_next):
                    scores(b, 0)
                    scores(b, 1)
                    if has_prev:
                        project(b - 1)
                    turn_probs(b, 0)
                    scores(b, 2)
                    turn_probs(b, 1)
                    scores(b, 3)
                    if has_next:
                        turn_xn(b + 1)
                    turn_probs(b, 2)
                    scores(b, 4)
                    turn_probs(b, 3)
                    scores(b, 5)
                    if has_next:
                        queries(b + 1, 0)
                        queries(b + 1, 1)
                    weigh(b, 0)
                    turn_probs(b, 4)
                    scores(b, 6)
                    if has_next:
                        keys(b + 1, 0)
                    turn_probs(b, 5)
                    scores(b, 7)
                    if has_next:
                        values(b + 1)
                    turn_probs(b, 6)
                    turn_probs(b, 7)
                    if has_next:
                        keys(b + 1, 1)
                    if has_prev:
                        turn_xn2(b - 1)
                    weigh(b, 1)

                turn_xn(0)
                pe.wait_ge(split_done, 1)
                for m in range(KC):
                    queries(0, m)
                for m in range(KC):
                    keys(0, m)
                values(0)
                graph(0, False, True)
                with pe.Fori(1, B - 1) as b:
                    graph(b, True, True)
                graph(B - 1, True, False)
                project(B - 1)
                turn_xn2(B - 1)


def load_lstm_weights(eng, t, a):
    for g, name in enumerate(("f", "i", "c", "o")):
        w, b = a[f"L0_ffn_W_{name}"], a[f"L0_ffn_b_{name}"]
        eng.dma_start(t.wx[:, :, g, :], w[0:D, :].rearrange("(c p) n -> p c n", p=P)).then_inc(t.lstm_weights_in, 16)
        rows = w[D:2 * D, :].rearrange("(j c d) n -> j d c n", j=Q, c=KC)
        for j in range(Q):
            part = slice(j * B, (j + 1) * B)
            eng.dma_start(t.wh[part, :, g, :], rows[j]).then_inc(t.lstm_weights_in, 16)
            eng.dma_start(t.bias[part, g, :], b[j * HQ:(j + 1) * HQ].partition_broadcast(B)).then_inc(t.lstm_weights_in, 16)


def lstm_phase(nc, t, a, hidden):
    with ExitStack() as ctx:
        def sb(name, shape, dt=F32):
            return ctx.enter_context(nc.sbuf_tensor("l_" + name, shape, dt))

        def sem(name):
            return ctx.enter_context(nc.semaphore("l_" + name))

        wx, wh, bias = t.wx, t.wh, t.bias
        xt = [sb(f"xt{i}", [P, KC, B]) for i in range(2)]
        hT = sb("hT", [P, KC, B])
        cell = sb("cell", [P, HQ])
        fi, og, cand = sb("fi", [P, 2, HQ]), sb("og", [P, HQ]), sb("cand", [P, HQ])
        kept, fresh, tanh_c = sb("kept", [P, HQ]), sb("fresh", [P, HQ]), sb("tanh_c", [P, HQ])
        hs = [sb(f"hs{i}", [P, SEG, HQ]) for i in range(2)]
        gate_bank, o_bank = ([ctx.enter_context(nc.psum_tensor(f"l_{n}{i}", [P, 512], F32)) for i in range(2)] for n in "GO")
        CELL = 3

        xt_done, xt_free, hT_done = sem("xt_done"), sem("xt_free"), sem("hT_done")
        o_ps = sem("o_ps")
        gates_ps, fi_done, cand_done, og_done, tanh_done = (
            sem(n) for n in ("gates_ps", "fi_done", "cand_done", "og_done", "tanh_done"))
        fresh_done, cell_done, h_done = sem("fresh_done"), sem("cell_done"), sem("h_done")
        stored = [sem("stored0"), sem("stored1")]
        STEPS = 2 * SEG

        with nc.Block() as block:

            @block.sync
            def _(sp):
                with sp.Fori(0, N // STEPS) as s:
                    for half in range(2):
                        sp.wait_ge(h_done, s * STEPS + (half + 1) * SEG)
                        for j in range(Q):
                            sp.dma_start(hidden[:, bass.ds(s * STEPS + half * SEG, SEG), j * HQ:(j + 1) * HQ],
                                         hs[half][j * B:(j + 1) * B, :, :]).then_inc(stored[half], 16)
                for half in range(2):
                    sp.wait_ge(stored[half], N // STEPS * Q * 16)

            @block.gpsimd
            def _(pool):
                with pool.Fori(0, N // 2) as s:
                    for i in range(2):
                        pool.wait_ge(xt_free, s * 2 + i + 1)
                        pool.tensor_copy(xt[i][:, :, :], t.seq[:, :, s * 2 + i, :]).then_inc(xt_done, 1)

            @block.tensor
            def _(pe):
                def step(n, u):
                    parts = ((gate_bank[u % 2], slice(0, CELL), gates_ps), (o_bank[u % 2], slice(CELL, GATES), o_ps))

                    def multiply(bank, gates, x, w, stop):
                        for c in range(KC):
                            for j in range(Q):
                                last = pe.matmul(bank[j * B:(j + 1) * B, 0:(gates.stop - gates.start) * HQ], x[:, c, :],
                                                 w[:, c, gates, j * HQ:(j + 1) * HQ], start=False,
                                                 stop=(stop and c == KC - 1), skip_group_check=True, tile_position=(0, j * B))
                        return last

                    for bank, gates, _ in parts:
                        pe.matmul(bank[:, 0:(gates.stop - gates.start) * HQ], t.ident[:, :], bias[:, gates, :],
                                  start=True, stop=False, skip_group_check=True)
                    pe.wait_ge(xt_done, n + 1)
                    for bank, gates, _ in parts:
                        last = multiply(bank, gates, xt[u % 2], wx, False)
                    last.then_inc(xt_free, 1)
                    pe.wait_ge(hT_done, n + 1)
                    for bank, gates, done in parts:
                        multiply(bank, gates, hT, wh, True).then_inc(done, 1)

                pe.sem_inc(xt_free, 2)
                pe.wait_ge(t.lstm_weights_in, 16 * GATES * (1 + 2 * Q))
                with pe.Fori(0, N // STEPS) as s:
                    for u in range(STEPS):
                        step(s * STEPS + u, u)

            @block.scalar
            def _(act):
                def step(n, u):
                    bank = gate_bank[u % 2]
                    act.wait_ge(gates_ps, n + 1)
                    act.activation(fi[:, :, :], bank[:, 0:2 * HQ], ACT.Sigmoid).then_inc(fi_done, 1)
                    act.activation(cand[:, :], bank[:, 2 * HQ:3 * HQ], ACT.Tanh).then_inc(cand_done, 1)
                    act.wait_ge(o_ps, n + 1)
                    act.activation(og[:, :], o_bank[u % 2][:, 0:HQ], ACT.Sigmoid).then_inc(og_done, 1)
                    act.wait_ge(cell_done, n + 2)
                    act.activation(tanh_c[:, :], cell[:, :], ACT.Tanh).then_inc(tanh_done, 1)

                with act.Fori(0, N // STEPS) as s:
                    for u in range(STEPS):
                        step(s * STEPS + u, u)

            @block.vector
            def _(dve):
                def step(s, u):
                    n, half = s * STEPS + u, u // SEG
                    dve.wait_ge(fi_done, n + 1)
                    dve.wait_ge(cell_done, n + 1)
                    dve.tensor_tensor(kept[:, :], fi[:, 0, :], cell[:, :], ALU.mult)
                    dve.wait_ge(cand_done, n + 1)
                    dve.tensor_tensor(fresh[:, :], fi[:, 1, :], cand[:, :], ALU.mult).then_inc(fresh_done, 1)
                    dve.wait_ge(fresh_done, n + 1)
                    dve.tensor_tensor(cell[:, :], kept[:, :], fresh[:, :], ALU.add).then_inc(cell_done, 1)
                    if u % SEG == 0:
                        dve.wait_ge(stored[half], s * Q * 16)
                    dve.wait_ge(og_done, n + 1)
                    dve.wait_ge(tanh_done, n + 1)
                    dve.tensor_tensor(hs[half][:, u % SEG, :], og[:, :], tanh_c[:, :], ALU.mult).then_inc(h_done, 1)
                    dve.wait_ge(h_done, n + 1)
                    dve.transpose(hT[:, :, :], hs[half][:, u % SEG, :]).then_inc(hT_done, 1)

                dve.memset(cell[:, :], 0.0).then_inc(cell_done, 1)
                dve.memset(hT[:, :, :], 0.0).then_inc(hT_done, 1)
                with dve.Fori(0, N // STEPS) as s:
                    for u in range(STEPS):
                        step(s, u)


def gnn_phase(nc, t, a, hidden, masks):
    with ExitStack() as ctx:
        def sb(name, shape, dt=F32):
            return ctx.enter_context(nc.sbuf_tensor("g_" + name, shape, dt))

        def ps(name):
            return ctx.enter_context(nc.psum_tensor("g_" + name, [P, 512], F32))

        def sem(name):
            return ctx.enter_context(nc.semaphore("g_" + name))

        small, used = sb("small", [P, 96]), []

        def tiny(*shape):
            n, at = int(np.prod(shape)), sum(used)
            used.append(n)
            part = small[:, at:at + n]
            return part if len(shape) == 1 else part.rearrange("p (t w) -> p t w", w=shape[1])

        w1, hT = sb("w1", [P, KC, FF]), sb("hT", [P, KC, N])
        w1_upper, w1_rest = sb("w1_upper", [P, KC, FF], F32R), sb("w1_rest", [P, KC, FF], F32R)
        hT_upper, hT_rest = sb("hT_upper", [P, KC, N], F32R), sb("hT_rest", [P, KC, N], F32R)
        w2 = sb("w2", [P, MC, D])
        aw, aw_first = sb("aw", [P, 2, D]), sb("aw_first", [P, 2, D])
        g1_row, beta1_row, g2_row, beta2_row = (sb(n, [P, D]) for n in ("g1_row", "beta1_row", "g2_row", "beta2_row"))
        g1_col, beta1_col, b1_col, ab_cols = tiny(KC), tiny(KC), tiny(MC), tiny(L)
        warm = tiny(NT)
        parts = sb("parts", [P, 2, NT], F32R)
        upper, lower = parts[:, 0, :], parts[:, 1, :]
        diag = sb("diag", [P, 2, NT, P], F32R)
        own, top, lead = tiny(NT), tiny(NT), tiny(NT)
        most, shift, shift2 = tiny(NT), tiny(NT), tiny(NT)
        probs = sb("probs", [P, NT, N])
        total, rtotal = tiny(NT), tiny(NT)
        probsT = sb("probsT", [P, NT, N])
        r1, h = sb("r1", [P, NT, D]), sb("h", [P, NT, D])
        steep = sb("steep", [P, NT, N])
        b2_rows = [h[:, 0, :]] + [aw_first[:, 0, :]] * (L - 1)
        product, entered_junk = steep, probs
        hs = probsT
        act1 = sb("act1", [P, MC, N])
        r2 = sb("r2", [P, NT, D])
        stats1, mv1, veps1, rstd1 = (tiny(NT, w) for w in (6, 2, 1, 1))
        stats3, mv3, veps3, rstd3 = (tiny(NT, w) for w in (6, 2, 1, 1))
        stats2, mv2, veps2, rstd2 = (tiny(NT, w) for w in (6, 2, 1, 1))

        score_bank, turn_bank, agg_bank, ff_bank = ps("S"), ps("T"), ps("A"), ps("F")
        hidden_bank = [ps(f"H{q}") for q in range(MC // 2)]
        NB = MC // 2

        att_in, net_in, finish_in = sem("att_in"), sem("net_in"), sem("finish_in")
        ATT_IN, NET_IN, FINISH_IN = 5 * 16, 2 * 16, 2 * 16
        w1_in, aw_in, aw_first_in, hs_in, hs_second_in = sem("w1_in"), sem("aw_in"), sem("aw_first_in"), sem("hs_in"), sem("hs_second_in")
        (entered_x, entered_stats, entered_mv, entered_veps, entered_rstd, entered_nodes, entered_product,
         entered_pair) = (sem("entered_" + n) for n in ("x", "stats", "mv", "veps", "rstd", "nodes", "product", "pair"))
        left_x, left_stats, left_mv, left_veps, left_rstd, left_nodes, left_most = (
            sem("left_" + n) for n in ("x", "stats", "mv", "veps", "rstd", "nodes", "most"))
        pair_done, nodes_done = sem("pair_done"), sem("nodes_done")
        (diag_done, scores_ps, own_done, top_done, lead_done, most_done, shift_done, exp_done, probs_done,
         rtotal_done, turned_ps, turned_done, agg_ps, r1_done, stats1_done, mv1_done, veps1_done, rstd1_done,
         norm1_done, hg_done, h_done, hT_ps, hT_done, hidden_ps, gelu_done, ff_ps, r2_done, stats2_done,
         mv2_done, veps2_done, rstd2_done, norm2_done, scaled_done, product_done) = (sem(n) for n in (
            "diag_done", "scores_ps", "own_done", "top_done", "lead_done", "most_done", "shift_done", "exp_done",
            "probs_done", "rtotal_done", "turned_ps", "turned_done", "agg_ps", "r1_done", "stats1_done", "mv1_done",
            "veps1_done", "rstd1_done", "norm1_done", "hg_done", "h_done", "hT_ps", "hT_done",
            "hidden_ps", "gelu_done", "ff_ps", "r2_done", "stats2_done", "mv2_done", "veps2_done", "rstd2_done",
            "norm2_done", "scaled_done", "product_done"))
        gmask_in, w1_upper_done, w1_done, hT_full_done, hT_upper_done = (
            sem(n) for n in ("gmask_in", "w1_upper_done", "w1_done", "hT_full_done", "hT_upper_done"))
        parts_done = sem("parts_done")
        rows_done, warm_done = sem("rows_done"), sem("warm_done")

        def walk(eng, start, body, end):
            start((0, 1), (0, 0))
            for l in range(L):
                if l > 0:
                    body((l, 1), (l, 0), (l - 1, B - 1), (l - 1, B - 2))
                body((l, 2), (l, 1), (l, 0), (l - 1, B - 1) if l > 0 else None)
                if l == L - 1:
                    body((l, 3), (l, 2), (l, 1), (l, 0))
                with eng.Fori(2 if l == L - 1 else 1, B - 2) as b:
                    body((l, b + 2), (l, b + 1), (l, b), (l, b - 1))
                body((l + 1, 0) if l < L - 1 else None, (l, B - 1), (l, B - 2), (l, B - 3))
            body(None, None, (L - 1, B - 1), (L - 1, B - 2))
            end((L - 1, B - 1))

        passed = sem("passed")
        with nc.Block() as block:

            @block.sync
            def _(sp):
                def load_hidden(e, dst, done):
                    sp.dma_start(dst[:, :, :], hidden[e].rearrange("(t p) d -> p t d", p=P)).then_inc(done, 16)

                load_hidden(0, hs, hs_in)
                sp.dma_start(aw_first[:, :, :], a["L1_gnn_attn_w"][0].rearrange("(s d) -> s d", s=2).partition_broadcast(P)
                             ).then_inc(aw_first_in, 16)
                sp.dma_start(ab_cols[:, :], a["L1_gnn_attn_b"].partition_broadcast(P)).then_inc(aw_first_in, 16)
                load_hidden(1, r2, hs_second_in)
                for l in range(L):
                    after(sp, w1_done, l)
                    sp.dma_start(w1[:, :, :], a["L1_gnn_W1"][l].rearrange("(c p) n -> p c n", p=P)).then_inc(w1_in, 16)
                    after(sp, h_done, l * B)
                    after(sp, hT_done, l * B)
                    row = lambda name, dst, done: sp.dma_start(dst[:, :], a[name][l].partition_broadcast(P)).then_inc(done, 16)
                    row("L1_gnn_g1", g1_row, att_in)
                    row("L1_gnn_beta1", beta1_row, att_in)
                    after(sp, entered_pair, min(l, 1) * B)
                    row("L1_gnn_b2", b2_rows[l], att_in)
                    with nc.allow_non_contiguous_dma(reason="columns"):
                        sp.dma_start(g1_col[:, :], a["L1_gnn_g1"][l].rearrange("(c p) -> p c", p=P)).then_inc(att_in, 16)
                        sp.dma_start(beta1_col[:, :], a["L1_gnn_beta1"][l].rearrange("(c p) -> p c", p=P)).then_inc(att_in, 16)
                    after(sp, ff_ps, l * B)
                    sp.dma_start(w2[:, :, :], a["L1_gnn_W2"][l].rearrange("(c p) n -> p c n", p=P)).then_inc(net_in, 16)
                    with nc.allow_non_contiguous_dma(reason="columns"):
                        sp.dma_start(b1_col[:, :], a["L1_gnn_b1"][l].rearrange("(c p) -> p c", p=P)).then_inc(net_in, 16)
                    after(sp, nodes_done, l * B)
                    row("L1_gnn_g2", g2_row, finish_in)
                    row("L1_gnn_beta2", beta2_row, finish_in)
                    if l < L - 1:
                        after(sp, pair_done, l * B)
                        sp.dma_start(aw[:, :, :], a["L1_gnn_attn_w"][l + 1].rearrange("(s d) -> s d", s=2
                                     ).partition_broadcast(P)).then_inc(aw_in, 16)
                    if l == 0:
                        with sp.Fori(2, B) as e:
                            sp.wait_ge(agg_ps, e - 1)
                            load_hidden(e, hs, hs_in)

            @block.gpsimd
            def _(pool):
                def rsqrt1(l, b):
                    n = l * B + b
                    pool.wait_ge(mv1_done, n + 1)
                    pool.tensor_tensor(veps1[:, :, 0], mv1[:, :, 1], t.eps[:, :], ALU.add).then_inc(veps1_done, 1)
                    pool.wait_ge(veps1_done, n + 1)
                    pool.tensor_tensor(rstd1[:, :, 0], veps1[:, :, 0], t.power[:, :], ALU.pow).then_inc(rstd1_done, 1)

                def residual(l, b):
                    n = l * B + b
                    if isinstance(b, int) and b == 0:
                        pool.wait_ge(att_in, (l + 1) * ATT_IN)
                        pool.tensor_tensor(beta1_row[:, :], beta1_row[:, :], b2_rows[l], ALU.add).then_inc(rows_done, 1)
                        pool.wait_ge(rows_done, l + 1)
                    pool.wait_ge(norm1_done, n + 1)
                    after(pool, r2_done, n)
                    for it in range(NT):
                        last = pool.tensor_tensor(h[:, it, :], r1[:, it, :], g1_row[:, :], ALU.mult)
                    last.then_inc(hg_done, 1)

                def residual_end(l, b):
                    n = l * B + b
                    pool.wait_ge(hg_done, n + 1)
                    for it in range(NT):
                        last = pool.tensor_tensor(h[:, it, :], h[:, it, :], beta1_row[:, :], ALU.add)
                    last.then_inc(h_done, 1)

                def rsqrt2(l, b):
                    n = l * B + b
                    pool.wait_ge(mv2_done, n + 1)
                    pool.tensor_tensor(veps2[:, :, 0], mv2[:, :, 1], t.eps[:, :], ALU.add).then_inc(veps2_done, 1)
                    pool.wait_ge(veps2_done, n + 1)
                    pool.tensor_tensor(rstd2[:, :, 0], veps2[:, :, 0], t.power[:, :], ALU.pow).then_inc(rstd2_done, 1)

                def scale(l, b):
                    n = l * B + b
                    pool.wait_ge(norm2_done, n + 1)
                    pool.wait_ge(finish_in, (l + 1) * FINISH_IN)
                    for it in range(NT):
                        last = pool.tensor_tensor(r2[:, it, :], r2[:, it, :], g2_row[:, :], ALU.mult)
                    last.then_inc(scaled_done, 1)

                def move(l, b):
                    n = l * B + b
                    pool.wait_ge(scaled_done, n + 1)
                    for it in range(NT):
                        last = pool.tensor_tensor(t.nodes[:, b, it, :], r2[:, it, :], beta2_row[:, :], ALU.add)
                    last.then_inc(nodes_done, 1)

                def enter(e):
                    second = isinstance(e, int) and e == 1
                    if second:
                        pool.wait_ge(hs_second_in, 16)
                    else:
                        pool.wait_ge(hs_in, max(e, 1) * 16 if isinstance(e, int) else e * 16)
                    pool.tensor_tensor(t.x[:, e, :, :], t.x[:, e, :, :], (r2 if second else hs)[:, :, :], ALU.add
                                       ).then_inc(entered_x, 1)

                def rsqrt_entered(e):
                    pool.wait_ge(entered_mv, e + 1)
                    pool.tensor_tensor(veps3[:, :, 0], mv3[:, :, 1], t.eps[:, :], ALU.add).then_inc(entered_veps, 1)
                    pool.wait_ge(entered_veps, e + 1)
                    pool.tensor_tensor(rstd3[:, :, 0], veps3[:, :, 0], t.power[:, :], ALU.pow).then_inc(entered_rstd, 1)

                def leave(b):
                    pool.wait_ge(nodes_done, (L - 1) * B + b + 1)
                    pool.tensor_tensor(t.x[:, b, :, :], t.x[:, b, :, :], t.nodes[:, b, :, :], ALU.add).then_inc(left_x, 1)

                def rsqrt_left(b):
                    pool.wait_ge(left_mv, b + 1)
                    pool.tensor_tensor(veps3[:, :, 0], mv3[:, :, 1], t.eps[:, :], ALU.add).then_inc(left_veps, 1)
                    pool.wait_ge(left_veps, b + 1)
                    pool.tensor_tensor(rstd3[:, :, 0], veps3[:, :, 0], t.power[:, :], ALU.pow).then_inc(left_rstd, 1)

                def start(soon, at):
                    for e in range(2):
                        enter(e)
                        rsqrt_entered(e)
                    rsqrt1(*at)

                def body(soon, ahead, now, behind):
                    entering = soon[1] if soon and soon[0] == 0 else None
                    leaving = behind and behind[0] == L - 1
                    if entering is not None:
                        enter(entering)
                        rsqrt_entered(entering)
                    residual(*now)
                    if behind:
                        rsqrt2(*behind)
                        scale(*behind)
                        move(*behind)
                    if leaving:
                        leave(behind[1])
                    if ahead:
                        rsqrt1(*ahead)
                    if leaving:
                        rsqrt_left(behind[1])
                    residual_end(*now)

                def end(at):
                    rsqrt2(*at)
                    scale(*at)
                    move(*at)
                    leave(at[1])
                    rsqrt_left(at[1])

                walk(pool, start, body, end)

            @block.scalar
            def _(act):
                def attend(l, b):
                    n = l * B + b
                    after(act, warm_done, n)
                    act.activation(warm[:, :], t.eps[:, :], ACT.Exp).then_inc(warm_done, 1)
                    act.wait_ge(shift_done, n + 1)
                    after(act, turned_ps, n)
                    for it in range(NT):
                        act.activation(probs[:, it, :], score_bank[:, it * N:(it + 1) * N], ACT.Exp, bias=shift[:, it:it + 1])
                        last = act.activation(steep[:, it, :], score_bank[:, it * N:(it + 1) * N], ACT.Exp,
                                              bias=shift2[:, it:it + 1], scale=0.2)
                    last.then_inc(exp_done, 1)

                def feed(l, b):
                    n = l * B + b
                    act.wait_ge(net_in, (l + 1) * NET_IN)
                    after(act, ff_ps, n)
                    for q in range(NB):
                        act.wait_ge(hidden_ps, n * NB + q + 1)
                        for i in range(2):
                            last = act.activation(act1[:, 2 * q + i, :], hidden_bank[q][:, i * N:(i + 1) * N], ACT.Gelu,
                                                  bias=b1_col[:, 2 * q + i:2 * q + i + 1])
                        last.then_inc(gelu_done, 1)

                def load_mask(l, b):
                    act.dma_start(t.gmask[:, :], masks[(b + 1) % B]).then_inc(gmask_in, 16)

                def hT_out(l, b):
                    n = l * B + b
                    act.wait_ge(hT_ps, n + 1)
                    act.wait_ge(att_in, (l + 1) * ATT_IN)
                    after(act, hT_done, n)
                    for c in range(KC):
                        last = act.activation(hT[:, c, :], turn_bank[:, c * N:(c + 1) * N], ACT.Identity,
                                              bias=beta1_col[:, c:c + 1], scale=g1_col[:, c:c + 1])
                    last.then_inc(hT_full_done, 1)

                def start(soon, at):
                    act.dma_start(t.gmask[:, :], masks[0]).then_inc(gmask_in, 16)
                    attend(*at)
                    load_mask(*at)
                    hT_out(*at)

                def body(soon, ahead, now, behind):
                    if ahead:
                        attend(*ahead)
                        load_mask(*ahead)
                    feed(*now)
                    if ahead:
                        hT_out(*ahead)

                walk(act, start, body, lambda at: act.wait_ge(gmask_in, (L * B + 1) * 16))

            @block.vector
            def _(dve):
                def as_neighbour(l, b):
                    n = l * B + b
                    pair = t.pair[:, b, :, :]
                    if l == 0:
                        dve.wait_ge(entered_pair, b + 1)
                    else:
                        dve.wait_ge(pair_done, n - B + 1)
                    after(dve, parts_done, 2 * n)
                    dve.tensor_scalar(upper[:, :], pair[:, :, 1], 1.0, None, ALU.mult).then_inc(parts_done, 1)
                    dve.wait_ge(parts_done, 2 * n + 1)
                    dve.tensor_tensor(lower[:, :], pair[:, :, 1], upper[:, :].bitcast(F32), ALU.subtract).then_inc(parts_done, 1)
                    after(dve, scores_ps, n)
                    dve.wait_ge(parts_done, 2 * n + 2)
                    for k, part in enumerate((upper, lower)):
                        for it in range(NT):
                            last = dve.tensor_scalar(diag[:, k, it, :], t.ident[:, :], part[:, it:it + 1].bitcast(F32),
                                                     None, ALU.mult)
                    last.then_inc(diag_done, 1)

                def largest(l, b):
                    n = l * B + b
                    dve.tensor_scalar(own[:, :], t.pair[:, b, :, 0], ab_cols[:, l:l + 1], None, ALU.add).then_inc(own_done, 1)
                    dve.wait_ge(scores_ps, n + 1)
                    dve.tensor_reduce(top[:, :], score_bank[:, :].rearrange("p (t k) -> p t k", t=NT), AX.X,
                                      ALU.max).then_inc(top_done, 1)
                    dve.wait_ge(top_done, n + 1)
                    dve.wait_ge(own_done, n + 1)
                    dve.tensor_tensor(lead[:, :], top[:, :], own[:, :], ALU.add).then_inc(lead_done, 1)
                    dve.wait_ge(lead_done, n + 1)
                    dve.scalar_tensor_tensor(out=most[:, :], in0=lead[:, :], scalar=0.2, in1=lead[:, :], op0=ALU.mult,
                                             op1=ALU.max).then_inc(most_done, 1)
                    dve.wait_ge(most_done, n + 1)
                    after(dve, exp_done, n)
                    dve.tensor_tensor(shift[:, :], own[:, :], most[:, :], ALU.subtract)
                    dve.scalar_tensor_tensor(out=shift2[:, :], in0=own[:, :], scalar=0.2, in1=most[:, :], op0=ALU.mult,
                                             op1=ALU.subtract).then_inc(shift_done, 1)

                def larger(l, b):
                    n = l * B + b
                    dve.wait_ge(exp_done, n + 1)
                    for it in range(NT):
                        last = dve.scalar_tensor_tensor(out=probs[:, it, :], in0=probs[:, it, :], scalar=1.0,
                                                        in1=steep[:, it, :], op0=ALU.mult, op1=ALU.max,
                                                        accum_out=total[:, it:it + 1])
                    last.then_inc(probs_done, 1)
                    dve.wait_ge(probs_done, n + 1)
                    dve.reciprocal(rtotal[:, :], total[:, :]).then_inc(rtotal_done, 1)

                def turned(l, b):
                    n = l * B + b
                    dve.wait_ge(turned_ps, n + 1)
                    after(dve, agg_ps, n)
                    if l == 0:
                        dve.wait_ge(entered_x, min(b + 2, B) if isinstance(b, int) else b + 2)
                    dve.tensor_copy(probsT[:, :, :], turn_bank[:, :]).then_inc(turned_done, 1)

                def norm1(l, b, meanwhile):
                    n = l * B + b
                    dve.wait_ge(agg_ps, n + 1)
                    dve.wait_ge(rtotal_done, n + 1)
                    after(dve, hT_ps, n)
                    after(dve, hg_done, n)
                    for it in range(NT):
                        last = dve.scalar_tensor_tensor(out=r1[:, it, :], in0=agg_bank[:, it * D:(it + 1) * D],
                                                        scalar=rtotal[:, it:it + 1], in1=t.nodes[:, b, it, :],
                                                        op0=ALU.mult, op1=ALU.add)
                    last.then_inc(r1_done, 1)
                    alone(dve, r1_done, n + 1, passed)
                    for it in range(NT):
                        last = dve.bn_stats(stats1[:, it, :], r1[:, it, :])
                    last.then_inc(stats1_done, 1)
                    alone(dve, stats1_done, n + 1, passed)
                    for it in range(NT):
                        last = dve.bn_aggr(mv1[:, it, :], stats1[:, it, :])
                    last.then_inc(mv1_done, 1)
                    meanwhile()
                    dve.wait_ge(rstd1_done, n + 1)
                    for it in range(NT):
                        last = dve.tensor_scalar(r1[:, it, :], r1[:, it, :], mv1[:, it, 0:1], rstd1[:, it, :],
                                                 ALU.subtract, ALU.mult)
                    last.then_inc(norm1_done, 1)

                def split_hT(l, b):
                    n = l * B + b
                    dve.wait_ge(hT_full_done, n + 1)
                    after(dve, hidden_ps, n * NB)
                    dve.tensor_copy(hT_upper[:, :, :], hT[:, :, :]).then_inc(hT_upper_done, 1)
                    dve.wait_ge(hT_upper_done, n + 1)
                    dve.tensor_tensor(hT_rest[:, :, :], hT[:, :, :], hT_upper[:, :, :].bitcast(F32),
                                      ALU.subtract).then_inc(hT_done, 1)

                def split_w1(l):
                    dve.wait_ge(w1_in, (l + 1) * 16)
                    after(dve, hidden_ps, l * B * NB)
                    dve.tensor_copy(w1_upper[:, :, :], w1[:, :, :]).then_inc(w1_upper_done, 1)
                    dve.wait_ge(w1_upper_done, l + 1)
                    dve.tensor_tensor(w1_rest[:, :, :], w1[:, :, :], w1_upper[:, :, :].bitcast(F32),
                                      ALU.subtract).then_inc(w1_done, 1)

                def feed(l, b):
                    n = l * B + b
                    dve.wait_ge(ff_ps, n + 1)
                    dve.wait_ge(h_done, n + 1)
                    after(dve, nodes_done, n)
                    dve.tensor_tensor(r2[:, :, :], ff_bank[:, :].rearrange("p (t d) -> p t d", t=NT), h[:, :, :],
                                      ALU.add).then_inc(r2_done, 1)
                    alone(dve, r2_done, n + 1, passed)
                    for it in range(NT):
                        last = dve.bn_stats(stats2[:, it, :], r2[:, it, :])
                    last.then_inc(stats2_done, 1)
                    alone(dve, stats2_done, n + 1, passed)
                    for it in range(NT):
                        last = dve.bn_aggr(mv2[:, it, :], stats2[:, it, :])
                    last.then_inc(mv2_done, 1)

                def norm2(l, b):
                    n = l * B + b
                    dve.wait_ge(rstd2_done, n + 1)
                    for it in range(NT):
                        last = dve.tensor_scalar(r2[:, it, :], r2[:, it, :], mv2[:, it, 0:1], rstd2[:, it, :],
                                                 ALU.subtract, ALU.mult)
                    last.then_inc(norm2_done, 1)

                def pairs(b, weights, product, product_done, done, count, which):
                    for s in which:
                        if s == 1:
                            dve.wait_ge(product_done, count + 1)
                        for it in range(NT):
                            last = dve.scalar_tensor_tensor(out=product[:, it, :], in0=t.nodes[:, b, it, :], scalar=1.0,
                                                            in1=weights[:, s, :], op0=ALU.mult, op1=ALU.mult,
                                                            accum_out=t.pair[:, b, it, s:s + 1])
                        last.then_inc(product_done if s == 0 else done, 1)

                def next_pair(l, b, which):
                    n = l * B + b
                    if which == 0:
                        dve.wait_ge(nodes_done, n + 1)
                        dve.wait_ge(aw_in, (l + 1) * 16)
                        dve.wait_ge(entered_pair, b + 1) if l == 0 else dve.wait_ge(pair_done, n - B + 1)
                    pairs(b, aw, product, product_done, pair_done, n, [which])

                def moments_entered(e):
                    alone(dve, entered_x, e + 1, passed)
                    for it in range(NT):
                        last = dve.bn_stats(stats3[:, it, :], t.x[:, e, it, :])
                    last.then_inc(entered_stats, 1)
                    alone(dve, entered_stats, e + 1, passed)
                    for it in range(NT):
                        last = dve.bn_aggr(mv3[:, it, :], stats3[:, it, :])
                    last.then_inc(entered_mv, 1)

                def norm_entered(e):
                    dve.wait_ge(entered_rstd, e + 1)
                    for it in range(NT):
                        last = dve.tensor_scalar(t.nodes[:, e, it, :], t.x[:, e, it, :], mv3[:, it, 0:1], rstd3[:, it, :],
                                                 ALU.subtract, ALU.mult)
                    last.then_inc(entered_nodes, 1)

                def pair_entered(e, which):
                    if which == 0:
                        dve.wait_ge(entered_nodes, e + 1)
                        after(dve, entered_pair, e)
                    pairs(e, aw_first, entered_junk, entered_product, entered_pair, e, [which])

                def moments_left(b):
                    alone(dve, left_x, b + 1, passed)
                    for it in range(NT):
                        last = dve.bn_stats(stats3[:, it, :], t.x[:, b, it, :])
                    last.then_inc(left_stats, 1)
                    alone(dve, left_stats, b + 1, passed)
                    for it in range(NT):
                        last = dve.bn_aggr(mv3[:, it, :], stats3[:, it, :])
                    last.then_inc(left_mv, 1)

                def norm_left(b):
                    dve.wait_ge(left_rstd, b + 1)
                    for it in range(NT):
                        last = dve.tensor_scalar(t.nodes[:, b, it, :], t.x[:, b, it, :], mv3[:, it, 0:1], rstd3[:, it, :],
                                                 ALU.subtract, ALU.mult)
                    last.then_inc(left_nodes, 1)
                    dve.wait_ge(left_nodes, b + 1)
                    dve.tensor_reduce(t.mosts[:, bass.ds(b, 1)], t.nodes[:, b, :, :], AX.XY, ALU.max,
                                      apply_absolute_value=True).then_inc(left_most, 1)

                def start(soon, at):
                    dve.wait_ge(aw_first_in, 2 * 16)
                    moments_entered(0)
                    norm_entered(0)
                    pair_entered(0, 0)
                    pair_entered(0, 1)
                    as_neighbour(*at)
                    moments_entered(1)
                    largest(*at)
                    norm_entered(1)
                    larger(*at)
                    turned(*at)
                    split_w1(0)
                    pair_entered(1, 0)
                    norm1(*at, lambda: pair_entered(1, 1))
                    as_neighbour(*soon)
                    split_hT(*at)

                def body(soon, ahead, now, behind):
                    entering = soon[1] if soon and soon[0] == 0 else None
                    leaving = behind and behind[0] == L - 1
                    if ahead:
                        largest(*ahead)
                    if entering is not None:
                        moments_entered(entering)
                    if behind:
                        feed(*behind)
                    if ahead:
                        larger(*ahead)
                    if behind:
                        norm2(*behind)
                    if ahead:
                        turned(*ahead)
                    if ahead and now[0] < ahead[0]:
                        split_w1(ahead[0])
                    if leaving and not (isinstance(behind[1], int) and behind[1] == 0):
                        norm_left(behind[1] - 1)
                    if entering is not None:
                        norm_entered(entering)
                        for which in range(2):
                            pair_entered(entering, which)

                    def meanwhile():
                        if behind and not leaving:
                            next_pair(*behind, 0)
                        if leaving:
                            moments_left(behind[1])

                    if ahead:
                        norm1(*ahead, meanwhile)
                    else:
                        meanwhile()
                    if soon:
                        as_neighbour(*soon)
                    if behind and not leaving:
                        next_pair(*behind, 1)
                    if ahead:
                        split_hT(*ahead)

                def end(at):
                    feed(*at)
                    norm2(*at)
                    norm_left(at[1] - 1)
                    moments_left(at[1])
                    norm_left(at[1])

                walk(dve, start, body, end)

            @block.tensor
            def _(pe):
                def scores(l, b):
                    n = l * B + b
                    pe.wait_ge(diag_done, n + 1)
                    pe.wait_ge(gmask_in, (n + 1) * 16)
                    after(pe, exp_done, n)
                    pe.matmul(score_bank[:, :], t.identb[:, :], t.gmask[:, :], start=True, stop=False,
                              skip_group_check=True)
                    for k in range(2):
                        for it in range(NT):
                            last = pe.matmul(score_bank[:, it * N:(it + 1) * N], t.ones_r[:, :].broadcast_to((P, P)),
                                             diag[:, k, :, :], start=False, stop=True, skip_group_check=True)
                    last.then_inc(scores_ps, 1)

                def turn_probs(l, b):
                    n = l * B + b
                    pe.wait_ge(probs_done, n + 1)
                    after(pe, hT_full_done, n)
                    for jt in range(NT):
                        for it in range(NT):
                            last = pe.transpose(turn_bank[:, jt * N + it * P:jt * N + (it + 1) * P],
                                                probs[:, it, jt * P:(jt + 1) * P], t.ident[:, :])
                    last.then_inc(turned_ps, 1)

                def aggregate(l, b):
                    n = l * B + b
                    pe.wait_ge(turned_done, n + 1)
                    after(pe, r1_done, n)
                    for it in range(NT):
                        for jt in range(NT):
                            last = pe.matmul(agg_bank[:, it * D:(it + 1) * D], probsT[:, jt, it * P:(it + 1) * P],
                                             t.nodes[:, b, jt, :], start=(jt == 0), stop=(jt == NT - 1))
                    last.then_inc(agg_ps, 1)

                def turn_h(l, b):
                    n = l * B + b
                    pe.wait_ge(norm1_done, n + 1)
                    pe.wait_ge(turned_done, n + 1)
                    for c in range(KC):
                        for it in range(NT):
                            last = pe.transpose(turn_bank[:, c * N + it * P:c * N + (it + 1) * P],
                                                r1[:, it, c * P:(c + 1) * P], t.ident[:, :])
                    last.then_inc(hT_ps, 1)

                def up(l, b, chunks):
                    n = l * B + b
                    if chunks[0] == 0:
                        pe.wait_ge(hT_done, n + 1)
                        pe.wait_ge(w1_done, l + 1)
                        after(pe, gelu_done, n * NB)
                    for m in chunks:
                        for c in range(KC):
                            for k, (w, x) in enumerate(((w1_upper, hT_upper), (w1_upper, hT_rest), (w1_rest, hT_upper))):
                                last = pe.matmul(hidden_bank[m // 2][:, m % 2 * N:(m % 2 + 1) * N],
                                                 w[:, c, m * P:(m + 1) * P], x[:, c, :], start=(c == 0 and k == 0),
                                                 stop=(c == KC - 1 and k == 2))
                        if m % 2 == 1:
                            last.then_inc(hidden_ps, 1)

                def down(l, b, chunks):
                    n = l * B + b
                    if chunks[0] == 0:
                        after(pe, r2_done, n)
                        pe.wait_ge(net_in, (l + 1) * NET_IN)
                    for m in chunks:
                        if m % 2 == 0:
                            pe.wait_ge(gelu_done, n * NB + m // 2 + 1)
                        for it in range(NT):
                            last = pe.matmul(ff_bank[:, it * D:(it + 1) * D], act1[:, m, it * P:(it + 1) * P],
                                             w2[:, m, :], start=(m == 0 and it == 0), stop=(m == MC - 1),
                                             skip_group_check=True)
                        if m == MC - 1:
                            last.then_inc(ff_ps, 1)

                def start(soon, at):
                    scores(*at)
                    turn_probs(*at)
                    aggregate(*at)
                    turn_h(*at)

                def body(soon, ahead, now, behind):
                    if ahead:
                        scores(*ahead)
                    up(*now, range(0, MC - 1))
                    if ahead:
                        turn_probs(*ahead)
                    up(*now, range(MC - 1, MC))
                    down(*now, range(0, 1))
                    if ahead:
                        aggregate(*ahead)
                    down(*now, range(1, 6))
                    if ahead:
                        turn_h(*ahead)
                    down(*now, range(6, MC))

                walk(pe, start, body, lambda at: None)


def last_phase(nc, t, a, out):
    STEP = float(2 ** 20)
    LEAST = 1.5 * 2 ** 14
    EXPONENT, HALF = 0x7F800000, 0x00400000
    U32 = mybir.dt.uint32
    with ExitStack() as ctx:
        def sb(name, shape, dt=F32):
            return ctx.enter_context(nc.sbuf_tensor("q_" + name, shape, dt))

        def sem(name):
            return ctx.enter_context(nc.semaphore("q_" + name))

        weight, wstep, wsum = (sb(n, [P, KC, D]) for n in ("weight", "wstep", "wsum"))
        wq = sb("wq", [P, KC, D], BF16)
        most, tops = sb("most", [P, 2]), sb("tops", [P, 2])
        floor, inv, scale, rscale, oscale = (sb(n, [P, 2]) for n in ("floor", "inv", "scale", "rscale", "oscale"))
        val, step_of, total = ([sb(f"{n}{i}", [P, NT, D]) for i in range(2)] for n in ("val", "step", "total"))
        xq = [sb(f"xq{i}", [P, NT, D], BF16) for i in range(2)]
        xqT = [sb(f"xqT{i}", [P, KC, N], BF16) for i in range(2)]
        res = [sb(f"res{i}", [P, NT, D]) for i in range(2)]
        turn_bank = [ctx.enter_context(nc.psum_tensor(f"q_T{i}", [P, 1024], BF16)) for i in range(2)]
        out_bank = [ctx.enter_context(nc.psum_tensor(f"q_O{i}", [P, 512], F32)) for i in range(2)]

        weight_in, most_done, tops_done, math_done, wq_done, wchain = (
            sem(n) for n in ("weight_in", "most_done", "tops_done", "math_done", "wq_done", "wchain"))
        (val_done, power_done, step_done,
         sum_done, xq_done, turned_ps, turned_done, out_ps, res_done, stored) = ([sem(f"{n}{i}") for i in range(2)] for n in (
            "val_done", "power_done", "step_done", "sum_done", "xq_done", "turned_ps", "turned_done", "out_ps", "res_done", "stored"))
        G = B // 2

        with nc.Block() as block:

            @block.sync
            def _(sp):
                sp.dma_start(weight[:, :, :], a["L1_ffn_weight"].rearrange("(c p) n -> p c n", p=P)).then_inc(weight_in, 16)
                with sp.Fori(0, G) as g:
                    for i in range(2):
                        sp.wait_ge(res_done[i], g + 1)
                        sp.dma_start(out[g * 2 + i].rearrange("(t p) d -> p t d", p=P), res[i][:, :, :]).then_inc(stored[i], 16)
                for i in range(2):
                    sp.wait_ge(stored[i], G * 16)

            @block.gpsimd
            def _(pool):
                pool.wait_ge(most_done, 2)
                pool.partition_all_reduce(tops[:, :], most[:, :], P, bass.bass_isa.ReduceOp.max).then_inc(tops_done, 1)
                with pool.Fori(0, G) as g:
                    for i in range(2):
                        pool.wait_ge(sum_done[i], g + 1)
                        pool.wait_ge(turned_ps[i], g)
                        pool.tensor_tensor(xq[i][:, :, :], total[i][:, :, :], step_of[i][:, :, :], ALU.subtract).then_inc(xq_done[i], 1)

            @block.scalar
            def _(act):
                with act.Fori(0, G) as g:
                    for i in range(2):
                        act.wait_ge(turned_ps[i], g + 1)
                        act.wait_ge(out_ps[i], g)
                        act.activation(xqT[i][:, :, :], turn_bank[i][:, 0:KC * N], ACT.Copy).then_inc(turned_done[i], 1)

            @block.tensor
            def _(pe):
                pe.wait_ge(wq_done, 1)
                with pe.Fori(0, G) as g:
                    for i in range(2):
                        pe.wait_ge(xq_done[i], g + 1)
                        pe.wait_ge(turned_done[i], g)
                        for c in range(KC):
                            for it in range(NT):
                                last = pe.transpose(turn_bank[i][:, c * N + it * P:c * N + (it + 1) * P],
                                                    xq[i][:, it, c * P:(c + 1) * P], t.identb[:, :])
                        last.then_inc(turned_ps[i], 1)
                        pe.wait_ge(turned_done[i], g + 1)
                        pe.wait_ge(res_done[i], g)
                        for it in range(NT):
                            for c in range(KC):
                                last = pe.matmul(out_bank[i][:, it * D:(it + 1) * D], xqT[i][:, c, it * P:(it + 1) * P],
                                                 wq[:, c, :], start=(c == 0), stop=(c == KC - 1))
                        last.then_inc(out_ps[i], 1)

            @block.vector
            def _(dve):
                dve.tensor_reduce(most[:, 0:1], t.mosts[:, :], AX.X, ALU.max).then_inc(most_done, 1)
                dve.wait_ge(weight_in, 16)
                dve.tensor_reduce(most[:, 1:2], weight[:, :, :], AX.XY, ALU.max, apply_absolute_value=True).then_inc(most_done, 1)
                dve.wait_ge(tops_done, 1)
                dve.tensor_scalar(floor[:, :], tops[:, :], 1e-12, None, ALU.max).then_inc(math_done, 1)
                dve.wait_ge(math_done, 1)
                dve.reciprocal(inv[:, :], floor[:, :]).then_inc(math_done, 1)
                dve.wait_ge(math_done, 2)
                dve.tensor_scalar(scale[:, :], inv[:, :], FP8_MAX, None, ALU.mult).then_inc(math_done, 1)
                dve.wait_ge(math_done, 3)
                dve.reciprocal(rscale[:, :], scale[:, :]).then_inc(math_done, 1)
                dve.wait_ge(math_done, 4)
                dve.tensor_tensor(oscale[:, 0:1], rscale[:, 0:1], rscale[:, 1:2], ALU.mult).then_inc(math_done, 1)
                dve.wait_ge(math_done, 5)

                dve.tensor_scalar(weight[:, :, :], weight[:, :, :], scale[:, 1:2], FP8_MAX, ALU.mult, ALU.min).then_inc(wchain, 1)
                dve.wait_ge(wchain, 1)
                dve.tensor_scalar(weight[:, :, :], weight[:, :, :], -FP8_MAX, None, ALU.max).then_inc(wchain, 1)
                dve.wait_ge(wchain, 2)
                dve.tensor_scalar(wstep[:, :, :].bitcast(U32), weight[:, :, :].bitcast(U32), EXPONENT, HALF,
                                  ALU.bitwise_and, ALU.bitwise_or).then_inc(wchain, 1)
                dve.wait_ge(wchain, 3)
                dve.tensor_scalar(wstep[:, :, :], wstep[:, :, :], STEP, LEAST, ALU.mult, ALU.max).then_inc(wchain, 1)
                dve.wait_ge(wchain, 4)
                dve.tensor_tensor(wsum[:, :, :], weight[:, :, :], wstep[:, :, :], ALU.add).then_inc(wchain, 1)
                dve.wait_ge(wchain, 5)
                dve.tensor_tensor(wq[:, :, :], wsum[:, :, :], wstep[:, :, :], ALU.subtract).then_inc(wq_done, 1)

                def quantise(g, i):
                    b = g * 2 + i
                    dve.wait_ge(xq_done[i], g)
                    dve.tensor_scalar(val[i][:, :, :], t.nodes[:, b, :, :], scale[:, 0:1], FP8_MAX, ALU.mult,
                                      ALU.min).then_inc(val_done[i], 1)
                    dve.wait_ge(val_done[i], g + 1)
                    dve.tensor_scalar(step_of[i][:, :, :].bitcast(U32), val[i][:, :, :].bitcast(U32), EXPONENT, HALF,
                                      ALU.bitwise_and, ALU.bitwise_or).then_inc(power_done[i], 1)
                    dve.wait_ge(power_done[i], g + 1)
                    dve.tensor_scalar(step_of[i][:, :, :], step_of[i][:, :, :], STEP, LEAST, ALU.mult,
                                      ALU.max).then_inc(step_done[i], 1)
                    dve.wait_ge(step_done[i], g + 1)
                    dve.scalar_tensor_tensor(out=total[i][:, :, :], in0=val[i][:, :, :], scalar=-FP8_MAX,
                                             in1=step_of[i][:, :, :], op0=ALU.max, op1=ALU.add).then_inc(sum_done[i], 1)

                def result(g, i):
                    dve.wait_ge(out_ps[i], g + 1)
                    dve.wait_ge(stored[i], g * 16)
                    dve.scalar_tensor_tensor(out=res[i][:, :, :], in0=out_bank[i][:, :].rearrange("p (t d) -> p t d", t=NT),
                                             scalar=oscale[:, 0:1], in1=t.x[:, g * 2 + i, :, :], op0=ALU.mult,
                                             op1=ALU.add).then_inc(res_done[i], 1)

                for i in range(2):
                    quantise(0, i)
                with dve.Fori(1, G) as g:
                    for i in range(2):
                        quantise(g, i)
                        result(g - 1, i)
                for i in range(2):
                    result(G - 1, i)


class Shared:
    pass


def build_program(nc, a, out):
    hidden = nc.dram_tensor("hidden", (B, N, D), F32, kind="Internal").ap()
    masks = nc.dram_tensor("masks", (B, P, NT * N), BF16, kind="Internal").ap()
    t = Shared()
    with ExitStack() as ctx:
        def sb(name, shape, dt=F32):
            return ctx.enter_context(nc.sbuf_tensor(name, shape, dt))

        t.x = sb("x", [P, B, NT, D])
        t.seq = sb("seq", [P, KC, N, B])
        t.nodes = t.seq[:, :, :, :].rearrange("p c n b -> p (c n b)").rearrange("p (g t d) -> p g t d", g=B, t=NT)
        t.pair = sb("pair", [P, B, NT, 2])
        t.mosts = sb("mosts", [P, B])
        t.gmask = sb("gmask", [P, NT * N], BF16)
        t.ident, t.identb, t.ones_r = sb("ident", [P, P]), sb("identb", [P, P], BF16), sb("ones_r", [P, 1], F32R)
        t.ones = t.ones_r[:, :].bitcast(F32)
        small = sb("eps_power", [P, 2, NT])
        t.eps, t.power = small[:, 0, :], small[:, 1, :]
        constants(nc, t)
        with ExitStack() as lstm:
            t.wx, t.wh = (lstm.enter_context(nc.sbuf_tensor(n, [P, KC, GATES, D], F32)) for n in ("wx", "wh"))
            t.bias = lstm.enter_context(nc.sbuf_tensor("bias", [P, GATES, HQ], F32))
            t.lstm_weights_in = lstm.enter_context(nc.semaphore("lstm_weights_in"))
            attention_phase(nc, t, a, masks)
            lstm_phase(nc, t, a, hidden)
        gnn_phase(nc, t, a, hidden, masks)
        last_phase(nc, t, a, out)


_INS = ['x', 'adj', 'L0_gnn_Wq', 'L0_gnn_bq', 'L0_gnn_Wk', 'L0_gnn_bk', 'L0_gnn_Wv', 'L0_gnn_bv', 'L0_gnn_Wo',
        'L0_gnn_bo', 'L0_ffn_W_f', 'L0_ffn_b_f', 'L0_ffn_W_i', 'L0_ffn_b_i', 'L0_ffn_W_c', 'L0_ffn_b_c',
        'L0_ffn_W_o', 'L0_ffn_b_o', 'L1_gnn_attn_w', 'L1_gnn_attn_b', 'L1_gnn_W1', 'L1_gnn_b1', 'L1_gnn_W2',
        'L1_gnn_b2', 'L1_gnn_g1', 'L1_gnn_beta1', 'L1_gnn_g2', 'L1_gnn_beta2', 'L1_ffn_weight']


def kernel(**inputs):
    import numpy as _np
    import concourse.bacc as _bacc
    from concourse import mybir as _mybir
    from concourse.bass_utils import run_bass_kernel_spmd as _run

    nc = _bacc.Bacc("TRN2", target_bir_lowering=False, num_devices=1)
    arrays, args = {}, {}
    for name in _INS:
        x = _np.ascontiguousarray(inputs[name])
        arrays[f"in_{name}_dram"] = x
        args[name] = nc.dram_tensor(f"in_{name}_dram", x.shape, _mybir.dt.from_np(x.dtype), kind="ExternalInput").ap()
    out = nc.dram_tensor("out_0_dram", (B, N, D), F32, kind="ExternalOutput").ap()
    build_program(nc, args, out)
    r = _run(nc, [arrays], core_ids=[0])
    return r.results[0]["out_0_dram"]
```
